# Optimizing a Trainium2 kernel written in Bass

```python
import numpy as np
import jax
import jax.numpy as jnp

def _softmax(x, axis=-1):
    return jax.nn.softmax(x, axis=axis)

def _gelu(x):
    return jax.nn.gelu(x, approximate=True)

def _silu(x):
    return jax.nn.silu(x)

def _sigmoid(x):
    return jax.nn.sigmoid(x)

def _layernorm(x, axis=-1, eps=1e-05):
    m = jnp.mean(x, axis=axis, keepdims=True)
    v = jnp.var(x, axis=axis, keepdims=True)
    return (x - m) / jnp.sqrt(v + eps)

def _scatter_add(tgt, idx, src, axis=0):
    return tgt.at[idx].add(src)

def _segment_sum(src, seg, n):
    return jax.ops.segment_sum(src, seg, n)
kernel_name = 'mk_gnn_preln_d2_gnn_r16_8c8140'

def setup_inputs(seed: int=0):
    np.random.seed(seed)
    _w = jnp.asarray

    def _rec_inputs():
        import jax
        import jax.numpy as jnp
        _gk = jax.random.key(seed)
        x = -0.0003713 + 1 * jax.random.normal(jax.random.fold_in(_gk, 1), (6250, 128), jnp.float32)
        src = jax.random.randint(jax.random.fold_in(_gk, 2), (200000,), 0, 6250, jnp.int32)
        dst = jnp.minimum((6250 * jax.random.uniform(jax.random.fold_in(_gk, 3), (200000,)) ** 2.0).astype(jnp.int32), 99999)
        _o = jnp.argsort(dst, stable=True)
        src = src[_o]
        dst = dst[_o]
        edge_attr_16 = 0.000312547 + 1.00004 * jax.random.normal(jax.random.fold_in(_gk, 12), (200000, 16), jnp.float32)
        return (x, src, dst, edge_attr_16)
    x, src, dst, edge_attr_16 = _rec_inputs()

    def _L0_gnn_setup():
        import jax, jax.numpy as jnp
        import numpy as np
        import math
        N = 6250
        E = 62500
        D = 128
        ED = 16
        L = 5
        MID = 3
        ALPHA = 0.2
        THETA = 0.2
        NEG_SLOPE_ATT = 0.2

        def _gat_layer(x, src, dst, ea, W, We, a_src, a_dst, a_edge, b, n):
            h = x @ W
            e = ea @ We
            s = (h @ a_src)[src] + (h @ a_dst)[dst] + e @ a_edge
            s = jax.nn.leaky_relu(s, NEG_SLOPE_ATT)
            smax = jax.ops.segment_max(s, dst, num_segments=n)
            ex = jnp.exp(s - jax.lax.stop_gradient(smax)[dst])
            denom = jax.ops.segment_sum(ex, dst, num_segments=n)
            alpha = ex / denom[dst]
            out = jax.ops.segment_sum(h[src] * alpha[:, None], dst, num_segments=n)
            return out + b

        def _forward(x, edge_index, edge_attr, Ws, Wes, a_srcs, a_dsts, a_edges, biases, mid_ws):
            n = x.shape[0]
            src0, dst0 = (edge_index[0], edge_index[1])
            deg = jax.ops.segment_sum(jnp.ones_like(dst0, dtype=x.dtype), dst0, num_segments=n)
            loop_attr = jax.ops.segment_sum(edge_attr, dst0, num_segments=n) / jnp.clip(deg, 1.0)[:, None]
            loops = jnp.arange(n, dtype=src0.dtype)
            src = jnp.concatenate([src0, loops])
            dst = jnp.concatenate([dst0, loops])
            ea = jnp.concatenate([edge_attr, loop_attr], axis=0)
            x0 = _gat_layer(x, src, dst, ea, Ws[0], Wes[0], a_srcs[0], a_dsts[0], a_edges[0], biases[0], n)
            h = x0
            for i in range(MID):
                c = _gat_layer(h, src, dst, ea, Ws[i + 1], Wes[i + 1], a_srcs[i + 1], a_dsts[i + 1], a_edges[i + 1], biases[i + 1], n)
                beta = math.log(THETA / (i + 1) + 1.0)
                h = (1.0 - ALPHA) * c + ALPHA * x0
                h = (1.0 - beta) * h + beta * (h @ mid_ws[i])
                h = jax.nn.leaky_relu(h, 0.01)
            return _gat_layer(h, src, dst, ea, Ws[L - 1], Wes[L - 1], a_srcs[L - 1], a_dsts[L - 1], a_edges[L - 1], biases[L - 1], n)
        key = jax.random.key(seed)
        ks = jax.random.split(key, 10)
        s = 1.0 / np.sqrt(D)
        se = 1.0 / np.sqrt(ED)
        return {'x': jax.random.normal(ks[0], (N, D), jnp.float32), 'edge_index': jax.random.randint(ks[1], (2, E), 0, N, dtype=jnp.int64), 'edge_attr': jax.random.normal(ks[2], (E, ED), jnp.float32), 'Ws': jax.random.normal(ks[3], (L, D, D), jnp.float32) * s, 'Wes': jax.random.normal(ks[4], (L, ED, D), jnp.float32) * se, 'a_srcs': jax.random.normal(ks[5], (L, D), jnp.float32) * s, 'a_dsts': jax.random.normal(ks[6], (L, D), jnp.float32) * s, 'a_edges': jax.random.normal(ks[7], (L, D), jnp.float32) * s, 'biases': jnp.zeros((L, D), jnp.float32), 'mid_ws': jax.random.normal(ks[8], (MID, D, D), jnp.float32) * s}
    _L0_gnn_all = _L0_gnn_setup()
    _L0_gnn_in = {k: v for k, v in _L0_gnn_all.items() if k in ('Ws', 'Wes', 'a_srcs', 'a_dsts', 'a_edges', 'biases', 'mid_ws')}
    del _L0_gnn_all

    def _L1_gnn_setup():
        import jax, jax.numpy as jnp
        import numpy as np
        N, E, C = (6250, 100000, 128)
        EPS = 1e-05

        def _bn(x, g, b):
            mu = jnp.mean(x, axis=0)
            var = jnp.mean((x - mu) ** 2, axis=0)
            return g * (x - mu) * jax.lax.rsqrt(var + EPS) + b
        key = jax.random.key(seed)
        ks = jax.random.split(key, 8)
        s = 1.0 / np.sqrt(C)
        return {'h': jax.random.normal(ks[0], (N, C), jnp.float32), 'src': jax.random.randint(ks[1], (E,), 0, N, jnp.int32), 'dst': jax.random.randint(ks[2], (E,), 0, N, jnp.int32), 'theta_w': jax.random.normal(ks[3], (C, C), jnp.float32) * s, 'phi_w': jax.random.normal(ks[4], (C, C), jnp.float32) * s, 'fc1_w': jax.random.normal(ks[5], (C, C), jnp.float32) * s, 'bn0_g': jnp.ones((C,), jnp.float32), 'bn0_b': jnp.zeros((C,), jnp.float32), 'bn1_g': jnp.ones((C,), jnp.float32), 'bn1_b': jnp.zeros((C,), jnp.float32)}
    _L1_gnn_all = _L1_gnn_setup()
    _L1_gnn_in = {k: v for k, v in _L1_gnn_all.items() if k in ('theta_w', 'phi_w', 'fc1_w', 'bn0_g', 'bn0_b', 'bn1_g', 'bn1_b')}
    del _L1_gnn_all
    return {'x': x, 'src': src, 'dst': dst, 'edge_attr_16': edge_attr_16, 'L0_gnn_Ws': _L0_gnn_in['Ws'], 'L0_gnn_Wes': _L0_gnn_in['Wes'], 'L0_gnn_a_srcs': _L0_gnn_in['a_srcs'], 'L0_gnn_a_dsts': _L0_gnn_in['a_dsts'], 'L0_gnn_a_edges': _L0_gnn_in['a_edges'], 'L0_gnn_biases': _L0_gnn_in['biases'], 'L0_gnn_mid_ws': _L0_gnn_in['mid_ws'], 'L1_gnn_theta_w': _L1_gnn_in['theta_w'], 'L1_gnn_phi_w': _L1_gnn_in['phi_w'], 'L1_gnn_fc1_w': _L1_gnn_in['fc1_w'], 'L1_gnn_bn0_g': _L1_gnn_in['bn0_g'], 'L1_gnn_bn0_b': _L1_gnn_in['bn0_b'], 'L1_gnn_bn1_g': _L1_gnn_in['bn1_g'], 'L1_gnn_bn1_b': _L1_gnn_in['bn1_b']}

def reference(x, src, dst, edge_attr_16, L0_gnn_Ws, L0_gnn_Wes, L0_gnn_a_srcs, L0_gnn_a_dsts, L0_gnn_a_edges, L0_gnn_biases, L0_gnn_mid_ws, L1_gnn_theta_w, L1_gnn_phi_w, L1_gnn_fc1_w, L1_gnn_bn0_g, L1_gnn_bn0_b, L1_gnn_bn1_g, L1_gnn_bn1_b):
    import jax
    import jax.numpy as jnp

    def _L0_gnn_ref(x, edge_index, edge_attr, Ws, Wes, a_srcs, a_dsts, a_edges, biases, mid_ws):
        import jax, jax.numpy as jnp
        import numpy as np
        import math
        N = 6250
        E = 62500
        D = 128
        ED = 16
        L = 5
        MID = 3
        ALPHA = 0.2
        THETA = 0.2
        NEG_SLOPE_ATT = 0.2

        def _gat_layer(x, src, dst, ea, W, We, a_src, a_dst, a_edge, b, n):
            h = x @ W
            e = ea @ We
            s = (h @ a_src)[src] + (h @ a_dst)[dst] + e @ a_edge
            s = jax.nn.leaky_relu(s, NEG_SLOPE_ATT)
            smax = jax.ops.segment_max(s, dst, num_segments=n)
            ex = jnp.exp(s - jax.lax.stop_gradient(smax)[dst])
            denom = jax.ops.segment_sum(ex, dst, num_segments=n)
            alpha = ex / denom[dst]
            out = jax.ops.segment_sum(h[src] * alpha[:, None], dst, num_segments=n)
            return out + b

        def _forward(x, edge_index, edge_attr, Ws, Wes, a_srcs, a_dsts, a_edges, biases, mid_ws):
            n = x.shape[0]
            src0, dst0 = (edge_index[0], edge_index[1])
            deg = jax.ops.segment_sum(jnp.ones_like(dst0, dtype=x.dtype), dst0, num_segments=n)
            loop_attr = jax.ops.segment_sum(edge_attr, dst0, num_segments=n) / jnp.clip(deg, 1.0)[:, None]
            loops = jnp.arange(n, dtype=src0.dtype)
            src = jnp.concatenate([src0, loops])
            dst = jnp.concatenate([dst0, loops])
            ea = jnp.concatenate([edge_attr, loop_attr], axis=0)
            x0 = _gat_layer(x, src, dst, ea, Ws[0], Wes[0], a_srcs[0], a_dsts[0], a_edges[0], biases[0], n)
            h = x0
            for i in range(MID):
                c = _gat_layer(h, src, dst, ea, Ws[i + 1], Wes[i + 1], a_srcs[i + 1], a_dsts[i + 1], a_edges[i + 1], biases[i + 1], n)
                beta = math.log(THETA / (i + 1) + 1.0)
                h = (1.0 - ALPHA) * c + ALPHA * x0
                h = (1.0 - beta) * h + beta * (h @ mid_ws[i])
                h = jax.nn.leaky_relu(h, 0.01)
            return _gat_layer(h, src, dst, ea, Ws[L - 1], Wes[L - 1], a_srcs[L - 1], a_dsts[L - 1], a_edges[L - 1], biases[L - 1], n)
        return _forward(x, edge_index, edge_attr, Ws, Wes, a_srcs, a_dsts, a_edges, biases, mid_ws)

    def _L1_gnn_ref(h, src, dst, theta_w, phi_w, fc1_w, bn0_g, bn0_b, bn1_g, bn1_b):
        import jax, jax.numpy as jnp
        import numpy as np
        N, E, C = (6250, 100000, 128)
        EPS = 1e-05

        def _bn(x, g, b):
            mu = jnp.mean(x, axis=0)
            var = jnp.mean((x - mu) ** 2, axis=0)
            return g * (x - mu) * jax.lax.rsqrt(var + EPS) + b
        n = h.shape[0]
        x_src = h[src]
        x_dst = h[dst]
        e = (x_dst - x_src) @ theta_w.T + x_src @ phi_w.T
        e = jax.nn.relu(_bn(e, bn0_g, bn0_b))
        e = e @ fc1_w.T
        e = jax.nn.relu(_bn(e, bn1_g, bn1_b))
        agg = jax.ops.segment_sum(e, dst, num_segments=n)
        cnt = jax.ops.segment_sum(jnp.ones((e.shape[0],), e.dtype), dst, num_segments=n)
        x = agg / jnp.maximum(cnt, 1.0)[:, None]
        return jax.nn.relu(x + h)
    edge_index = jnp.stack([src, dst])
    h = jnp.maximum(_layernorm(x, axis=-1), 0.0)
    x = x + _L0_gnn_ref(h, edge_index, edge_attr_16, L0_gnn_Ws, L0_gnn_Wes, L0_gnn_a_srcs, L0_gnn_a_dsts, L0_gnn_a_edges, L0_gnn_biases, L0_gnn_mid_ws)
    h = jnp.maximum(_layernorm(x, axis=-1), 0.0)
    x = x + _L1_gnn_ref(h, src, dst, L1_gnn_theta_w, L1_gnn_phi_w, L1_gnn_fc1_w, L1_gnn_bn0_g, L1_gnn_bn0_b, L1_gnn_bn1_g, L1_gnn_bn1_b)
    return x

_drawn_inputs = setup_inputs


def setup_inputs(seed=0):
    import zlib

    import numpy as np

    out = dict(_drawn_inputs(seed))
    spreads = {'L0_gnn_biases': (0.0, 0.1),
     'L1_gnn_bn0_g': (1.0, 0.2),
     'L1_gnn_bn0_b': (0.0, 0.601),
     'L1_gnn_bn1_g': (1.0, 0.2),
     'L1_gnn_bn1_b': (0.0, 0.281)}
    factors = {'edge_attr_16': 8.0,
     'L0_gnn_Wes': 8.0,
     'L0_gnn_a_srcs': 8.0,
     'L0_gnn_a_dsts': 8.0,
     'L0_gnn_a_edges': 8.0,
     'L0_gnn_mid_ws': 6.345}
    for name, (base, spread) in spreads.items():
        noise = np.random.default_rng([zlib.crc32(name.encode()), seed]).standard_normal(out[name].shape)
        drawn = base * np.exp(spread * noise) if base else spread * noise
        out[name] = jnp.asarray(drawn.astype(out[name].dtype))
    for name, factor in factors.items():
        out[name] = (out[name] * factor).astype(out[name].dtype)
    return out
```

```python
import math
from contextlib import ExitStack

import numpy as np
import concourse.bass as bass
from concourse import mybir

ALU = mybir.AluOpType
ACT = mybir.ActivationFunctionType
AX = mybir.AxisListType
F32 = mybir.dt.float32
BF16 = mybir.dt.bfloat16
I32 = mybir.dt.int32
U32 = mybir.dt.uint32

P = 128
G = 4
GE = G * P
RING = 8
REC = 8
R_SRC, R_LANE, R_TERM = 0, 1, 2
NO_LANE = 255.0
BIG = 2.0 ** 100
NO_MAX = -1e20
ATT_SLOPE, OUT_SLOPE = 0.2, 0.01
ALPHA, THETA = 0.2, 0.2
EPS = 1e-5


class Chain:

    def __init__(self, eng, sem, base=0):
        self.eng, self.sem, self.base, self.n = eng, sem, base, 0

    def link(self, ins):
        self.n += 1
        ins.then_inc(self.sem, 1)
        self.eng.wait_ge(self.sem, self.base + self.n)


def at(i):
    return slice(i, i + 1) if isinstance(i, int) else bass.ds(i, 1)


def span(start, size):
    return slice(start, start + size) if isinstance(start, int) else bass.ds(start, size)


def past(i, n):
    return i >= n if isinstance(i, int) else True


def software_pipeline(eng, n, unroll, stages):
    low, high = min(o for o, _ in stages), max(o for o, _ in stages)
    first = -(-(unroll - low) // unroll)
    last = (n - high) // unroll

    def step(turn, k):
        for offset, stage in stages:
            i = turn * unroll + (k + offset)
            if not isinstance(i, int) or 0 <= i < n:
                stage(i, (k + offset) % unroll, turn + (k + offset) // unroll)

    for j in range(-high, first * unroll):
        step(j // unroll, j % unroll)
    if last > first:
        with eng.Fori(first, last) as turn:
            for k in range(unroll):
                step(turn, k)
    for j in range(max(last, first) * unroll, n - low):
        step(j // unroll, j % unroll)


def gnn_kernel(nc, x, src, dst, edge_attr_16, Ws, Wes, a_srcs, a_dsts, a_edges, biases, mid_ws,
               theta_w, phi_w, fc1_w, bn0_g, bn0_b, bn1_g, bn1_b, out):
    N, C = x.shape
    E = src.shape[0]
    ED = edge_attr_16.shape[1]
    L = Ws.shape[0]
    assert C == P and L == 5 and REC == L + 3
    NB = -(-N // P)
    TAIL = N - (NB - 1) * P
    NG = -(-((E + NB * (GE - 1)) // GE) // RING) * RING
    SLOTS = NG * GE
    NGP = -(-NG // P)
    EP = max(p for p in range(1, P + 1) if E % p == 0)
    ET = E // EP
    CH = 16
    assert ET % (2 * CH) == 0
    NCH = ET // CH
    TW = P + 2
    HW = L + 1
    LANE_BITS = 7
    betas = [math.log(THETA / (i + 1) + 1.0) for i in range(mid_ws.shape[0])]

    rec_dram = nc.dram_tensor("edge_records", [SLOTS, REC], F32, kind="Internal").ap()
    tab_dram = nc.dram_tensor("node_table", [NB * P, TW], F32, kind="Internal").ap()
    bid_dram = nc.dram_tensor("group_blocks", [NGP * P], I32, kind="Internal").ap()
    e0_dram = nc.dram_tensor("edge_features", [P, SLOTS], F32, kind="Internal").ap()
    rec_groups = rec_dram.rearrange("(g p q) w -> g p (q w)", p=P, q=G)
    tab_blocks = tab_dram.rearrange("(b p) c -> p b c", p=P)

    ctx = ExitStack()
    with ctx:
        def sb(name, shape, dt=F32):
            return ctx.enter_context(nc.sbuf_tensor(name, shape, dt))

        def sem(name):
            return ctx.enter_context(nc.semaphore(name))

        ident = sb("ident", [P, P])
        mask_ident = sb("mask_ident", [P, P], BF16)
        lane_row = sb("lane_row", [P, P])
        lane_row_b = sb("lane_row_b", [P, P], BF16)
        lane_col = sb("lane_col", [P, 1])
        before = sb("before", [P, P])
        ones = sb("ones", [P, P])
        block_rep = sb("block_rep", [P, NB, HW])
        group_no = sb("group_no", [P, NGP])
        slopes = sb("slopes", [P, 2])
        coef = sb("coef", [P, L, 4])
        eps_col = sb("eps_col", [P, 1])
        real_rows = sb("real_rows", [P, NB])
        w_ext = sb("w_ext", [P, L, TW])
        mix = sb("mix", [P, L - 1, P])
        bias_all = sb("bias_all", [P, L, P])
        mix_cur = sb("mix_cur", [P, P])
        bias_cur = sb("bias_cur", [P, P])
        uv_w = sb("uv_w", [P, 2 * P])
        fc_in = sb("fc_in", [P, P])
        fc_t = sb("fc_t", [P, P])
        fc_scaled_t = sb("fc_scaled_t", [P, P])
        term_w = sb("term_w", [P, L * ED])
        bn_par = sb("bn_par", [P, 4])
        acc = sb("acc", [P, NB, P + 1])
        hx = sb("hx", [P, NB, TW])
        x0 = sb("x0", [P, NB, P])
        ub = sb("ub", [P, NB, P])
        blk = sb("blk", [P, NB, 3])
        sums = sb("sums", [P, NB, HW])
        loop_term = sb("loop_term", [P, L, NB])
        inv_deg = sb("inv_deg", [P, NB])
        small = sb("small", [P, 8, NB])
        ln_stat = sb("ln_stat", [P, NB, 6])
        ln_mv = sb("ln_mv", [P, NB, 2])
        bid = sb("bid", [1, NGP * P], I32)
        group_block = sb("group_block", [P, 2, NGP])
        recs = sb("recs", [P, RING, G * REC])
        rows = sb("rows", [P, RING, G * TW])
        other_lane = sb("other_lane", [P, 2, G * P], BF16)
        u_edge = sb("u_edge", [P, 2, G])
        exp_pair = sb("exp_pair", [P, 2, 2, GE])
        att_t = sb("att_t", [P, 2, GE])
        att = sb("att", [P, 2, GE])
        cur = sb("cur", [P, 2, 3])
        gmax = sb("gmax", [P, 2, 4])
        shift = sb("shift", [P, 2, 3])
        rescale = sb("rescale", [P, RING, 1])
        bn_st = sb("bn_st", [P, NG, 6])
        bn_mv = sb("bn_mv", [P, 2])
        aff = sb("aff", [P, 12])
        ring_a = sb("ring_a", [P, 4, GE])
        ring_b = sb("ring_b", [P, 2, GE])
        node_ring = sb("node_ring", [P, 5, 2, P])
        hot = sb("hot", [P, 2, GE])
        ea_ring = sb("ea_ring", [EP, 2, CH, ED])
        rec_ring = sb("rec_ring", [EP, 2, CH, REC])
        slot_ring = sb("slot_ring", [EP, 2, CH], U32)
        key_ring = sb("key_ring", [EP, 2, 2, CH])
        prod = sb("prod", [EP, CH, L, ED])
        lane_hot = sb("lane_hot", [EP, 2, P])
        block_terms = sb("block_terms", [EP, 2, NB, HW])

        bank = [ctx.enter_context(nc.psum_tensor(f"bank{i}", [P, 512], F32)) for i in range(8)]

        x0_flat = x0[:, :, :].rearrange("p b c -> p (b c)")
        acc_flat = acc[:, :, :].rearrange("p b c -> p (b c)")
        assert 3 * ET <= NB * P and 4 * ET <= NB * P + ET
        slot_f = x0_flat[0:EP, 0:ET]
        lane_f = x0_flat[0:EP, ET:2 * ET]
        src_i = x0_flat[0:EP, 2 * ET:3 * ET].bitcast(I32)
        hi_f = acc_flat[0:EP, 0:ET]
        hit_i = acc_flat[0:EP, ET:2 * ET].bitcast(I32)
        run_f = acc_flat[0:EP, 2 * ET:3 * ET]
        dst_i = ub[:, :, :].rearrange("p b c -> p (b c)")[0:EP, 0:ET].bitcast(I32)
        tmp_i = ub[:, :, :].rearrange("p b c -> p (b c)")[0:EP, ET:2 * ET].bitcast(I32)
        hit_f = ub[:, :, :].rearrange("p b c -> p (b c)")[0:EP, 2 * ET:3 * ET]

        loaded = sem("loaded")
        constants_made = sem("constants_made")
        dve_chain = sem("dve_chain")
        pool_chain = sem("pool_chain")
        transposed = sem("transposed")
        copied = sem("copied")
        projected = sem("projected")
        count_chain = sem("count_chain")
        slot_chain = sem("slot_chain")
        counted = sem("counted")
        offsets_made = sem("offsets_made")
        summed = sem("summed")
        bid_stored = sem("bid_stored")
        bid_loaded = sem("bid_loaded")
        pads_made = sem("pads_made")
        pads_stored = sem("pads_stored")
        terms_landed = [sem(f"terms_landed{i}") for i in range(2)]
        scattered = [sem(f"scattered{i}") for i in range(2)]
        chunk_made = sem("chunk_made")
        column_made = sem("column_made")
        column_summed = sem("column_summed")
        chunk_chain = sem("chunk_chain")
        x_landed = sem("x_landed")
        ln_act = sem("ln_act")
        ln_counted = sem("ln_counted")
        ln_chain = sem("ln_chain")
        src_made = sem("src_made")
        src_transposed = sem("src_transposed")
        src_copied = sem("src_copied")
        src_chain = sem("src_chain")
        mixed = sem("mixed")
        mix_copied = sem("mix_copied")
        mix_bent = sem("mix_bent")
        rows_made = sem("rows_made")
        rows_copied = sem("rows_copied")
        table_ready = sem("table_ready")
        table_stored = sem("table_stored")
        table_chain = sem("table_chain")
        rec_landed = [sem(f"rec_landed{i}") for i in range(RING)]
        rows_landed = [sem(f"rows_landed{i}") for i in range(RING)]
        slot_free = sem("slot_free")
        u_made = sem("u_made")
        logits_made = sem("logits_made")
        max_chain = sem("max_chain")
        shift_made = sem("shift_made")
        exps_made = sem("exps_made")
        att_t_made = sem("att_t_made")
        att_turned = sem("att_turned")
        att_made = sem("att_made")
        acc_added = sem("acc_added")
        mrg_chain = sem("mrg_chain")
        mrg_sub = sem("mrg_sub")
        degree_chain = sem("degree_chain")
        mrg_exp = sem("mrg_exp")
        fin_chain = sem("fin_chain")
        lanes_spread = sem("lanes_spread")
        hot_made = sem("hot_made")
        feat_made = sem("feat_made")
        feat_counted = sem("feat_counted")
        feat_copied = sem("feat_copied")
        feat_stored = [sem(f"feat_stored{i}") for i in range(2)]
        bn_chain = sem("bn_chain")
        bn_chain1 = sem("bn_chain1")
        bn_ready = sem("bn_ready")
        bn_pad = sem("bn_pad")
        fc_scaled = sem("fc_scaled")
        keep_chain = sem("keep_chain")
        waited = {e: sem(f"waited_{e}") for e in ("dve", "pool", "sp")}
        bn_act = sem("bn_act")
        bn_pe = sem("bn_pe")
        feat_landed = [sem(f"feat_landed{i}") for i in range(4)]
        relu_made = sem("relu_made")
        fc_made = sem("fc_made")
        fc_counted = sem("fc_counted")
        c_landed = [sem(f"c_landed{i}") for i in range(4)]
        c_relu = sem("c_relu")
        c_hot = sem("c_hot")
        c_fc = sem("c_fc")
        c_biased = sem("c_biased")
        c_msg = sem("c_msg")
        c_summed = sem("c_summed")
        c_added = sem("c_added")
        out_made = sem("out_made")
        out_stored = sem("out_stored")

        def stand_alone(eng, name):
            eng.sem_inc(waited[name], 1)

        wst = hx[:, 0:L, 0:P]
        w_t = hx[:, L:2 * L, 0:P]
        midst = hx[:, 2 * L:2 * L + 3, 0:P]
        thst, phst = hx[:, 13, 0:P], hx[:, 14, 0:P]
        west, aest = hx[0:L * ED, 15, 0:P], hx[0:L * ED, 16, 0:P]
        a_rows = [hx[0:L, 17, 0:P], hx[0:L, 18, 0:P]]
        a_cols = small[:, 0:2, 0:L]
        term_col = small[0:L * ED, 2, 0:1]
        loads = [
            (dst_i, dst.rearrange("(p t) -> p t", p=EP)),
            (src_i, src.rearrange("(p t) -> p t", p=EP)),
            (wst, Ws.rearrange("l k j -> k l j")),
            (midst, mid_ws.rearrange("l k j -> k l j")),
            (thst, theta_w), (phst, phi_w), (fc_in[:, :], fc1_w),
            (west, Wes.rearrange("l k j -> (l k) j")),
            (a_rows[0], a_dsts), (a_rows[1], a_srcs),
        ]
        for l in range(L):
            loads.append((hx[l * ED:(l + 1) * ED, 16, 0:P], a_edges[l:l + 1, :].broadcast_to([ED, P])))
            loads.append((bias_all[:, l, :], biases[l:l + 1, :].broadcast_to([P, P])))
        for i, v in enumerate((bn0_g, bn0_b, bn1_g, bn1_b)):
            loads.append((bn_par[:, i:i + 1], v.rearrange("(p a) -> p a", a=1)))

        with nc.Block() as block:
            @block.sync
            def _(sp):
                for to, of in loads:
                    sp.dma_start(to, of).then_inc(loaded, 16)

            @block.gpsimd
            def _(pool):
                c = Chain(pool, pool_chain)
                c.link(nc.gpsimd.memset(ident[:, :], 0.0))
                c.link(nc.gpsimd.affine_select(out=ident[:, :], in_=ident[:, :], compare_op=ALU.not_equal,
                                               fill=1.0, base=0, pattern=[[-1, P]], channel_multiplier=1))
                for to, pattern, lane_step in ((lane_row[:, :], [[1, P]], 0), (lane_row_b[:, :], [[1, P]], 0),
                                               (lane_col[:, :], [[0, 1]], 1),
                                               (block_rep[:, :, :], [[1, NB], [0, HW]], 0),
                                               (group_no[:, :], [[1, NGP]], NGP)):
                    nc.gpsimd.iota(to, pattern=pattern, base=0, channel_multiplier=lane_step,
                                   allow_small_or_imprecise_dtypes=True)
                c.link(nc.gpsimd.memset(ones[:, :], 1.0))
                nc.gpsimd.affine_select(out=before[:, :], in_=ones[:, :], compare_op=ALU.is_gt,
                                        fill=0.0, base=0, pattern=[[1, P]], channel_multiplier=-1)
                nc.gpsimd.affine_select(out=real_rows[:, :], in_=ones[:, 0:NB], compare_op=ALU.is_gt,
                                        fill=0.0, base=N, pattern=[[-P, NB]], channel_multiplier=-1)
                nc.gpsimd.memset(slopes[:, 0:1], 1.0)
                nc.gpsimd.memset(slopes[:, 1:2], ATT_SLOPE)
                nc.gpsimd.memset(eps_col[:, :], EPS)
                for l in range(L):
                    own = ((1.0, 0.0, 1.0, 1.0) if l == 0 else (1.0, 0.0, 1.0, 0.0) if l == L - 1
                           else (1.0 - ALPHA, ALPHA, OUT_SLOPE, 0.0))
                    for i, v in enumerate(own):
                        nc.gpsimd.memset(coef[:, l, i:i + 1], v)
                nc.gpsimd.memset(rec_ring[:, :, :, R_TERM + L:REC], 1.0)
                nc.gpsimd.memset(small[:, :, :], 0.0).then_inc(constants_made, 1)

            @block.vector
            def _(dve):
                c = Chain(dve, dve_chain)
                dve.wait_ge(constants_made, 1)
                dve.wait_ge(loaded, 16 * len(loads))
                nc.vector.tensor_scalar(out=mask_ident[:, :], in0=ident[:, :], scalar1=-BIG, scalar2=None,
                                        op0=ALU.mult)
                nc.vector.tensor_copy(mix[:, 0, :], ident[:, :])
                for i, beta in enumerate(betas):
                    c.link(nc.vector.tensor_scalar(out=mix[:, i + 1, :], in0=ident[:, :], scalar1=1.0 - beta,
                                                   scalar2=None, op0=ALU.mult))
                    nc.vector.scalar_tensor_tensor(out=mix[:, i + 1, :], in0=midst[:, i, :], scalar=beta,
                                                   in1=mix[:, i + 1, :], op0=ALU.mult, op1=ALU.add)
                nc.vector.tensor_copy(w_ext[:, :, 0:P], wst)
                nc.vector.tensor_sub(phst, phst, thst)
                c.link(nc.vector.tensor_mul(west, west, aest))
                nc.vector.reduce_sum(term_col, west, AX.X)
                c.link(nc.vector.tensor_single_scalar(tmp_i, dst_i, LANE_BITS, op=ALU.arith_shift_right))
                c.link(nc.vector.tensor_copy(hi_f, tmp_i))
                c.link(nc.vector.tensor_single_scalar(tmp_i, dst_i, P - 1, op=ALU.bitwise_and))
                nc.vector.tensor_copy(lane_f, tmp_i)

        with nc.Block() as block:
            @block.tensor
            def _(pe):
                for l in range(L):
                    nc.tensor.transpose(bank[l // 4][:, (l % 4) * P:(l % 4 + 1) * P], wst[:, l, :], ident[:, :])
                nc.tensor.transpose(bank[2][:, 0:P], thst, ident[:, :])
                nc.tensor.transpose(bank[2][:, P:2 * P], phst, ident[:, :])
                nc.tensor.transpose(bank[2][:, 2 * P:3 * P], fc_in[:, :], ident[:, :])
                for i in range(2):
                    nc.tensor.transpose(bank[3][:, i * L:(i + 1) * L], a_rows[i], ident[0:L, 0:L])
                nc.tensor.matmul(bank[4][:, 0:L * ED], term_col.broadcast_to([L * ED, P]),
                                 ident[0:L * ED, 0:L * ED], start=True, stop=True).then_inc(transposed, 1)
                pe.wait_ge(copied, 1)
                for l in range(L):
                    last = nc.tensor.matmul(bank[5][:, 2 * l:2 * l + 2], w_t[:, l, :], a_cols[:, :, l],
                                            start=True, stop=True)
                last.then_inc(projected, 1)

            @block.vector
            def _(dve):
                dve.wait_ge(transposed, 1)
                for l in range(L):
                    nc.vector.tensor_copy(w_t[:, l, :], bank[l // 4][:, (l % 4) * P:(l % 4 + 1) * P])
                nc.vector.tensor_copy(uv_w[:, :], bank[2][:, 0:2 * P])
                nc.vector.tensor_copy(fc_t[:, :], bank[2][:, 2 * P:3 * P])
                nc.vector.tensor_copy(term_w[:, :], bank[4][:, 0:L * ED])
                nc.vector.tensor_copy(a_cols, bank[3][:, 0:2 * L].rearrange("p (s l) -> p s l", s=2))\
                    .then_inc(copied, 1)
                dve.wait_ge(projected, 1)
                nc.vector.tensor_copy(w_ext[:, :, P:P + 2],
                                      bank[5][:, 0:2 * L].rearrange("p (l s) -> p l s", s=2))

        cnt = small[0:EP, 3, :]
        total, groups, ends, base = (small[:, i, :] for i in (4, 5, 6, 7))
        ones_nb = ones[:, 0:NB]
        whole_i = small[:, 0, :].bitcast(I32)
        bid_f, bid_i = group_block[:, 0, :], group_block[:, 1, :].bitcast(I32)
        below = ln_stat[:, :, 0]
        pad = hx[:, :, :].rearrange("p b c -> p (b c)")
        PARTS = -(-(SLOTS // P * REC) // (NB * TW))
        while SLOTS // P % PARTS:
            PARTS += 1
        PR = SLOTS // P // PARTS
        pad_recs = pad[:, 0:PR * REC].rearrange("p (r w) -> p r w", w=REC)
        with nc.Block() as block:
            @block.gpsimd
            def _(pool):
                c = Chain(pool, pads_made)
                c.link(nc.gpsimd.memset(pad_recs, 0.0))
                nc.gpsimd.memset(pad_recs[:, :, R_SRC].bitcast(I32), N)
                c.link(nc.gpsimd.memset(pad_recs[:, :, R_LANE], NO_LANE))

            @block.sync
            def _(sp):
                sp.wait_ge(pads_made, 2)
                lanes = rec_dram.rearrange("(p a r) w -> a p (r w)", p=P, a=PARTS)
                for a in range(PARTS):
                    sp.dma_start(lanes[a], pad[:, 0:PR * REC]).then_inc(pads_stored, 16)
                sp.wait_ge(summed, 1)
                sp.dma_start(bid_dram.rearrange("(p j) -> p j", j=NGP), bid_i).then_inc(bid_stored, 16)
                sp.wait_ge(bid_stored, 16)
                sp.dma_start(bid[:, :], bid_dram.rearrange("(a g) -> a g", a=1)).then_inc(bid_loaded, 16)
                sp.wait_ge(bid_loaded, 16)
                sp.wait_ge(pads_stored, 16 * PARTS)

            @block.vector
            def _(dve):
                with dve.Fori(0, NB) as b:
                    Chain(dve, count_chain, b).link(
                        nc.vector.tensor_scalar(out=hit_f, in0=hi_f, scalar1=lane_row[0:EP, at(b)], scalar2=None,
                                                op0=ALU.is_equal, op1=ALU.add, accum_out=cnt[:, at(b)]))
                    stand_alone(dve, "dve")
                c = Chain(dve, offsets_made)
                c.link(nc.vector.memset(bid_f, 0.0))
                dve.wait_ge(counted, 1)
                c.link(nc.vector.tensor_scalar_add(total, bank[6][:, 64:64 + NB], float(GE - 1)))
                c.link(nc.vector.tensor_copy(whole_i, total))
                c.link(nc.vector.tensor_single_scalar(whole_i, whole_i, GE.bit_length() - 1,
                                                      op=ALU.arith_shift_right))
                c.link(nc.vector.tensor_copy(groups, whole_i))
                c.link(nc.vector.tensor_tensor_scan(ends, ones_nb, groups, 0.0, ALU.mult, ALU.add))
                c.link(nc.vector.tensor_sub(base, ends, groups))
                c.link(nc.vector.tensor_scalar(out=base, in0=base, scalar1=float(GE), scalar2=-1.0,
                                               op0=ALU.mult, op1=ALU.add))
                c.link(nc.vector.tensor_add(base, base, bank[6][:, 0:NB]))
                for j in range(NGP):
                    c.link(nc.vector.tensor_scalar(out=below, in0=ends, scalar1=group_no[:, j:j + 1], scalar2=None,
                                                   op0=ALU.is_le, op1=ALU.add, accum_out=bid_f[:, j:j + 1]))
                c.link(nc.vector.tensor_scalar_min(bid_f, bid_f, float(NB - 1)))
                nc.vector.tensor_copy(bid_i, bid_f).then_inc(summed, 1)
                with dve.Fori(0, NB) as b:
                    c = Chain(dve, slot_chain, b * 3)
                    c.link(nc.vector.tensor_scalar(out=hit_i, in0=hi_f, scalar1=lane_row[0:EP, at(b)], scalar2=None,
                                                   op0=ALU.is_equal))
                    c.link(nc.vector.tensor_tensor_scan(run_f, hit_i, hit_i, base[0:EP, at(b)],
                                                        ALU.add, ALU.bypass))
                    stand_alone(dve, "dve")
                    c.link(nc.vector.copy_predicated(slot_f, hit_i, run_f))
                    stand_alone(dve, "dve")

            @block.tensor
            def _(pe):
                pe.wait_ge(count_chain, NB)
                nc.tensor.matmul(bank[6][:, 0:NB], before[0:EP, :], cnt, start=True, stop=True)
                nc.tensor.matmul(bank[6][:, 64:64 + NB], ones[0:EP, :], cnt, start=True, stop=True)\
                    .then_inc(counted, 1)

        ea_cols = edge_attr_16.rearrange("(p t) k -> p t k", p=EP)
        node_sums = bank[7][:, 0:NB * HW]
        with nc.Block() as block:
            @block.sync
            def _(sp):
                def load(i, k, turn):
                    if past(i, 2):
                        sp.wait_ge(chunk_made, i - 1)
                    sp.dma_start(ea_ring[:, k, :, :], ea_cols[:, span(i * CH, CH), :]).then_inc(terms_landed[k], 16)
                software_pipeline(sp, NCH, 2, [(0, load)])

            @block.vector
            def _(dve):
                def chunk(i, k, turn):
                    c = Chain(dve, chunk_chain, i)
                    dve.wait_ge(terms_landed[k], 16 * (turn + 1))
                    if past(i, 2):
                        dve.wait_ge(scattered[k], 16 * CH * turn)
                    c.link(nc.vector.tensor_tensor(
                        out=prod[:, :, :, :], in0=ea_ring[:, k, :, :].rearrange("p t (a d) -> p t a d", a=1)
                        .broadcast_to([EP, CH, L, ED]),
                        in1=term_w[0:EP, :].rearrange("p (a l d) -> p a l d", a=1, l=L)
                        .broadcast_to([EP, CH, L, ED]), op=ALU.mult))
                    nc.vector.tensor_copy(rec_ring[:, k, :, R_SRC].bitcast(I32), src_i[:, span(i * CH, CH)])
                    nc.vector.tensor_copy(rec_ring[:, k, :, R_LANE], lane_f[:, span(i * CH, CH)])
                    nc.vector.tensor_copy(slot_ring[:, k, :], slot_f[:, span(i * CH, CH)])
                    nc.vector.tensor_copy(key_ring[:, k, 0, :], hi_f[:, span(i * CH, CH)])
                    nc.vector.tensor_copy(key_ring[:, k, 1, :], lane_f[:, span(i * CH, CH)])
                    nc.vector.reduce_sum(rec_ring[:, k, :, R_TERM:R_TERM + L], prod[:, :, :, :], AX.X)\
                        .then_inc(chunk_made, 1)
                    dve.wait_ge(chunk_made, i + 1)
                    for t in range(CH):
                        if t >= 2 or past(i, 1):
                            dve.wait_ge(column_summed, i * CH + t - 1)
                        nc.vector.tensor_scalar(out=lane_hot[:, t % 2, :], in0=lane_row[0:EP, :],
                                                scalar1=key_ring[:, k, 1, t:t + 1], scalar2=None, op0=ALU.is_equal)
                        nc.vector.scalar_tensor_tensor(
                            out=block_terms[:, t % 2, :, :], in0=block_rep[0:EP, :, :],
                            scalar=key_ring[:, k, 0, t:t + 1],
                            in1=rec_ring[:, k, t:t + 1, R_TERM:REC].broadcast_to([EP, NB, HW]),
                            op0=ALU.is_equal, op1=ALU.mult).then_inc(column_made, 1)

                software_pipeline(dve, NCH, 2, [(0, chunk)])
                dve.wait_ge(column_summed, ET + 1)
                nc.vector.tensor_copy(sums[:, :, :].rearrange("p b h -> p (b h)"), node_sums)

            @block.gpsimd
            def _(pool):
                def scatter(i, k, turn):
                    pool.wait_ge(chunk_made, i + 1)
                    stand_alone(pool, "pool")
                    for t in range(CH):
                        nc.gpsimd.indirect_dma_start(
                            rec_dram, bass.IndirectOffsetOnAxis(ap=slot_ring[:, k, t:t + 1], axis=0),
                            rec_ring[:, k, t, :], None).then_inc(scattered[k], 16)
                software_pipeline(pool, NCH, 2, [(0, scatter)])
                for k in range(2):
                    pool.wait_ge(scattered[k], 16 * CH * (NCH // 2))

            @block.tensor
            def _(pe):
                def column(i, k, turn):
                    for t in range(CH):
                        pe.wait_ge(column_made, i * CH + t + 1)
                        first = isinstance(i, int) and i == 0 and t == 0
                        nc.tensor.matmul(node_sums, lane_hot[:, t % 2, :],
                                         block_terms[:, t % 2, :, :].rearrange("p b h -> p (b h)"),
                                         start=first, stop=False, skip_group_check=True).then_inc(column_summed, 1)
                software_pipeline(pe, NCH, 2, [(0, column)])
                nc.tensor.matmul(node_sums, before[0:1, 0:1].broadcast_to([1, P]),
                                 block_rep[0:1, :, :].rearrange("p b h -> p (b h)"),
                                 start=False, stop=True, skip_group_check=True).then_inc(column_summed, 1)

        with nc.Block() as block:
            @block.vector
            def _(dve):
                c = Chain(dve, degree_chain)
                c.link(nc.vector.tensor_scalar_max(inv_deg[:, :], sums[:, :, L], 1.0))
                c.link(nc.vector.reciprocal(inv_deg[:, :], inv_deg[:, :]))
                for l in range(L):
                    nc.vector.tensor_mul(loop_term[:, l, :], sums[:, :, l], inv_deg[:, :])

        hp, hp_t, mx, hm_t, part = (node_ring[:, i, :, :] for i in range(5))

        def prepare_rows(block, call, source, mixed_call, weights, evacuate):
            width = weights.shape[1]
            n0 = call * NB
            m0 = 0 if mixed_call is None else mixed_call * NB

            @block.vector
            def _(dve):
                def make(i, k, turn):
                    if past(i, 2):
                        dve.wait_ge(src_transposed, n0 + i - 1)
                    source(dve, i, k).then_inc(src_made, 1)

                def bend(i, k, turn):
                    dve.wait_ge(mix_copied, m0 + i + 1)
                    if past(i, 2):
                        dve.wait_ge(rows_made, n0 + i - 1)
                    nc.vector.scalar_tensor_tensor(out=hm_t[:, k, :], in0=mx[:, k, :], scalar=mix_slope,
                                                   in1=mx[:, k, :], op0=ALU.mult, op1=ALU.max).then_inc(mix_bent, 1)
                software_pipeline(dve, NB, 2, [(0, make)] + ([] if mixed_call is None else [(-1, bend)]))

            @block.tensor
            def _(pe):
                def turn_rows(i, k, turn):
                    pe.wait_ge(src_made, n0 + i + 1)
                    if past(i, 2):
                        pe.wait_ge(src_copied, n0 + i - 1)
                    nc.tensor.transpose(bank[k][:, 0:P], hp[:, k, :], ident[:, :]).then_inc(src_transposed, 1)

                def mix_rows(i, k, turn):
                    pe.wait_ge(src_copied, n0 + i + 1)
                    if past(i, 2):
                        pe.wait_ge(mix_copied, m0 + i - 1)
                    nc.tensor.matmul(bank[2 + k][:, 0:P], mix_cur[:, :], hp_t[:, k, :], start=True, stop=True)\
                        .then_inc(mixed, 1)

                def project(i, k, turn):
                    if mixed_call is None:
                        pe.wait_ge(src_copied, n0 + i + 1)
                    else:
                        pe.wait_ge(mix_bent, m0 + i + 1)
                    if past(i, 2):
                        pe.wait_ge(rows_copied, n0 + i - 1)
                    rows_t = hp_t if mixed_call is None else hm_t
                    nc.tensor.matmul(bank[4 + k][:, 0:width], rows_t[:, k, :], weights, start=True, stop=True)\
                        .then_inc(rows_made, 1)
                software_pipeline(pe, NB, 2, [(0, turn_rows)] + ([] if mixed_call is None else [(-1, mix_rows)])
                                  + [(-2, project)])

            @block.scalar
            def _(act):
                def copy_turned(i, k, turn):
                    act.wait_ge(src_transposed, n0 + i + 1)
                    if past(i, 2):
                        if mixed_call is None:
                            act.wait_ge(rows_made, n0 + i - 1)
                        else:
                            act.wait_ge(mixed, m0 + i - 1)
                    nc.scalar.activation(hp_t[:, k, :], bank[k][:, 0:P], ACT.Copy).then_inc(src_copied, 1)

                def copy_mixed(i, k, turn):
                    act.wait_ge(mixed, m0 + i + 1)
                    if past(i, 2):
                        act.wait_ge(mix_bent, m0 + i - 1)
                    nc.scalar.activation(mx[:, k, :], bank[2 + k][:, 0:P], ACT.Copy).then_inc(mix_copied, 1)

                def copy_rows(i, k, turn):
                    act.wait_ge(rows_made, n0 + i + 1)
                    evacuate(i, bank[4 + k][:, 0:width]).then_inc(rows_copied, 1)
                software_pipeline(act, NB, 2, [(0, copy_turned)]
                                  + ([] if mixed_call is None else [(-1, copy_mixed)]) + [(-2, copy_rows)])

        def normalise(block, call, rows_in):
            @block.vector
            def _(dve):
                with dve.Fori(0, NB) as b:
                    nc.vector.bn_stats(ln_stat[:, at(b), :].rearrange("p a c -> p (a c)"),
                                       rows_in[:, at(b), :].rearrange("p a c -> p (a c)")).then_inc(ln_counted, 1)
                dve.wait_ge(ln_counted, (call + 1) * NB)
                c = Chain(dve, ln_chain, call * 6)
                mean_e, mean_o, sq_e, sq_o = (ln_stat[:, :, i] for i in (1, 4, 2, 5))
                half_gap = ln_stat[:, :, 0]
                c.link(nc.vector.tensor_add(ln_mv[:, :, 0], mean_e, mean_o))
                c.link(nc.vector.tensor_sub(half_gap, mean_e, mean_o))
                c.link(nc.vector.tensor_scalar(out=ln_mv[:, :, 0], in0=ln_mv[:, :, 0], scalar1=0.5, scalar2=None,
                                               op0=ALU.mult))
                c.link(nc.vector.tensor_mul(half_gap, half_gap, half_gap))
                c.link(nc.vector.tensor_add(sq_e, sq_e, sq_o))
                c.link(nc.vector.scalar_tensor_tensor(out=sq_e, in0=half_gap, scalar=C / 4.0, in1=sq_e,
                                                      op0=ALU.mult, op1=ALU.add))
                dve.wait_ge(ln_act, call + 1)
                nc.vector.reciprocal(ln_mv[:, :, 1], ln_stat[:, :, 3])

            @block.scalar
            def _(act):
                act.wait_ge(ln_chain, (call + 1) * 6)
                nc.scalar.activation(ln_stat[:, :, 3], ln_stat[:, :, 2], ACT.Sqrt, bias=eps_col[:, :], scale=1.0 / C)\
                    .then_inc(ln_act, 1)

        def block_of(t, b, width=None):
            view = t[:, at(b), :] if width is None else t[:, at(b), 0:width]
            return view.rearrange("p a c -> p (a c)")

        with nc.Block() as block:
            @block.vector
            def _(dve):
                dve.memset(x0[:, NB - 1, :], 0.0).then_inc(x_landed, 1)

            @block.sync
            def _(sp):
                sp.wait_ge(x_landed, 1)
                sp.dma_start(x0[:, 0:NB - 1, :], x[0:(NB - 1) * P, :].rearrange("(b p) c -> p b c", p=P))\
                    .then_inc(loaded, 16)
                sp.dma_start(x0[0:TAIL, NB - 1, :], x[(NB - 1) * P:N, :]).then_inc(loaded, 16)
                sp.wait_ge(loaded, 16 * (len(loads) + 2))

        with nc.Block() as block:
            normalise(block, 0, x0)

        def norm_relu(t, to_rows=None):
            def source(dve, i, k):
                Chain(dve, src_chain, source.base + i).link(
                    nc.vector.tensor_scalar(out=part[:, k, :], in0=block_of(t, i), scalar1=ln_mv[:, at(i), 0],
                                            scalar2=ln_mv[:, at(i), 1], op0=ALU.subtract, op1=ALU.mult))
                return nc.vector.tensor_scalar_max(hp[:, k, :], part[:, k, :], 0.0)
            source.base = 0
            return source

        def to_hx(i, product):
            return nc.scalar.activation(block_of(hx, i), product, ACT.Copy)

        mix_slope = coef[:, 0, 2:3]
        with nc.Block() as block:
            prepare_rows(block, 0, norm_relu(x0), None, w_ext[:, 0, :], to_hx)

        def store_table(call):
            with nc.Block() as block:
                @block.vector
                def _(dve):
                    c = Chain(dve, table_chain, call)
                    nc.vector.tensor_copy(blk[:, :, 0], hx[:, :, P])
                    c.link(nc.vector.tensor_scalar_mul(blk[:, :, 1], hx[:, :, P], ATT_SLOPE))
                    nc.vector.memset(hx[:, :, P], 1.0).then_inc(table_ready, 1)
                    nc.vector.memset(blk[:, :, 2], NO_MAX)

                @block.gpsimd
                def _(pool):
                    nc.gpsimd.memset(acc[:, :, :], 0.0)

                @block.sync
                def _(sp):
                    sp.wait_ge(table_ready, call + 1)
                    sp.dma_start(tab_blocks, hx[:, :, :]).then_inc(table_stored, 16)
                    sp.wait_ge(table_stored, 16 * (call + 1))
                    stand_alone(sp, "sp")

        def rec_word(k, q, word):
            return recs[:, k, q * REC + word:q * REC + word + 1]

        def row_words(k, q, lo, hi):
            return rows[:, k, q * TW + lo:q * TW + hi]

        def stream_rows(block, layer):
            g0 = layer * NG
            t0 = layer * (NG // RING)

            @block.sync
            def _(sp):
                def load(i, k, turn):
                    sp.wait_ge(slot_free, g0 + i + 1)
                    sp.dma_start(recs[:, k, :], rec_groups[at(i)].rearrange("a p w -> (a p) w"))\
                        .then_inc(rec_landed[k], 16)
                software_pipeline(sp, NG, RING, [(0, load)])

            @block.gpsimd
            def _(pool):
                def gather(i, k, turn):
                    pool.wait_ge(rec_landed[k], 16 * (t0 + turn + 1))
                    stand_alone(pool, "pool")
                    for q in range(G):
                        nc.gpsimd.indirect_dma_start(
                            row_words(k, q, 0, TW), None, tab_dram,
                            bass.IndirectOffsetOnAxis(ap=rec_word(k, q, R_SRC).bitcast(U32), axis=0))\
                            .then_inc(rows_landed[k], 16)
                software_pipeline(pool, NG, RING, [(0, gather)])

        MAX_LINKS = 4

        def attend(block, layer):
            g0 = layer * NG
            t0 = layer * (NG // RING)
            term_word = R_TERM + layer
            stream_rows(block, layer)

            @block.vector
            def _(dve):
                def edge_side(i, k, turn):
                    r = k % 2
                    dve.wait_ge(rec_landed[k], 16 * (t0 + turn + 1))
                    for q in range(G):
                        nc.vector.tensor_scalar(out=other_lane[:, r, q * P:(q + 1) * P], in0=lane_row_b[:, :],
                                                scalar1=rec_word(k, q, R_LANE), scalar2=None,
                                                op0=ALU.not_equal)
                    dve.wait_ge(rows_landed[k], 16 * G * (t0 + turn + 1))
                    nc.vector.tensor_add(
                        u_edge[:, r, :], rows[:, k, :].rearrange("p (q w) -> p q w", w=TW)[:, :, P + 1],
                        recs[:, k, :].rearrange("p (q w) -> p q w", w=REC)[:, :, at(term_word)]
                        .rearrange("p q a -> p (q a)")).then_inc(u_made, 1)

                def maximum(i, k, turn):
                    r = k % 2
                    c = Chain(dve, max_chain, (g0 + i) * MAX_LINKS)
                    b = dve.value_load(bid[0:1, at(i)], min_val=0, max_val=NB - 1)
                    nc.vector.tensor_copy(cur[:, r, :], block_of(blk, b))
                    dve.wait_ge(logits_made, g0 + i + 1)
                    c.link(nc.vector.reduce_max(gmax[:, r, 0:1], bank[r][:, :], AX.X))
                    c.link(nc.vector.scalar_tensor_tensor(out=gmax[:, r, 1:3], in0=slopes[:, :],
                                                          scalar=gmax[:, r, 0:1], in1=cur[:, r, 0:2],
                                                          op0=ALU.mult, op1=ALU.add))
                    c.link(nc.vector.tensor_scalar(out=gmax[:, r, 3:4], in0=gmax[:, r, 1:2],
                                                   scalar1=gmax[:, r, 2:3], scalar2=cur[:, r, 2:3],
                                                   op0=ALU.max, op1=ALU.max))
                    nc.vector.tensor_scalar(out=shift[:, r, :], in0=cur[:, r, :], scalar1=gmax[:, r, 3:4],
                                            scalar2=None, op0=ALU.subtract).then_inc(shift_made, 1)
                    c.link(nc.vector.tensor_copy(blk[:, at(b), 2], gmax[:, r, 3:4]))

                def larger_exp(i, k, turn):
                    r = k % 2
                    dve.wait_ge(exps_made, g0 + i + 1)
                    if past(i, 2):
                        dve.wait_ge(att_turned, g0 + i - 1)
                    nc.vector.tensor_max(att_t[:, r, :], exp_pair[:, r, 0, :], exp_pair[:, r, 1, :])\
                        .then_inc(att_t_made, 1)

                def accumulate(i, k, turn):
                    b = dve.value_load(bid[0:1, at(i)], min_val=0, max_val=NB - 1)
                    dve.wait_ge(slot_free, RING + g0 + i + 1)
                    if past(i, 1):
                        dve.wait_ge(acc_added, g0 + i)
                    nc.vector.scalar_tensor_tensor(out=block_of(acc, b), in0=block_of(acc, b),
                                                   scalar=rescale[:, k, :], in1=bank[4 + k % 2][:, 0:P + 1],
                                                   op0=ALU.mult, op1=ALU.add).then_inc(acc_added, 1)
                software_pipeline(dve, NG, RING, [(0, maximum), (-1, larger_exp), (2, edge_side), (-4, accumulate)])

            @block.tensor
            def _(pe):
                def logits(i, k, turn):
                    r = k % 2
                    pe.wait_ge(u_made, g0 + i + 1)
                    if past(i, 2):
                        pe.wait_ge(exps_made, g0 + i - 1)
                    for q in range(G):
                        nc.tensor.matmul(bank[r][:, q * P:(q + 1) * P], u_edge[:, r, q:q + 1].broadcast_to([P, P]),
                                         ident[:, :], start=True, stop=False)
                        last = nc.tensor.matmul(bank[r][:, q * P:(q + 1) * P], other_lane[:, r, q * P:(q + 1) * P],
                                                mask_ident[:, :], start=False, stop=True)
                    last.then_inc(logits_made, 1)

                def turn_att(i, k, turn):
                    r = k % 2
                    pe.wait_ge(att_t_made, g0 + i + 1)
                    if past(i, 2):
                        pe.wait_ge(att_made, g0 + i - 1)
                    for q in range(G):
                        last = nc.tensor.transpose(bank[2 + r][:, q * P:(q + 1) * P],
                                                   att_t[:, r, q * P:(q + 1) * P], ident[:, :])
                    last.then_inc(att_turned, 1)

                def weigh(i, k, turn):
                    r = k % 2
                    pe.wait_ge(att_made, g0 + i + 1)
                    pe.wait_ge(rows_landed[k], 16 * G * (t0 + turn + 1))
                    if past(i, 2):
                        pe.wait_ge(acc_added, g0 + i - 1)
                    for q in range(G):
                        last = nc.tensor.matmul(bank[4 + r][:, 0:P + 1], att[:, r, q * P:(q + 1) * P],
                                                row_words(k, q, 0, P + 1), start=(q == 0), stop=(q == G - 1))
                    last.then_inc(slot_free, 1)
                software_pipeline(pe, NG, RING, [(-3, weigh), (2, logits), (-1, turn_att)])

            @block.scalar
            def _(act):
                def exps(i, k, turn):
                    r = k % 2
                    act.wait_ge(shift_made, g0 + i + 1)
                    if past(i, 2):
                        act.wait_ge(att_t_made, g0 + i - 1)
                    nc.scalar.activation(rescale[:, k, :], shift[:, r, 2:3], ACT.Exp)
                    nc.scalar.activation(exp_pair[:, r, 0, :], bank[r][:, :], ACT.Exp, bias=shift[:, r, 0:1])
                    nc.scalar.activation(exp_pair[:, r, 1, :], bank[r][:, :], ACT.Exp, bias=shift[:, r, 1:2],
                                         scale=ATT_SLOPE).then_inc(exps_made, 1)

                def copy_att(i, k, turn):
                    r = k % 2
                    act.wait_ge(att_turned, g0 + i + 1)
                    if past(i, 2):
                        act.wait_ge(slot_free, RING + g0 + i - 1)
                    nc.scalar.activation(att[:, r, :], bank[2 + r][:, :], ACT.Copy).then_inc(att_made, 1)
                software_pipeline(act, NG, RING, [(0, exps), (-2, copy_att)])

        MERGE_LINKS = 9
        from_acc, from_self = small[:, 0, :], small[:, 1, :]

        def merge_self_loops(layer):
            logit, sloped, top, diff, weight, share = (small[:, i, :] for i in range(2, 8))
            share_of_conv = coef[:, at(layer), 0]
            with nc.Block() as block:
                @block.vector
                def _(dve):
                    c = Chain(dve, mrg_chain, layer * MERGE_LINKS)
                    nc.vector.tensor_copy(mix_cur[:, :], block_of(mix, min_layer(layer)))
                    nc.vector.tensor_scalar(out=bias_cur[:, :], in0=block_of(bias_all, layer), scalar1=share_of_conv,
                                            scalar2=None, op0=ALU.mult)
                    c.link(nc.vector.tensor_add(logit, hx[:, :, P + 1], blk[:, :, 0]))
                    c.link(nc.vector.tensor_add(logit, logit, loop_term[:, at(layer), :].rearrange("p a b -> p (a b)")))
                    c.link(nc.vector.scalar_tensor_tensor(out=sloped, in0=logit, scalar=ATT_SLOPE, in1=logit,
                                                          op0=ALU.mult, op1=ALU.max))
                    c.link(nc.vector.tensor_max(top, sloped, blk[:, :, 2]))
                    c.link(nc.vector.tensor_sub(diff, blk[:, :, 2], top))
                    nc.vector.tensor_sub(logit, sloped, top).then_inc(mrg_sub, 1)
                    dve.wait_ge(mrg_exp, layer + 1)
                    c.link(nc.vector.tensor_mul(weight, acc[:, :, P], from_acc))
                    c.link(nc.vector.tensor_add(weight, weight, from_self))
                    c.link(nc.vector.reciprocal(share, weight))
                    c.link(nc.vector.tensor_scalar(out=share, in0=share, scalar1=share_of_conv, scalar2=None,
                                                   op0=ALU.mult))
                    nc.vector.tensor_mul(from_acc, from_acc, share)
                    nc.vector.tensor_mul(from_self, from_self, share)

                @block.scalar
                def _(act):
                    act.wait_ge(mrg_sub, layer + 1)
                    nc.scalar.activation(from_acc, diff, ACT.Exp)
                    nc.scalar.activation(from_self, logit, ACT.Exp).then_inc(mrg_exp, 1)

        def min_layer(layer):
            return min(layer, L - 2) if isinstance(layer, int) else layer

        CONV_LINKS = 3

        def layer_output(dve, chain, i, k):
            chain.link(nc.vector.scalar_tensor_tensor(out=part[:, k, :], in0=block_of(acc, i, P),
                                                      scalar=from_acc[:, at(i)], in1=bias_cur[:, :],
                                                      op0=ALU.mult, op1=ALU.add))
            chain.link(nc.vector.scalar_tensor_tensor(out=part[:, k, :], in0=block_of(hx, i, P),
                                                      scalar=from_self[:, at(i)], in1=part[:, k, :],
                                                      op0=ALU.mult, op1=ALU.add))

        with nc.Block() as block:
            @block.vector
            def _(dve):
                nc.vector.memset(x0[:, :, :], 0.0)

            @block.gpsimd
            def _(pool):
                pool.sem_inc(slot_free, RING)

        with nc.Fori(0, L - 1) as layer:
            store_table(layer)
            with nc.Block() as block:
                attend(block, layer)
            merge_self_loops(layer)
            mix_slope = coef[:, at(layer), 2]

            def residual(dve, i, k):
                c = Chain(dve, src_chain, NB + (layer * NB + i) * CONV_LINKS)
                layer_output(dve, c, i, k)
                c.link(nc.vector.scalar_tensor_tensor(out=block_of(x0, i), in0=part[:, k, :],
                                                      scalar=coef[:, at(layer), 3], in1=block_of(x0, i),
                                                      op0=ALU.mult, op1=ALU.add))
                return nc.vector.scalar_tensor_tensor(out=hp[:, k, :], in0=block_of(x0, i),
                                                      scalar=coef[:, at(layer), 1], in1=part[:, k, :],
                                                      op0=ALU.mult, op1=ALU.add)
            with nc.Block() as block:
                prepare_rows(block, layer + 1, residual, layer,
                             w_ext[:, bass.ds(layer + 1, 1), :].rearrange("p a c -> p (a c)"), to_hx)

        store_table(L - 1)
        with nc.Block() as block:
            attend(block, L - 1)

            @block.scalar
            def _(act):
                act.dma_start(x0[:, 0:NB - 1, :], x[0:(NB - 1) * P, :].rearrange("(b p) c -> p b c", p=P))\
                    .then_inc(loaded, 16)
                act.dma_start(x0[0:TAIL, NB - 1, :], x[(NB - 1) * P:N, :]).then_inc(loaded, 16)
        merge_self_loops(L - 1)

        FIN0 = NB + (L - 1) * NB * CONV_LINKS
        with nc.Block() as block:
            @block.vector
            def _(dve):
                dve.wait_ge(loaded, 16 * (len(loads) + 4))

                def add(i, k, turn):
                    c = Chain(dve, src_chain, FIN0 + i * CONV_LINKS)
                    layer_output(dve, c, i, k)
                    c.link(nc.vector.tensor_add(block_of(x0, i), block_of(x0, i), part[:, k, :]))
                software_pipeline(dve, NB, 2, [(0, add)])

        with nc.Block() as block:
            normalise(block, 1, x0)

        def norm_relu_kept(dve, i, k):
            c = Chain(dve, keep_chain, i * 2)
            c.link(nc.vector.tensor_scalar(out=part[:, k, :], in0=block_of(x0, i), scalar1=ln_mv[:, at(i), 0],
                                           scalar2=ln_mv[:, at(i), 1], op0=ALU.subtract, op1=ALU.mult))
            c.link(nc.vector.tensor_scalar(out=block_of(hx, i, P), in0=part[:, k, :], scalar1=real_rows[:, at(i)],
                                           scalar2=0.0, op0=ALU.mult, op1=ALU.max))
            return nc.vector.tensor_scalar_max(hp[:, k, :], block_of(hx, i, P), 0.0)

        def to_uv(i, product):
            nc.scalar.activation(block_of(ub, i), product[:, 0:P], ACT.Copy)
            return nc.scalar.activation(block_of(acc, i, P), product[:, P:2 * P], ACT.Copy)

        with nc.Block() as block:
            prepare_rows(block, L, norm_relu_kept, None, uv_w[:, :], to_uv)

        with nc.Block() as block:
            @block.sync
            def _(sp):
                sp.dma_start(tab_blocks[:, :, 0:P], acc[:, :, 0:P]).then_inc(table_stored, 16)
                sp.wait_ge(table_stored, 16 * (L + 1))

        hot_t = exp_pair[:, :, 0, :]
        u_cur = exp_pair[:, :, 1, 0:P]
        feat = ring_b
        g0, t0 = L * NG, L * (NG // RING)
        with nc.Block() as block:
            stream_rows(block, L)

            @block.tensor
            def _(pe):
                def spread_lanes(i, k, turn):
                    r = k % 2
                    pe.wait_ge(rec_landed[k], 16 * (t0 + turn + 1))
                    if past(i, 2):
                        pe.wait_ge(hot_made, i - 1)
                    for q in range(G):
                        last = nc.tensor.matmul(bank[r][:, q * P:(q + 1) * P],
                                                rec_word(k, q, R_LANE).broadcast_to([P, P]), ident[:, :],
                                                start=True, stop=True)
                    last.then_inc(lanes_spread, 1)

                def features(i, k, turn):
                    r = k % 2
                    pe.wait_ge(hot_made, i + 1)
                    pe.wait_ge(rows_landed[k], 16 * G * (t0 + turn + 1))
                    if past(i, 2):
                        pe.wait_ge(feat_copied, i - 1)
                    nc.tensor.matmul(bank[2 + r][:, :], u_cur[:, r, :], hot_t[:, r, :], start=True, stop=False)
                    for q in range(G):
                        last = nc.tensor.matmul(bank[2 + r][:, q * P:(q + 1) * P], row_words(k, q, 0, P),
                                                ident[:, :], start=False, stop=(q == G - 1))
                    last.then_inc(slot_free, 1)
                software_pipeline(pe, NG, RING, [(1, spread_lanes), (0, features)])

            @block.vector
            def _(dve):
                def one_hot(i, k, turn):
                    r = k % 2
                    b = dve.value_load(bid[0:1, at(i)], min_val=0, max_val=NB - 1)
                    if past(i, 2):
                        dve.wait_ge(slot_free, RING + g0 + i - 1)
                        stand_alone(dve, "dve")
                    nc.vector.tensor_copy(u_cur[:, r, :], block_of(ub, b))
                    dve.wait_ge(lanes_spread, i + 1)
                    nc.vector.tensor_scalar(out=hot_t[:, r, :], in0=bank[r][:, :], scalar1=lane_col[:, :],
                                            scalar2=None, op0=ALU.is_equal).then_inc(hot_made, 1)

                def count(i, k, turn):
                    dve.wait_ge(feat_copied, i + 1)
                    nc.vector.bn_stats(bn_st[:, at(i), :].rearrange("p a c -> p (a c)"), feat[:, k % 2, :])\
                        .then_inc(feat_counted, 1)
                software_pipeline(dve, NG, RING, [(1, one_hot), (-1, count)])

            @block.scalar
            def _(act):
                def store(i, k, turn):
                    r = k % 2
                    act.wait_ge(slot_free, RING + g0 + i + 1)
                    if past(i, 2):
                        act.wait_ge(feat_counted, i - 1)
                        act.wait_ge(feat_stored[r], 16 * stored_turns(i, k, turn))
                    nc.scalar.activation(feat[:, r, :], bank[2 + r][:, :], ACT.Copy).then_inc(feat_copied, 1)
                    act.wait_ge(feat_copied, i + 1)
                    act.dma_start(e0_dram[:, span(i * GE, GE)], feat[:, r, :]).then_inc(feat_stored[r], 16)

                def stored_turns(i, k, turn):
                    return turn * (RING // 2) + k // 2
                software_pipeline(act, NG, RING, [(0, store)])
                for r in range(2):
                    act.wait_ge(feat_stored[r], 16 * (NG // 2))

        FILL = SLOTS / E
        mean, var, scale, shift_c, tmp, pad_y = (aff[:, i:i + 1] for i in range(6))
        scale1, shift1 = aff[:, 6:7], aff[:, 7:8]

        def affine(dve, act_turn, c, gamma, beta, to_scale, to_shift):
            c.link(nc.vector.tensor_mul(tmp, mean, mean))
            nc.vector.tensor_sub(var, var, tmp).then_inc(bn_ready, 1)
            dve.wait_ge(bn_act, act_turn)
            c.link(nc.vector.reciprocal(var, var))
            c.link(nc.vector.tensor_mul(to_scale, var, gamma))
            c.link(nc.vector.tensor_mul(tmp, mean, to_scale))
            c.link(nc.vector.tensor_sub(to_shift, beta, tmp))

        def whole_moments(c, factor):
            c.link(nc.vector.bn_aggr(bn_mv[:, :], bn_st[:, :, :].rearrange("p a c -> p (a c)")))
            c.link(nc.vector.tensor_mul(tmp, bn_mv[:, 0:1], bn_mv[:, 0:1]))
            c.link(nc.vector.tensor_add(var, bn_mv[:, 1:2], tmp))
            c.link(nc.vector.tensor_scalar(out=var, in0=var, scalar1=factor, scalar2=None, op0=ALU.mult))
            c.link(nc.vector.tensor_scalar(out=mean, in0=bn_mv[:, 0:1], scalar1=factor, scalar2=None, op0=ALU.mult))

        def square_root(act, turn):
            act.wait_ge(bn_ready, turn)
            nc.scalar.activation(var, var, ACT.Sqrt, bias=eps_col[:, :]).then_inc(bn_act, 1)

        with nc.Block() as block:
            @block.vector
            def _(dve):
                c = Chain(dve, bn_chain)
                whole_moments(c, FILL)
                affine(dve, 1, c, bn_par[:, 0:1], bn_par[:, 1:2], scale, shift_c)
                nc.vector.tensor_scalar_max(tmp, shift_c, 0.0).then_inc(bn_pad, 1)

            @block.scalar
            def _(act):
                square_root(act, 1)

        feat_in, relued = ring_a, ring_b
        with nc.Block() as block:
            @block.sync
            def _(sp):
                def load(i, k, turn):
                    if past(i, 4):
                        sp.wait_ge(relu_made, i - 3)
                    sp.dma_start(feat_in[:, k % 4, :], e0_dram[:, span(i * GE, GE)]).then_inc(feat_landed[k % 4], 16)
                software_pipeline(sp, NG, RING, [(0, load)])

            @block.scalar
            def _(act):
                def relu(i, k, turn):
                    act.wait_ge(feat_landed[k % 4], 16 * (turn * 2 + k // 4 + 1))
                    if past(i, 2):
                        act.wait_ge(fc_made, i - 1)
                    nc.scalar.activation(relued[:, k % 2, :], feat_in[:, k % 4, :], ACT.Relu, bias=shift_c, scale=scale)\
                        .then_inc(relu_made, 1)
                software_pipeline(act, NG, RING, [(0, relu)])

            @block.tensor
            def _(pe):
                def multiply(i, k, turn):
                    pe.wait_ge(relu_made, i + 1)
                    if past(i, 2):
                        pe.wait_ge(fc_counted, i - 1)
                    nc.tensor.matmul(bank[k % 2][:, :], fc_t[:, :], relued[:, k % 2, :], start=True, stop=True)\
                        .then_inc(fc_made, 1)
                software_pipeline(pe, NG, RING, [(0, multiply)])
                pe.wait_ge(bn_pad, 1)
                nc.tensor.matmul(bank[2][:, 0:1], fc_t[:, :], tmp, start=True, stop=True).then_inc(bn_pe, 1)

            @block.vector
            def _(dve):
                def count(i, k, turn):
                    dve.wait_ge(fc_made, i + 1)
                    nc.vector.bn_stats(bn_st[:, at(i), :].rearrange("p a c -> p (a c)"), bank[k % 2][:, :])\
                        .then_inc(fc_counted, 1)
                software_pipeline(dve, NG, RING, [(0, count)])
                dve.wait_ge(bn_pe, 1)
                nc.vector.tensor_copy(pad_y, bank[2][:, 0:1])

        EMPTY = (SLOTS - E) / E
        shift_row = ring_b
        with nc.Block() as block:
            @block.vector
            def _(dve):
                c = Chain(dve, bn_chain1)
                whole_moments(c, FILL)
                c.link(nc.vector.scalar_tensor_tensor(out=mean, in0=pad_y, scalar=-EMPTY, in1=mean,
                                                      op0=ALU.mult, op1=ALU.add))
                c.link(nc.vector.tensor_mul(tmp, pad_y, pad_y))
                c.link(nc.vector.scalar_tensor_tensor(out=var, in0=tmp, scalar=-EMPTY, in1=var,
                                                      op0=ALU.mult, op1=ALU.add))
                affine(dve, 2, c, bn_par[:, 2:3], bn_par[:, 3:4], scale1, shift1)
                nc.vector.tensor_scalar(out=fc_in[:, :], in0=fc_in[:, :], scalar1=scale1, scalar2=None, op0=ALU.mult)\
                    .then_inc(fc_scaled, 1)
                dve.wait_ge(bn_pe, 2)
                nc.vector.tensor_copy(fc_scaled_t[:, :], bank[0][:, 0:P])
                for q in range(G):
                    nc.vector.tensor_copy(shift_row[:, 0, q * P:(q + 1) * P], bank[0][:, P:2 * P])
                nc.vector.memset(acc[:, :, :], 0.0)

            @block.scalar
            def _(act):
                square_root(act, 2)

            @block.tensor
            def _(pe):
                pe.wait_ge(fc_scaled, 1)
                nc.tensor.transpose(bank[0][:, 0:P], fc_in[:, :], ident[:, :])
                nc.tensor.matmul(bank[0][:, P:2 * P], shift1.broadcast_to([P, P]), ident[:, :], start=True, stop=True)\
                    .then_inc(bn_pe, 1)

        relued3 = att_t
        lane_hots, biased, message = exp_pair, att, hot
        with nc.Block() as block:
            @block.sync
            def _(sp):
                def load(i, k, turn):
                    if past(i, 4):
                        sp.wait_ge(c_summed, i - 3)
                    sp.dma_start(recs[:, k % 4, :], rec_groups[at(i)].rearrange("a p w -> (a p) w"))\
                        .then_inc(c_landed[k % 4], 16)
                    sp.dma_start(feat_in[:, k % 4, :], e0_dram[:, span(i * GE, GE)]).then_inc(c_landed[k % 4], 16)
                software_pipeline(sp, NG, RING, [(0, load)])

            @block.scalar
            def _(act):
                def relu(i, k, turn):
                    act.wait_ge(c_landed[k % 4], 32 * (turn * 2 + k // 4 + 1))
                    if past(i, 2):
                        act.wait_ge(c_fc, i - 1)
                    nc.scalar.activation(relued3[:, k % 2, :], feat_in[:, k % 4, :], ACT.Relu, bias=shift_c, scale=scale)\
                        .then_inc(c_relu, 1)

                def relu_message(i, k, turn):
                    act.wait_ge(c_biased, i + 1)
                    if past(i, 2):
                        act.wait_ge(c_summed, i - 1)
                    nc.scalar.activation(message[:, k % 2, :], biased[:, k % 2, :], ACT.Relu).then_inc(c_msg, 1)
                software_pipeline(act, NG, RING, [(1, relu), (-1, relu_message)])

            @block.tensor
            def _(pe):
                def multiply(i, k, turn):
                    pe.wait_ge(c_relu, i + 1)
                    if past(i, 2):
                        pe.wait_ge(c_biased, i - 1)
                    for q in range(G):
                        last = nc.tensor.matmul(bank[k % 2][:, q * P:(q + 1) * P],
                                                relued3[:, k % 2, q * P:(q + 1) * P], fc_scaled_t[:, :],
                                                start=True, stop=True)
                    last.then_inc(c_fc, 1)

                def add_up(i, k, turn):
                    pe.wait_ge(c_msg, i + 1)
                    pe.wait_ge(c_hot, i + 1)
                    if past(i, 2):
                        pe.wait_ge(c_added, i - 1)
                    for q in range(G):
                        last = nc.tensor.matmul(bank[2 + k % 2][:, 0:P], lane_hots[:, k % 2, 0, q * P:(q + 1) * P],
                                                message[:, k % 2, q * P:(q + 1) * P],
                                                start=(q == 0), stop=(q == G - 1))
                    last.then_inc(c_summed, 1)
                software_pipeline(pe, NG, RING, [(1, multiply), (-1, add_up)])

            @block.vector
            def _(dve):
                def hots(i, k, turn):
                    dve.wait_ge(c_landed[k % 4], 32 * (turn * 2 + k // 4 + 1))
                    if past(i, 2):
                        dve.wait_ge(c_summed, i - 1)
                    for q in range(G):
                        last = nc.vector.tensor_scalar(out=lane_hots[:, k % 2, 0, q * P:(q + 1) * P], in0=lane_row[:, :],
                                                       scalar1=rec_word(k % 4, q, R_LANE), scalar2=None,
                                                       op0=ALU.is_equal)
                    last.then_inc(c_hot, 1)

                def add_shift(i, k, turn):
                    dve.wait_ge(c_fc, i + 1)
                    if past(i, 2):
                        dve.wait_ge(c_msg, i - 1)
                    nc.vector.tensor_add(biased[:, k % 2, :], bank[k % 2][:, :], shift_row[:, 0, :])\
                        .then_inc(c_biased, 1)

                def add_group(i, k, turn):
                    b = dve.value_load(bid[0:1, at(i)], min_val=0, max_val=NB - 1)
                    dve.wait_ge(c_summed, i + 1)
                    if past(i, 1):
                        dve.wait_ge(c_added, i)
                    nc.vector.tensor_add(block_of(acc, b, P), block_of(acc, b, P), bank[2 + k % 2][:, 0:P])\
                        .then_inc(c_added, 1)
                software_pipeline(dve, NG, RING, [(0, add_shift), (0, hots), (-2, add_group)])

        with nc.Block() as block:
            @block.vector
            def _(dve):
                def finish(i, k, turn):
                    c = Chain(dve, fin_chain, i)
                    c.link(nc.vector.scalar_tensor_tensor(out=part[:, k, :], in0=block_of(acc, i, P),
                                                          scalar=inv_deg[:, at(i)], in1=block_of(hx, i, P),
                                                          op0=ALU.mult, op1=ALU.add))
                    nc.vector.scalar_tensor_tensor(out=block_of(ub, i), in0=part[:, k, :], scalar=0.0,
                                                   in1=block_of(x0, i), op0=ALU.max, op1=ALU.add)\
                        .then_inc(out_made, 1)
                software_pipeline(dve, NB, 2, [(0, finish)])

            @block.sync
            def _(sp):
                sp.wait_ge(out_made, NB)
                sp.dma_start(out[0:(NB - 1) * P, :].rearrange("(b p) c -> p b c", p=P), ub[:, 0:NB - 1, :])\
                    .then_inc(out_stored, 16)
                sp.dma_start(out[(NB - 1) * P:N, :], ub[0:TAIL, NB - 1, :]).then_inc(out_stored, 16)
                sp.wait_ge(out_stored, 32)

    return None


_INS = ['x', 'src', 'dst', 'edge_attr_16', 'L0_gnn_Ws', 'L0_gnn_Wes', 'L0_gnn_a_srcs', 'L0_gnn_a_dsts',
        'L0_gnn_a_edges', 'L0_gnn_biases', 'L0_gnn_mid_ws', 'L1_gnn_theta_w', 'L1_gnn_phi_w', 'L1_gnn_fc1_w',
        'L1_gnn_bn0_g', 'L1_gnn_bn0_b', 'L1_gnn_bn1_g', 'L1_gnn_bn1_b']


def kernel(**inputs):
    import concourse.bacc as bacc
    from concourse.bass_utils import run_bass_kernel_spmd

    nc = bacc.Bacc("TRN2", target_bir_lowering=False, num_devices=1)
    arrays, args = {}, []
    for name in _INS:
        a = np.ascontiguousarray(inputs[name])
        arrays[f"in_{name}"] = a
        args.append(nc.dram_tensor(f"in_{name}", a.shape, mybir.dt.from_np(a.dtype), kind="ExternalInput").ap())
    shape = tuple(inputs['x'].shape)
    out = nc.dram_tensor("out", shape, F32, kind="ExternalOutput").ap()
    gnn_kernel(nc, *args, out)
    r = run_bass_kernel_spmd(nc, [arrays], core_ids=[0])
    return r.results[0]["out"]
```

```python
import math
from contextlib import ExitStack

import numpy as np
import concourse.bass as bass
from concourse import mybir

ALU = mybir.AluOpType
ACT = mybir.ActivationFunctionType
AX = mybir.AxisListType
F32 = mybir.dt.float32
BF16 = mybir.dt.bfloat16
I32 = mybir.dt.int32
U32 = mybir.dt.uint32

P = 128
G = 4
GE = G * P
RING = 8
REC = 8
R_SRC, R_LANE, R_TERM = 0, 1, 2
NO_LANE = 255.0
BIG = 2.0 ** 100
NO_MAX = -1e20
ATT_SLOPE, OUT_SLOPE = 0.2, 0.01
ALPHA, THETA = 0.2, 0.2
EPS = 1e-5


class Chain:

    def __init__(self, eng, sem, base=0):
        self.eng, self.sem, self.base, self.n = eng, sem, base, 0

    def link(self, ins):
        self.n += 1
        ins.then_inc(self.sem, 1)
        self.eng.wait_ge(self.sem, self.base + self.n)


def at(i):
    return slice(i, i + 1) if isinstance(i, int) else bass.ds(i, 1)


def span(start, size):
    return slice(start, start + size) if isinstance(start, int) else bass.ds(start, size)


def past(i, n):
    return i >= n if isinstance(i, int) else True


def software_pipeline(eng, n, unroll, stages):
    low, high = min(o for o, _ in stages), max(o for o, _ in stages)
    first = -(-(unroll - low) // unroll)
    last = (n - high) // unroll

    def step(turn, k):
        for offset, stage in stages:
            i = turn * unroll + (k + offset)
            if not isinstance(i, int) or 0 <= i < n:
                stage(i, (k + offset) % unroll, turn + (k + offset) // unroll)

    for j in range(-high, first * unroll):
        step(j // unroll, j % unroll)
    if last > first:
        with eng.Fori(first, last) as turn:
            for k in range(unroll):
                step(turn, k)
    for j in range(max(last, first) * unroll, n - low):
        step(j // unroll, j % unroll)


def gnn_kernel(nc, x, src, dst, edge_attr_16, Ws, Wes, a_srcs, a_dsts, a_edges, biases, mid_ws,
               theta_w, phi_w, fc1_w, bn0_g, bn0_b, bn1_g, bn1_b, out):
    N, C = x.shape
    E = src.shape[0]
    ED = edge_attr_16.shape[1]
    L = Ws.shape[0]
    assert C == P and L == 5 and REC == L + 3
    NB = -(-N // P)
    TAIL = N - (NB - 1) * P
    NG = -(-((E + NB * (GE - 1)) // GE) // RING) * RING
    SLOTS = NG * GE
    NGP = -(-NG // P)
    EP = max(p for p in range(1, P + 1) if E % p == 0)
    ET = E // EP
    CH = 32
    TC = P // ED
    BATCH = 8
    assert ET % (2 * CH) == 0 and CH * ED == GE and P % ED == 0 and NG % BATCH == 0
    NCH = ET // CH
    TW = P + 2
    HW = L + 1
    LANE_BITS = 7
    betas = [math.log(THETA / (i + 1) + 1.0) for i in range(mid_ws.shape[0])]

    listed_dram = nc.dram_tensor("records_as_listed", [E + GE, REC], F32, kind="Internal").ap()
    first_dram = nc.dram_tensor("group_firsts", [NGP * P], I32, kind="Internal").ap()
    base_dram = nc.dram_tensor("group_bases", [NGP * P], F32, kind="Internal").ap()
    rec_dram = nc.dram_tensor("edge_records", [SLOTS, REC], F32, kind="Internal").ap()
    tab_dram = nc.dram_tensor("node_table", [NB * P, TW], F32, kind="Internal").ap()
    bid_dram = nc.dram_tensor("group_blocks", [NGP * P], I32, kind="Internal").ap()
    e0_dram = nc.dram_tensor("edge_features", [P, SLOTS], F32, kind="Internal").ap()
    rec_groups = rec_dram.rearrange("(g p q) w -> g p (q w)", p=P, q=G)
    tab_blocks = tab_dram.rearrange("(b p) c -> p b c", p=P)

    ctx = ExitStack()
    with ctx:
        def sb(name, shape, dt=F32):
            return ctx.enter_context(nc.sbuf_tensor(name, shape, dt))

        def sem(name):
            return ctx.enter_context(nc.semaphore(name))

        ident = sb("ident", [P, P])
        mask_ident = sb("mask_ident", [P, P], BF16)
        lane_row = sb("lane_row", [P, P])
        lane_row_b = sb("lane_row_b", [P, P], BF16)
        lane_col = sb("lane_col", [P, 1])
        before = sb("before", [P, P])
        ones = sb("ones", [P, P])
        group_no = sb("group_no", [P, NGP])
        slopes = sb("slopes", [P, 2])
        eps_col = sb("eps_col", [P, 1])
        real_rows = sb("real_rows", [P, NB])
        w_ext = sb("w_ext", [P, L, TW])
        mix = sb("mix", [P, L - 2, P])
        bias_all = sb("bias_all", [P, L, P])
        mix_cur = sb("mix_cur", [P, P])
        bias_cur = sb("bias_cur", [P, P])
        uv_w = sb("uv_w", [P, 2 * P])
        fc_in = sb("fc_in", [P, P])
        fc_t = sb("fc_t", [P, P])
        fc_scaled_t = sb("fc_scaled_t", [P, P])
        own_columns = sb("own_columns", [P, TC, L])
        term_w = sb("term_w", [P, TC, L])
        bn_par = sb("bn_par", [P, 4])
        acc = sb("acc", [P, NB, P + 1])
        hx = sb("hx", [P, NB, TW])
        x0 = sb("x0", [P, NB, P])
        ub = sb("ub", [P, NB, P])
        blk = sb("blk", [P, NB, 3])
        sums = sb("sums", [P, NB, HW])
        loop_term = sb("loop_term", [P, L, NB])
        inv_deg = sb("inv_deg", [P, NB])
        small = sb("small", [P, 8, NB])
        ln_stat = sb("ln_stat", [P, NB, 6])
        ln_mv = sb("ln_mv", [P, NB, 2])
        bid = sb("bid", [1, NGP * P], I32)
        first = sb("first", [1, NGP * P], I32)
        flag = sb("flag", [1, 1], I32)
        group_tables = sb("group_tables", [P, 5, NGP])
        recs = sb("recs", [P, RING, G * REC])
        rows = sb("rows", [P, RING, G * TW])
        other_lane = sb("other_lane", [P, 2, G * P], BF16)
        u_edge = sb("u_edge", [P, 2, G])
        exp_pair = sb("exp_pair", [P, 2, 2, GE])
        att_t = sb("att_t", [P, 2, GE])
        att = sb("att", [P, 2, GE])
        cur = sb("cur", [P, 2, 3])
        gmax = sb("gmax", [P, 2, 4])
        shift = sb("shift", [P, 2, 3])
        rescale = sb("rescale", [P, RING, 1])
        bn_st = sb("bn_st", [P, NG, 6])
        bn_mv = sb("bn_mv", [P, 2])
        aff = sb("aff", [P, 12])
        ring_a = sb("ring_a", [P, 4, GE])
        ring_b = sb("ring_b", [P, 2, GE])
        node_ring = sb("node_ring", [P, 5, 2, P])
        hot = sb("hot", [P, 2, GE])
        slot_ring = sb("slot_ring", [EP, 2, CH], U32)

        bank = [ctx.enter_context(nc.psum_tensor(f"bank{i}", [P, 512], F32)) for i in range(8)]

        x0_flat = x0[:, :, :].rearrange("p b c -> p (b c)")
        acc_flat = acc[:, :, :].rearrange("p b c -> p (b c)")
        ub_flat = ub[:, :, :].rearrange("p b c -> p (b c)")
        assert 3 * ET <= NB * P and 4 * CH * REC <= 2 * GE and 4 * BATCH * G * REC <= 2 * GE and NGP * P <= GE
        slot_f = x0_flat[0:EP, 0:ET]
        dst_f = x0_flat[0:EP, ET:2 * ET]
        src_i = x0_flat[0:EP, 2 * ET:3 * ET].bitcast(I32)
        hi_f = acc_flat[0:EP, 0:ET]
        hit_i = acc_flat[0:EP, ET:2 * ET].bitcast(I32)
        run_f = acc_flat[0:EP, 2 * ET:3 * ET]
        dst_i = ub_flat[0:EP, 0:ET].bitcast(I32)
        tmp_i = ub_flat[0:EP, ET:2 * ET].bitcast(I32)
        lane_f = ub_flat[0:EP, ET:2 * ET]
        hit_f = ub_flat[0:EP, 2 * ET:3 * ET]
        attr_ring, attr_t = ring_a, ring_b
        rec_ring = exp_pair[0:EP, 0, :, :].rearrange("p a e -> p (a e)").rearrange("p (r t w) -> p r t w", r=4, w=REC)
        move_ring = exp_pair[:, 1, :, :].rearrange("p a e -> p (a e)").rearrange("p (r e) -> p r e", r=4)
        group_base = att[:, 0, :]

        loaded = sem("loaded")
        constants_made = sem("constants_made")
        dve_chain = sem("dve_chain")
        pool_chain = sem("pool_chain")
        transposed = sem("transposed")
        copied = sem("copied")
        projected = sem("projected")
        count_chain = sem("count_chain")
        slot_chain = sem("slot_chain")
        counted = sem("counted")
        offsets_made = sem("offsets_made")
        summed = sem("summed")
        tables_stored = sem("tables_stored")
        tables_loaded = sem("tables_loaded")
        order_seen = sem("order_seen")
        order_chain = sem("order_chain")
        order_summed = sem("order_summed")
        attr_landed = [sem(f"attr_landed{i}") for i in range(4)]
        attr_turned = sem("attr_turned")
        attr_copied = sem("attr_copied")
        terms_made = sem("terms_made")
        terms_copied = sem("terms_copied")
        ends_copied = sem("ends_copied")
        listed = [sem(f"listed{i}") for i in range(4)]
        tail_made = sem("tail_made")
        tail_stored = sem("tail_stored")
        move_landed = [sem(f"move_landed{i}") for i in range(4)]
        moved = [sem(f"moved{i}") for i in range(4)]
        move_chain = sem("move_chain")
        pads_made = sem("pads_made")
        pads_stored = sem("pads_stored")
        chunk_landed = [sem(f"chunk_landed{i}") for i in range(2)]
        scattered = [sem(f"scattered{i}") for i in range(2)]
        chunk_made = sem("chunk_made")
        lanes_hot = sem("lanes_hot")
        sums_made = sem("sums_made")
        sums_cleared = sem("sums_cleared")
        sums_added = sem("sums_added")
        x_landed = sem("x_landed")
        ln_act = sem("ln_act")
        ln_counted = sem("ln_counted")
        ln_chain = sem("ln_chain")
        src_made = sem("src_made")
        src_transposed = sem("src_transposed")
        src_copied = sem("src_copied")
        src_chain = sem("src_chain")
        mixed = sem("mixed")
        mix_copied = sem("mix_copied")
        mix_bent = sem("mix_bent")
        rows_made = sem("rows_made")
        rows_copied = sem("rows_copied")
        table_ready = sem("table_ready")
        table_stored = sem("table_stored")
        table_chain = sem("table_chain")
        rec_landed = [sem(f"rec_landed{i}") for i in range(RING)]
        rows_landed = [sem(f"rows_landed{i}") for i in range(RING)]
        slot_free = sem("slot_free")
        u_made = sem("u_made")
        logits_made = sem("logits_made")
        max_chain = sem("max_chain")
        shift_made = sem("shift_made")
        exps_made = sem("exps_made")
        att_t_made = sem("att_t_made")
        att_turned = sem("att_turned")
        att_made = sem("att_made")
        acc_added = sem("acc_added")
        mrg_chain = sem("mrg_chain")
        mrg_sub = sem("mrg_sub")
        degree_chain = sem("degree_chain")
        mrg_exp = sem("mrg_exp")
        fin_chain = sem("fin_chain")
        lanes_spread = sem("lanes_spread")
        hot_made = sem("hot_made")
        feat_made = sem("feat_made")
        feat_counted = sem("feat_counted")
        feat_copied = sem("feat_copied")
        feat_stored = [sem(f"feat_stored{i}") for i in range(2)]
        bn_chain = sem("bn_chain")
        bn_chain1 = sem("bn_chain1")
        bn_ready = sem("bn_ready")
        bn_pad = sem("bn_pad")
        fc_scaled = sem("fc_scaled")
        keep_chain = sem("keep_chain")
        waited = {e: sem(f"waited_{e}") for e in ("dve", "pool", "sp")}
        bn_act = sem("bn_act")
        bn_pe = sem("bn_pe")
        feat_landed = [sem(f"feat_landed{i}") for i in range(4)]
        relu_made = sem("relu_made")
        fc_made = sem("fc_made")
        fc_counted = sem("fc_counted")
        c_landed = [sem(f"c_landed{i}") for i in range(4)]
        c_relu = sem("c_relu")
        c_hot = sem("c_hot")
        c_fc = sem("c_fc")
        c_biased = sem("c_biased")
        c_msg = sem("c_msg")
        c_summed = sem("c_summed")
        c_added = sem("c_added")
        out_made = sem("out_made")
        out_stored = sem("out_stored")

        def stand_alone(eng, name):
            eng.sem_inc(waited[name], 1)

        wst = hx[:, 0:L, 0:P]
        w_t = hx[:, L:2 * L, 0:P]
        midst = hx[:, 2 * L:2 * L + 3, 0:P]
        thst, phst = hx[:, 13, 0:P], hx[:, 14, 0:P]
        west, aest = hx[:, 19:19 + L, 0:P], hx[:, 19 + L:19 + 2 * L, 0:P]
        a_rows = [hx[0:L, 17, 0:P], hx[0:L, 18, 0:P]]
        a_cols = small[:, 0:2, 0:L]
        term_cols = small[:, 2, 0:L]
        loads = [
            (dst_i, dst.rearrange("(p t) -> p t", p=EP)),
            (src_i, src.rearrange("(p t) -> p t", p=EP)),
            (wst, Ws.rearrange("l k j -> k l j")),
            (midst, mid_ws.rearrange("l k j -> k l j")),
            (thst, theta_w), (phst, phi_w), (fc_in[:, :], fc1_w),
            (a_rows[0], a_dsts), (a_rows[1], a_srcs),
        ]
        for l in range(L):
            loads.append((aest[:, l, :], a_edges[l:l + 1, :].broadcast_to([P, P])))
            loads.append((bias_all[:, l, :], biases[l:l + 1, :].broadcast_to([P, P])))
        for t in range(TC):
            loads.append((west[t * ED:(t + 1) * ED, :, :], Wes.rearrange("l k j -> k l j")))
        for i, v in enumerate((bn0_g, bn0_b, bn1_g, bn1_b)):
            loads.append((bn_par[:, i:i + 1], v.rearrange("(p a) -> p a", a=1)))

        with nc.Block() as block:
            @block.sync
            def _(sp):
                for to, of in loads:
                    sp.dma_start(to, of).then_inc(loaded, 16)

            @block.gpsimd
            def _(pool):
                c = Chain(pool, pool_chain)
                c.link(nc.gpsimd.memset(ident[:, :], 0.0))
                c.link(nc.gpsimd.affine_select(out=ident[:, :], in_=ident[:, :], compare_op=ALU.not_equal,
                                               fill=1.0, base=0, pattern=[[-1, P]], channel_multiplier=1))
                for to, pattern, lane_step in ((lane_row[:, :], [[1, P]], 0), (lane_row_b[:, :], [[1, P]], 0),
                                               (lane_col[:, :], [[0, 1]], 1),
                                               (group_no[:, :], [[1, NGP]], NGP)):
                    nc.gpsimd.iota(to, pattern=pattern, base=0, channel_multiplier=lane_step,
                                   allow_small_or_imprecise_dtypes=True)
                c.link(nc.gpsimd.memset(ones[:, :], 1.0))
                nc.gpsimd.affine_select(out=before[:, :], in_=ones[:, :], compare_op=ALU.is_gt,
                                        fill=0.0, base=0, pattern=[[1, P]], channel_multiplier=-1)
                nc.gpsimd.affine_select(out=real_rows[:, :], in_=ones[:, 0:NB], compare_op=ALU.is_gt,
                                        fill=0.0, base=N, pattern=[[-P, NB]], channel_multiplier=-1)
                c.link(nc.gpsimd.memset(own_columns[:, :, :], 1.0))
                c.link(nc.gpsimd.affine_select(out=own_columns[:, :, :], in_=own_columns[:, :, :],
                                               compare_op=ALU.is_ge, fill=0.0, base=0, pattern=[[-ED, TC], [0, L]],
                                               channel_multiplier=1))
                nc.gpsimd.affine_select(out=own_columns[:, :, :], in_=own_columns[:, :, :], compare_op=ALU.is_gt,
                                        fill=0.0, base=ED, pattern=[[ED, TC], [0, L]], channel_multiplier=-1)
                nc.gpsimd.memset(slopes[:, 0:1], 1.0)
                nc.gpsimd.memset(slopes[:, 1:2], ATT_SLOPE)
                nc.gpsimd.memset(eps_col[:, :], EPS)
                nc.gpsimd.memset(rec_ring[:, :, :, R_TERM + L:REC], 1.0)
                c.link(nc.gpsimd.memset(recs[:, 0, :], 1.0))
                tail = recs[:, 0, :].rearrange("p (q w) -> p q w", w=REC)
                nc.gpsimd.memset(tail[:, :, R_SRC].bitcast(I32), N)
                nc.gpsimd.memset(tail[:, :, R_LANE], float(2 * NB * P))
                nc.gpsimd.memset(small[:, :, :], 0.0).then_inc(constants_made, 1)

            @block.vector
            def _(dve):
                c = Chain(dve, dve_chain)
                dve.wait_ge(constants_made, 1)
                dve.wait_ge(loaded, 16 * len(loads))
                nc.vector.tensor_scalar(out=mask_ident[:, :], in0=ident[:, :], scalar1=-BIG, scalar2=None,
                                        op0=ALU.mult)
                for i, beta in enumerate(betas):
                    c.link(nc.vector.tensor_scalar(out=mix[:, i, :], in0=ident[:, :], scalar1=1.0 - beta,
                                                   scalar2=None, op0=ALU.mult))
                    nc.vector.scalar_tensor_tensor(out=mix[:, i, :], in0=midst[:, i, :], scalar=beta,
                                                   in1=mix[:, i, :], op0=ALU.mult, op1=ALU.add)
                nc.vector.tensor_copy(w_ext[:, :, 0:P], wst)
                nc.vector.tensor_sub(phst, phst, thst)
                c.link(nc.vector.tensor_mul(west, west, aest))
                c.link(nc.vector.reduce_sum(term_cols, west, AX.X))
                nc.vector.tensor_tensor(
                    out=term_w[:, :, :], in0=own_columns[:, :, :],
                    in1=term_cols.rearrange("p (a l) -> p a l", a=1).broadcast_to([P, TC, L]), op=ALU.mult)
                nc.vector.tensor_copy(dst_f, dst_i)
                c.link(nc.vector.tensor_single_scalar(tmp_i, dst_i, LANE_BITS, op=ALU.arith_shift_right))
                c.link(nc.vector.tensor_copy(hi_f, tmp_i))
                c.link(nc.vector.tensor_single_scalar(tmp_i, dst_i, P - 1, op=ALU.bitwise_and))
                nc.vector.tensor_copy(lane_f, tmp_i)

        with nc.Block() as block:
            @block.tensor
            def _(pe):
                for l in range(L):
                    nc.tensor.transpose(bank[l // 4][:, (l % 4) * P:(l % 4 + 1) * P], wst[:, l, :], ident[:, :])
                nc.tensor.transpose(bank[2][:, 0:P], thst, ident[:, :])
                nc.tensor.transpose(bank[2][:, P:2 * P], phst, ident[:, :])
                nc.tensor.transpose(bank[2][:, 2 * P:3 * P], fc_in[:, :], ident[:, :])
                for i in range(2):
                    last = nc.tensor.transpose(bank[3][:, i * L:(i + 1) * L], a_rows[i], ident[0:L, 0:L])
                last.then_inc(transposed, 1)
                pe.wait_ge(copied, 1)
                for l in range(L):
                    last = nc.tensor.matmul(bank[5][:, 2 * l:2 * l + 2], w_t[:, l, :], a_cols[:, :, l],
                                            start=True, stop=True)
                last.then_inc(projected, 1)

            @block.vector
            def _(dve):
                dve.wait_ge(transposed, 1)
                for l in range(L):
                    nc.vector.tensor_copy(w_t[:, l, :], bank[l // 4][:, (l % 4) * P:(l % 4 + 1) * P])
                nc.vector.tensor_copy(uv_w[:, :], bank[2][:, 0:2 * P])
                nc.vector.tensor_copy(fc_t[:, :], bank[2][:, 2 * P:3 * P])
                nc.vector.tensor_copy(a_cols, bank[3][:, 0:2 * L].rearrange("p (s l) -> p s l", s=2))\
                    .then_inc(copied, 1)
                dve.wait_ge(projected, 1)
                nc.vector.tensor_copy(w_ext[:, :, P:P + 2],
                                      bank[5][:, 0:2 * L].rearrange("p (l s) -> p l s", s=2))

        cnt = small[0:EP, 3, :]
        total, groups, ends, base = (small[:, i, :] for i in (4, 5, 6, 7))
        filled = small[:, 1, :]
        out_of_order = small[0:EP, 2, 0:1]
        ones_nb = ones[:, 0:NB]
        whole_i = small[:, 0, :].bitcast(I32)
        bid_f, base_f, first_f = (group_tables[:, i, :] for i in range(3))
        bid_i, first_i = (group_tables[:, i, :].bitcast(I32) for i in (3, 4))
        below = ln_stat[:, :, 0]
        attr_cols = edge_attr_16.rearrange("(p t) k -> p t k", p=EP)
        listed_cols = listed_dram[0:E, :].rearrange("(p t) w -> p t w", p=EP)
        with nc.Block() as block:
            @block.sync
            def _(sp):
                sp.dma_start(listed_dram[E:E + GE, :].rearrange("(p q) w -> p (q w)", p=P), recs[:, 0, :])\
                    .then_inc(tail_stored, 16)

                def load(i, k, turn):
                    if past(i, 4):
                        sp.wait_ge(attr_turned, i - 3)
                    sp.dma_start(attr_ring[0:EP, k, :].rearrange("p (t d) -> p t d", d=ED),
                                 attr_cols[:, span(i * CH, CH), :]).then_inc(attr_landed[k], 16)

                def store(i, k, turn):
                    sp.wait_ge(terms_copied, i + 1)
                    sp.wait_ge(ends_copied, i + 1)
                    sp.dma_start(listed_cols[:, span(i * CH, CH), :], rec_ring[:, k, :, :]).then_inc(listed[k], 16)
                software_pipeline(sp, NCH, 4, [(2, load), (-1, store)])
                sp.wait_ge(summed, 1)
                for to, of in ((bid_dram, bid_i), (first_dram, first_i), (base_dram, base_f)):
                    sp.dma_start(to.rearrange("(p j) -> p j", j=NGP), of).then_inc(tables_stored, 16)
                sp.wait_ge(tables_stored, 48)
                sp.dma_start(bid[:, :], bid_dram.rearrange("(a g) -> a g", a=1)).then_inc(tables_loaded, 16)
                sp.dma_start(first[:, :], first_dram.rearrange("(a g) -> a g", a=1)).then_inc(tables_loaded, 16)
                sp.dma_start(group_base[:, 0:NGP * P],
                             base_dram.rearrange("(a g) -> a g", a=1).broadcast_to([P, NGP * P]))\
                    .then_inc(tables_loaded, 16)
                sp.wait_ge(tables_loaded, 48)
                sp.wait_ge(tail_stored, 16)
                for k in range(4):
                    sp.wait_ge(listed[k], 16 * len(range(k, NCH, 4)))

            @block.tensor
            def _(pe):
                def turn_attributes(i, k, turn):
                    r = k % 2
                    pe.wait_ge(attr_landed[k], 16 * (turn + 1))
                    if past(i, 2):
                        pe.wait_ge(attr_copied, i - 1)
                    for j in range(CH // TC):
                        last = nc.tensor.transpose(bank[r][:, j * EP:(j + 1) * EP],
                                                   attr_ring[0:EP, k, j * P:(j + 1) * P], ident[0:EP, 0:EP])
                    last.then_inc(attr_turned, 1)

                def make_terms(i, k, turn):
                    r = k % 2
                    pe.wait_ge(attr_copied, i + 1)
                    if past(i, 2):
                        pe.wait_ge(terms_copied, i - 1)
                    for j in range(CH // TC):
                        last = nc.tensor.matmul(bank[2 + r][0:EP, j * TC * L:(j + 1) * TC * L],
                                                attr_t[:, r, j * EP:(j + 1) * EP],
                                                term_w[:, :, :].rearrange("p t l -> p (t l)"), start=True, stop=True)
                    last.then_inc(terms_made, 1)
                software_pipeline(pe, NCH, 4, [(0, turn_attributes), (-1, make_terms)])
                pe.wait_ge(count_chain, NB)
                nc.tensor.matmul(bank[6][:, 0:NB], before[0:EP, :], cnt, start=True, stop=True)
                nc.tensor.matmul(bank[6][:, 64:64 + NB], ones[0:EP, :], cnt, start=True, stop=True)
                nc.tensor.matmul(bank[6][0:EP - 1, 128:129], ident[0:EP, 1:EP], hi_f[:, 0:1], start=True, stop=True)\
                    .then_inc(counted, 1)
                pe.wait_ge(order_seen, 1)
                nc.tensor.matmul(bank[6][0:1, 130:131], out_of_order, ones[0:EP, 0:1], start=True, stop=True)\
                    .then_inc(order_summed, 1)

            @block.scalar
            def _(act):
                def copy_turned(i, k, turn):
                    act.wait_ge(attr_turned, i + 1)
                    if past(i, 2):
                        act.wait_ge(terms_made, i - 1)
                    nc.scalar.activation(attr_t[:, k % 2, 0:EP * (CH // TC)], bank[k % 2][:, 0:EP * (CH // TC)], ACT.Copy)\
                        .then_inc(attr_copied, 1)

                def copy_terms(i, k, turn):
                    act.wait_ge(terms_made, i + 1)
                    if past(i, 4):
                        act.wait_ge(listed[k], 16 * turn)
                    nc.scalar.activation(rec_ring[:, k, :, R_TERM:R_TERM + L],
                                         bank[2 + k % 2][0:EP, 0:CH * L].rearrange("p (t l) -> p t l", l=L), ACT.Copy)\
                        .then_inc(terms_copied, 1)
                software_pipeline(act, NCH, 4, [(0, copy_turned), (-1, copy_terms)])

            @block.gpsimd
            def _(pool):
                def copy_ends(i, k, turn):
                    if past(i, 4):
                        pool.wait_ge(listed[k], 16 * turn)
                        stand_alone(pool, "pool")
                    nc.gpsimd.tensor_copy(rec_ring[:, k, :, R_SRC].bitcast(I32), src_i[:, span(i * CH, CH)])
                    nc.gpsimd.tensor_copy(rec_ring[:, k, :, R_LANE], dst_f[:, span(i * CH, CH)]).then_inc(ends_copied, 1)
                software_pipeline(pool, NCH, 4, [(0, copy_ends)])

            @block.vector
            def _(dve):
                with dve.Fori(0, NB) as b:
                    Chain(dve, count_chain, b).link(
                        nc.vector.tensor_scalar(out=hit_f, in0=hi_f, scalar1=lane_row[0:EP, at(b)], scalar2=None,
                                                op0=ALU.is_equal, op1=ALU.add, accum_out=cnt[:, at(b)]))
                    stand_alone(dve, "dve")
                c = Chain(dve, order_chain)
                c.link(nc.vector.tensor_tensor(out=hit_f[:, 0:ET - 1], in0=hi_f[:, 0:ET - 1], in1=hi_f[:, 1:ET],
                                               op=ALU.is_gt))
                c.link(nc.vector.reduce_sum(out_of_order, hit_f[:, 0:ET - 1], AX.X))
                dve.wait_ge(counted, 1)
                c.link(nc.vector.tensor_tensor(out=hit_f[0:EP - 1, 0:1], in0=hi_f[0:EP - 1, ET - 1:ET],
                                               in1=bank[6][0:EP - 1, 128:129], op=ALU.is_gt))
                c.link(nc.vector.tensor_add(out_of_order[0:EP - 1, :], out_of_order[0:EP - 1, :],
                                            hit_f[0:EP - 1, 0:1]))
                c = Chain(dve, offsets_made)
                c.link(nc.vector.tensor_scalar_add(total, bank[6][:, 64:64 + NB], float(GE - 1)))
                c.link(nc.vector.tensor_copy(whole_i, total))
                c.link(nc.vector.tensor_single_scalar(whole_i, whole_i, GE.bit_length() - 1,
                                                      op=ALU.arith_shift_right))
                c.link(nc.vector.tensor_copy(groups, whole_i))
                c.link(nc.vector.tensor_tensor_scan(ends, ones_nb, groups, 0.0, ALU.mult, ALU.add))
                c.link(nc.vector.tensor_sub(base, ends, groups))
                c.link(nc.vector.tensor_scalar(out=base, in0=base, scalar1=float(GE), scalar2=-1.0,
                                               op0=ALU.mult, op1=ALU.add))
                c.link(nc.vector.tensor_add(base, base, bank[6][:, 0:NB]))
                c.link(nc.vector.scalar_tensor_tensor(out=filled, in0=groups, scalar=float(GE), in1=total,
                                                      op0=ALU.mult, op1=ALU.subtract))
                c.link(nc.vector.tensor_scalar_add(filled, filled, float(GE - 1)))
                nc.vector.memset(bid_f, 0.0).then_inc(order_seen, 1)
                dve.wait_ge(order_seen, 1)
                for j in range(NGP):
                    c.link(nc.vector.tensor_scalar(out=below, in0=ends, scalar1=group_no[:, j:j + 1], scalar2=None,
                                                   op0=ALU.is_le, op1=ALU.add, accum_out=bid_f[:, j:j + 1]))
                    c.link(nc.vector.tensor_mul(below, below, filled))
                    c.link(nc.vector.reduce_sum(first_f[:, j:j + 1], below, AX.X))
                c.link(nc.vector.scalar_tensor_tensor(out=first_f, in0=group_no[:, :], scalar=float(GE), in1=first_f,
                                                      op0=ALU.mult, op1=ALU.subtract))
                c.link(nc.vector.tensor_scalar(out=first_f, in0=first_f, scalar1=float(E), scalar2=0.0,
                                               op0=ALU.min, op1=ALU.max))
                c.link(nc.vector.tensor_scalar_min(bid_f, bid_f, float(NB - 1)))
                nc.vector.tensor_scalar(out=base_f, in0=bid_f, scalar1=float(P), scalar2=None, op0=ALU.mult)
                nc.vector.tensor_copy(first_i, first_f)
                nc.vector.tensor_copy(bid_i, bid_f).then_inc(summed, 1)
                dve.wait_ge(order_summed, 1)
                nc.vector.tensor_scalar_min(flag[:, 0:1], bank[6][0:1, 130:131], 1.0)

        move_groups = rec_dram.rearrange("(a g p q) w -> a p g (q w)", g=BATCH, p=P, q=G)
        NBATCH = NG // BATCH
        MOVE_LINKS = 4
        pad = hx[:, :, :].rearrange("p b c -> p (b c)")
        PARTS = -(-(SLOTS // P * REC) // (NB * TW))
        while SLOTS // P % PARTS:
            PARTS += 1
        PR = SLOTS // P // PARTS
        pad_recs = pad[:, 0:PR * REC].rearrange("p (r w) -> p r w", w=REC)

        def load_in_order(sp):
            def load(i, k, turn):
                if past(i, 4):
                    sp.wait_ge(moved[k], 16 * turn)
                for j in range(BATCH):
                    start = sp.value_load(first[0:1, at(i * BATCH + j)], min_val=0, max_val=E)
                    sp.dma_start(move_ring[:, k, j * G * REC:(j + 1) * G * REC],
                                 listed_dram[bass.ds(start, GE), :].rearrange("(p q) w -> p (q w)", p=P))\
                        .then_inc(move_landed[k], 16)
            software_pipeline(sp, NBATCH, 4, [(0, load)])

        def place_in_order(dve):
            source_f, kept = (att_t[:, i, 0:BATCH * G].rearrange("p (g q) -> p g q", q=G) for i in range(2))

            def place(i, k, turn):
                c = Chain(dve, move_chain, i * MOVE_LINKS)
                words = move_ring[:, k, :].rearrange("p (g q w) -> p g q w", g=BATCH, w=REC)
                lanes, sources = words[:, :, :, R_LANE], words[:, :, :, R_SRC].bitcast(I32)
                dve.wait_ge(move_landed[k], 16 * BATCH * (turn + 1))
                stand_alone(dve, "dve")
                nc.vector.tensor_copy(source_f, sources)
                c.link(nc.vector.tensor_tensor(
                    out=lanes, in0=lanes,
                    in1=group_base[:, span(i * BATCH, BATCH)].rearrange("p (g a) -> p g a", a=1)
                    .broadcast_to([P, BATCH, G]), op=ALU.subtract))
                c.link(nc.vector.tensor_scalar_add(source_f, source_f, -float(N)))
                c.link(nc.vector.scalar_tensor_tensor(out=kept, in0=lanes, scalar=float(P), in1=source_f,
                                                      op0=ALU.is_lt, op1=ALU.mult))
                c.link(nc.vector.tensor_scalar_add(sources, kept, float(N)))
            software_pipeline(dve, NBATCH, 4, [(0, place)])

        def store_in_order(act):
            def store(i, k, turn):
                act.wait_ge(move_chain, (i + 1) * MOVE_LINKS)
                act.dma_start(move_groups[at(i)].rearrange("a p g w -> p (a g) w"),
                              move_ring[:, k, :].rearrange("p (g w) -> p g w", g=BATCH)).then_inc(moved[k], 16)
            software_pipeline(act, NBATCH, 4, [(0, store)])
            for k in range(4):
                act.wait_ge(moved[k], 16 * len(range(k, NBATCH, 4)))

        def load_for_scatter(sp):
            sp.wait_ge(pads_made, 2)
            lanes = rec_dram.rearrange("(p a r) w -> a p (r w)", p=P, a=PARTS)
            for a in range(PARTS):
                sp.dma_start(lanes[a], pad[:, 0:PR * REC]).then_inc(pads_stored, 16)

            def load(i, k, turn):
                if past(i, 2):
                    sp.wait_ge(scattered[k], 16 * CH * turn)
                sp.dma_start(rec_ring[:, k, :, :], listed_cols[:, span(i * CH, CH), :]).then_inc(chunk_landed[k], 16)
            software_pipeline(sp, NCH, 2, [(0, load)])

        def place_for_scatter(dve):
            with dve.Fori(0, NB) as b:
                c = Chain(dve, slot_chain, b * 3)
                c.link(nc.vector.tensor_scalar(out=hit_i, in0=hi_f, scalar1=lane_row[0:EP, at(b)], scalar2=None,
                                               op0=ALU.is_equal))
                c.link(nc.vector.tensor_tensor_scan(run_f, hit_i, hit_i, base[0:EP, at(b)], ALU.add, ALU.bypass))
                stand_alone(dve, "dve")
                c.link(nc.vector.copy_predicated(slot_f, hit_i, run_f))
                stand_alone(dve, "dve")

            def place(i, k, turn):
                dve.wait_ge(chunk_landed[k], 16 * (turn + 1))
                if past(i, 2):
                    dve.wait_ge(scattered[k], 16 * CH * turn)
                stand_alone(dve, "dve")
                nc.vector.tensor_copy(rec_ring[:, k, :, R_LANE], lane_f[:, span(i * CH, CH)])
                nc.vector.tensor_copy(slot_ring[:, k, :], slot_f[:, span(i * CH, CH)]).then_inc(chunk_made, 1)
            software_pipeline(dve, NCH, 2, [(0, place)])

        def scatter_all(pool):
            c = Chain(pool, pads_made)
            c.link(nc.gpsimd.memset(pad_recs, 0.0))
            nc.gpsimd.memset(pad_recs[:, :, R_SRC].bitcast(I32), N)
            c.link(nc.gpsimd.memset(pad_recs[:, :, R_LANE], NO_LANE))
            pool.wait_ge(pads_stored, 16 * PARTS)

            def scatter(i, k, turn):
                pool.wait_ge(chunk_made, i + 1)
                stand_alone(pool, "pool")
                for t in range(CH):
                    nc.gpsimd.indirect_dma_start(
                        rec_dram, bass.IndirectOffsetOnAxis(ap=slot_ring[:, k, t:t + 1], axis=0),
                        rec_ring[:, k, t, :], None).then_inc(scattered[k], 16)
            software_pipeline(pool, NCH, 2, [(0, scatter)])
            for k in range(2):
                pool.wait_ge(scattered[k], 16 * CH * len(range(k, NCH, 2)))

        with nc.Block() as block:
            @block.sync
            def _(sp):
                unordered = sp.value_load(flag[0:1, 0:1], min_val=0, max_val=1)
                with sp.If(unordered == 0):
                    load_in_order(sp)
                with sp.Else():
                    load_for_scatter(sp)

            @block.vector
            def _(dve):
                unordered = dve.value_load(flag[0:1, 0:1], min_val=0, max_val=1)
                with dve.If(unordered == 0):
                    place_in_order(dve)
                with dve.Else():
                    place_for_scatter(dve)

            @block.scalar
            def _(act):
                unordered = act.value_load(flag[0:1, 0:1], min_val=0, max_val=1)
                with act.If(unordered == 0):
                    store_in_order(act)

            @block.gpsimd
            def _(pool):
                unordered = pool.value_load(flag[0:1, 0:1], min_val=0, max_val=1)
                with pool.If(unordered == 1):
                    scatter_all(pool)

        hp, hp_t, mx, hm_t, part = (node_ring[:, i, :, :] for i in range(5))

        def prepare_rows(block, call, source, mixed_call, weights, evacuate):
            width = weights.shape[1]
            n0 = call * NB
            m0 = 0 if mixed_call is None else mixed_call * NB

            @block.vector
            def _(dve):
                def make(i, k, turn):
                    if past(i, 2):
                        dve.wait_ge(src_transposed, n0 + i - 1)
                    source(dve, i, k).then_inc(src_made, 1)

                def bend(i, k, turn):
                    dve.wait_ge(mix_copied, m0 + i + 1)
                    if past(i, 2):
                        dve.wait_ge(rows_made, n0 + i - 1)
                    nc.vector.scalar_tensor_tensor(out=hm_t[:, k, :], in0=mx[:, k, :], scalar=OUT_SLOPE,
                                                   in1=mx[:, k, :], op0=ALU.mult, op1=ALU.max).then_inc(mix_bent, 1)
                software_pipeline(dve, NB, 2, [(0, make)] + ([] if mixed_call is None else [(-1, bend)]))

            @block.tensor
            def _(pe):
                def turn_rows(i, k, turn):
                    pe.wait_ge(src_made, n0 + i + 1)
                    if past(i, 2):
                        pe.wait_ge(src_copied, n0 + i - 1)
                    nc.tensor.transpose(bank[k][:, 0:P], hp[:, k, :], ident[:, :]).then_inc(src_transposed, 1)

                def mix_rows(i, k, turn):
                    pe.wait_ge(src_copied, n0 + i + 1)
                    if past(i, 2):
                        pe.wait_ge(mix_copied, m0 + i - 1)
                    nc.tensor.matmul(bank[2 + k][:, 0:P], mix_cur[:, :], hp_t[:, k, :], start=True, stop=True)\
                        .then_inc(mixed, 1)

                def project(i, k, turn):
                    if mixed_call is None:
                        pe.wait_ge(src_copied, n0 + i + 1)
                    else:
                        pe.wait_ge(mix_bent, m0 + i + 1)
                    if past(i, 2):
                        pe.wait_ge(rows_copied, n0 + i - 1)
                    rows_t = hp_t if mixed_call is None else hm_t
                    nc.tensor.matmul(bank[4 + k][:, 0:width], rows_t[:, k, :], weights, start=True, stop=True)\
                        .then_inc(rows_made, 1)
                software_pipeline(pe, NB, 2, [(0, turn_rows)] + ([] if mixed_call is None else [(-1, mix_rows)])
                                  + [(-2, project)])

            @block.scalar
            def _(act):
                def copy_turned(i, k, turn):
                    act.wait_ge(src_transposed, n0 + i + 1)
                    if past(i, 2):
                        if mixed_call is None:
                            act.wait_ge(rows_made, n0 + i - 1)
                        else:
                            act.wait_ge(mixed, m0 + i - 1)
                    nc.scalar.activation(hp_t[:, k, :], bank[k][:, 0:P], ACT.Copy).then_inc(src_copied, 1)

                def copy_mixed(i, k, turn):
                    act.wait_ge(mixed, m0 + i + 1)
                    if past(i, 2):
                        act.wait_ge(mix_bent, m0 + i - 1)
                    nc.scalar.activation(mx[:, k, :], bank[2 + k][:, 0:P], ACT.Copy).then_inc(mix_copied, 1)

                def copy_rows(i, k, turn):
                    act.wait_ge(rows_made, n0 + i + 1)
                    evacuate(i, bank[4 + k][:, 0:width]).then_inc(rows_copied, 1)
                software_pipeline(act, NB, 2, [(0, copy_turned)]
                                  + ([] if mixed_call is None else [(-1, copy_mixed)]) + [(-2, copy_rows)])

        def normalise(block, call, rows_in):
            @block.vector
            def _(dve):
                with dve.Fori(0, NB) as b:
                    nc.vector.bn_stats(ln_stat[:, at(b), :].rearrange("p a c -> p (a c)"),
                                       rows_in[:, at(b), :].rearrange("p a c -> p (a c)")).then_inc(ln_counted, 1)
                dve.wait_ge(ln_counted, (call + 1) * NB)
                c = Chain(dve, ln_chain, call * 6)
                mean_e, mean_o, sq_e, sq_o = (ln_stat[:, :, i] for i in (1, 4, 2, 5))
                half_gap = ln_stat[:, :, 0]
                c.link(nc.vector.tensor_add(ln_mv[:, :, 0], mean_e, mean_o))
                c.link(nc.vector.tensor_sub(half_gap, mean_e, mean_o))
                c.link(nc.vector.tensor_scalar(out=ln_mv[:, :, 0], in0=ln_mv[:, :, 0], scalar1=0.5, scalar2=None,
                                               op0=ALU.mult))
                c.link(nc.vector.tensor_mul(half_gap, half_gap, half_gap))
                c.link(nc.vector.tensor_add(sq_e, sq_e, sq_o))
                c.link(nc.vector.scalar_tensor_tensor(out=sq_e, in0=half_gap, scalar=C / 4.0, in1=sq_e,
                                                      op0=ALU.mult, op1=ALU.add))
                dve.wait_ge(ln_act, call + 1)
                nc.vector.reciprocal(ln_mv[:, :, 1], ln_stat[:, :, 3])

            @block.scalar
            def _(act):
                act.wait_ge(ln_chain, (call + 1) * 6)
                nc.scalar.activation(ln_stat[:, :, 3], ln_stat[:, :, 2], ACT.Sqrt, bias=eps_col[:, :], scale=1.0 / C)\
                    .then_inc(ln_act, 1)

        def block_of(t, b, width=None):
            view = t[:, at(b), :] if width is None else t[:, at(b), 0:width]
            return view.rearrange("p a c -> p (a c)")

        with nc.Block() as block:
            @block.vector
            def _(dve):
                dve.memset(x0[:, NB - 1, :], 0.0).then_inc(x_landed, 1)

            @block.sync
            def _(sp):
                sp.wait_ge(x_landed, 1)
                sp.dma_start(x0[:, 0:NB - 1, :], x[0:(NB - 1) * P, :].rearrange("(b p) c -> p b c", p=P))\
                    .then_inc(loaded, 16)
                sp.dma_start(x0[0:TAIL, NB - 1, :], x[(NB - 1) * P:N, :]).then_inc(loaded, 16)
                sp.wait_ge(loaded, 16 * (len(loads) + 2))

        with nc.Block() as block:
            normalise(block, 0, x0)

        def norm_relu(t, to_rows=None):
            def source(dve, i, k):
                Chain(dve, src_chain, source.base + i).link(
                    nc.vector.tensor_scalar(out=part[:, k, :], in0=block_of(t, i), scalar1=ln_mv[:, at(i), 0],
                                            scalar2=ln_mv[:, at(i), 1], op0=ALU.subtract, op1=ALU.mult))
                return nc.vector.tensor_scalar_max(hp[:, k, :], part[:, k, :], 0.0)
            source.base = 0
            return source

        def to_hx(i, product):
            return nc.scalar.activation(block_of(hx, i), product, ACT.Copy)

        with nc.Block() as block:
            prepare_rows(block, 0, norm_relu(x0), None, w_ext[:, 0, :], to_hx)

        def store_table(call):
            with nc.Block() as block:
                @block.vector
                def _(dve):
                    c = Chain(dve, table_chain, call)
                    nc.vector.tensor_copy(blk[:, :, 0], hx[:, :, P])
                    c.link(nc.vector.tensor_scalar_mul(blk[:, :, 1], hx[:, :, P], ATT_SLOPE))
                    nc.vector.memset(hx[:, :, P], 1.0).then_inc(table_ready, 1)
                    nc.vector.memset(blk[:, :, 2], NO_MAX)

                @block.gpsimd
                def _(pool):
                    nc.gpsimd.memset(acc[:, :, :], 0.0)

                @block.sync
                def _(sp):
                    sp.wait_ge(table_ready, call + 1)
                    sp.dma_start(tab_blocks, hx[:, :, :]).then_inc(table_stored, 16)
                    sp.wait_ge(table_stored, 16 * (call + 1))
                    stand_alone(sp, "sp")

        def rec_word(k, q, word):
            return recs[:, k, q * REC + word:q * REC + word + 1]

        def row_words(k, q, lo, hi):
            return rows[:, k, q * TW + lo:q * TW + hi]

        def stream_rows(block, layer):
            g0 = layer * NG
            t0 = layer * (NG // RING)

            @block.sync
            def _(sp):
                def load(i, k, turn):
                    sp.wait_ge(slot_free, g0 + i + 1)
                    sp.dma_start(recs[:, k, :], rec_groups[at(i)].rearrange("a p w -> (a p) w"))\
                        .then_inc(rec_landed[k], 16)
                software_pipeline(sp, NG, RING, [(0, load)])

            @block.gpsimd
            def _(pool):
                def gather(i, k, turn):
                    pool.wait_ge(rec_landed[k], 16 * (t0 + turn + 1))
                    stand_alone(pool, "pool")
                    for q in range(G):
                        nc.gpsimd.indirect_dma_start(
                            row_words(k, q, 0, TW), None, tab_dram,
                            bass.IndirectOffsetOnAxis(ap=rec_word(k, q, R_SRC).bitcast(U32), axis=0))\
                            .then_inc(rows_landed[k], 16)
                software_pipeline(pool, NG, RING, [(0, gather)])

        MAX_LINKS = 4

        def attend(block, layer, with_sums=False):
            g0 = layer * NG
            t0 = layer * (NG // RING)
            term_word = R_TERM + layer
            stream_rows(block, layer)

            @block.vector
            def _(dve):
                def edge_side(i, k, turn):
                    r = k % 2
                    dve.wait_ge(rec_landed[k], 16 * (t0 + turn + 1))
                    if with_sums and past(i, 2):
                        dve.wait_ge(lanes_hot, i - 1)
                    for q in range(G):
                        nc.vector.tensor_scalar(out=other_lane[:, r, q * P:(q + 1) * P], in0=lane_row_b[:, :],
                                                scalar1=rec_word(k, q, R_LANE), scalar2=None,
                                                op0=ALU.not_equal)
                    dve.wait_ge(rows_landed[k], 16 * G * (t0 + turn + 1))
                    nc.vector.tensor_add(
                        u_edge[:, r, :], rows[:, k, :].rearrange("p (q w) -> p q w", w=TW)[:, :, P + 1],
                        recs[:, k, :].rearrange("p (q w) -> p q w", w=REC)[:, :, at(term_word)]
                        .rearrange("p q a -> p (q a)")).then_inc(u_made, 1)

                def maximum(i, k, turn):
                    r = k % 2
                    c = Chain(dve, max_chain, (g0 + i) * MAX_LINKS)
                    b = dve.value_load(bid[0:1, at(i)], min_val=0, max_val=NB - 1)
                    nc.vector.tensor_copy(cur[:, r, :], block_of(blk, b))
                    dve.wait_ge(logits_made, g0 + i + 1)
                    c.link(nc.vector.reduce_max(gmax[:, r, 0:1], bank[r][:, :], AX.X))
                    c.link(nc.vector.scalar_tensor_tensor(out=gmax[:, r, 1:3], in0=slopes[:, :],
                                                          scalar=gmax[:, r, 0:1], in1=cur[:, r, 0:2],
                                                          op0=ALU.mult, op1=ALU.add))
                    c.link(nc.vector.tensor_scalar(out=gmax[:, r, 3:4], in0=gmax[:, r, 1:2],
                                                   scalar1=gmax[:, r, 2:3], scalar2=cur[:, r, 2:3],
                                                   op0=ALU.max, op1=ALU.max))
                    nc.vector.tensor_scalar(out=shift[:, r, :], in0=cur[:, r, :], scalar1=gmax[:, r, 3:4],
                                            scalar2=None, op0=ALU.subtract).then_inc(shift_made, 1)
                    c.link(nc.vector.tensor_copy(blk[:, at(b), 2], gmax[:, r, 3:4]))

                def larger_exp(i, k, turn):
                    r = k % 2
                    dve.wait_ge(exps_made, g0 + i + 1)
                    if past(i, 2):
                        dve.wait_ge(att_turned, g0 + i - 1)
                    nc.vector.tensor_max(att_t[:, r, :], exp_pair[:, r, 0, :], exp_pair[:, r, 1, :])\
                        .then_inc(att_t_made, 1)

                def accumulate(i, k, turn):
                    b = dve.value_load(bid[0:1, at(i)], min_val=0, max_val=NB - 1)
                    dve.wait_ge(slot_free, RING + g0 + i + 1)
                    if past(i, 1):
                        dve.wait_ge(acc_added, g0 + i)
                    nc.vector.scalar_tensor_tensor(out=block_of(acc, b), in0=block_of(acc, b),
                                                   scalar=rescale[:, k, :], in1=bank[4 + k % 2][:, 0:P + 1],
                                                   op0=ALU.mult, op1=ALU.add).then_inc(acc_added, 1)

                def add_sums(i, k, turn):
                    b = dve.value_load(bid[0:1, at(i)], min_val=0, max_val=NB - 1)
                    dve.wait_ge(sums_made, i + 1)
                    if past(i, 1):
                        dve.wait_ge(sums_added, i)
                    nc.vector.tensor_add(block_of(sums, b), block_of(sums, b), bank[6 + k % 2][:, 0:HW])\
                        .then_inc(sums_added, 1)
                if with_sums:
                    nc.vector.memset(sums[:, :, :], 0.0).then_inc(sums_cleared, 1)
                    dve.wait_ge(sums_cleared, 1)
                software_pipeline(dve, NG, RING, [(0, maximum), (-1, larger_exp), (2, edge_side), (-4, accumulate)]
                                  + ([(-1, add_sums)] if with_sums else []))

            @block.tensor
            def _(pe):
                def logits(i, k, turn):
                    r = k % 2
                    pe.wait_ge(u_made, g0 + i + 1)
                    if past(i, 2):
                        pe.wait_ge(exps_made, g0 + i - 1)
                    for q in range(G):
                        nc.tensor.matmul(bank[r][:, q * P:(q + 1) * P], u_edge[:, r, q:q + 1].broadcast_to([P, P]),
                                         ident[:, :], start=True, stop=False)
                        last = nc.tensor.matmul(bank[r][:, q * P:(q + 1) * P], other_lane[:, r, q * P:(q + 1) * P],
                                                mask_ident[:, :], start=False, stop=True)
                    last.then_inc(logits_made, 1)

                def turn_att(i, k, turn):
                    r = k % 2
                    pe.wait_ge(att_t_made, g0 + i + 1)
                    if past(i, 2):
                        pe.wait_ge(att_made, g0 + i - 1)
                    for q in range(G):
                        last = nc.tensor.transpose(bank[2 + r][:, q * P:(q + 1) * P],
                                                   att_t[:, r, q * P:(q + 1) * P], ident[:, :])
                    last.then_inc(att_turned, 1)

                def weigh(i, k, turn):
                    r = k % 2
                    pe.wait_ge(att_made, g0 + i + 1)
                    pe.wait_ge(rows_landed[k], 16 * G * (t0 + turn + 1))
                    if past(i, 2):
                        pe.wait_ge(acc_added, g0 + i - 1)
                    for q in range(G):
                        last = nc.tensor.matmul(bank[4 + r][:, 0:P + 1], att[:, r, q * P:(q + 1) * P],
                                                row_words(k, q, 0, P + 1), start=(q == 0), stop=(q == G - 1))
                    last.then_inc(slot_free, 1)

                def sum_terms(i, k, turn):
                    pe.wait_ge(lanes_hot, i + 1)
                    if past(i, 2):
                        pe.wait_ge(sums_added, i - 1)
                    for q in range(G):
                        last = nc.tensor.matmul(bank[6 + k % 2][:, 0:HW], hot[:, k % 2, q * P:(q + 1) * P],
                                                recs[:, k, q * REC + R_TERM:(q + 1) * REC],
                                                start=(q == 0), stop=(q == G - 1))
                    last.then_inc(sums_made, 1)
                software_pipeline(pe, NG, RING, [(-3, weigh), (2, logits), (-1, turn_att)]
                                  + ([(0, sum_terms)] if with_sums else []))

            @block.scalar
            def _(act):
                def exps(i, k, turn):
                    r = k % 2
                    act.wait_ge(shift_made, g0 + i + 1)
                    if past(i, 2):
                        act.wait_ge(att_t_made, g0 + i - 1)
                    nc.scalar.activation(rescale[:, k, :], shift[:, r, 2:3], ACT.Exp)
                    nc.scalar.activation(exp_pair[:, r, 0, :], bank[r][:, :], ACT.Exp, bias=shift[:, r, 0:1])
                    nc.scalar.activation(exp_pair[:, r, 1, :], bank[r][:, :], ACT.Exp, bias=shift[:, r, 1:2],
                                         scale=ATT_SLOPE).then_inc(exps_made, 1)

                def copy_att(i, k, turn):
                    r = k % 2
                    act.wait_ge(att_turned, g0 + i + 1)
                    if past(i, 2):
                        act.wait_ge(slot_free, RING + g0 + i - 1)
                    nc.scalar.activation(att[:, r, :], bank[2 + r][:, :], ACT.Copy).then_inc(att_made, 1)

                def hot_lanes(i, k, turn):
                    act.wait_ge(u_made, g0 + i + 1)
                    if past(i, 2):
                        act.wait_ge(sums_made, i - 1)
                    nc.scalar.activation(hot[:, k % 2, :], other_lane[:, k % 2, :], ACT.Identity,
                                         bias=slopes[:, 0:1], scale=-1.0).then_inc(lanes_hot, 1)
                software_pipeline(act, NG, RING, [(0, exps), (-2, copy_att)]
                                  + ([(1, hot_lanes)] if with_sums else []))

        MERGE_LINKS = 9
        from_acc, from_self = small[:, 0, :], small[:, 1, :]

        def merge_self_loops(layer):
            logit, sloped, top, diff, weight, share = (small[:, i, :] for i in range(2, 8))
            inner = not isinstance(layer, int)
            share_of_conv = 1.0 - ALPHA if inner else 1.0
            with nc.Block() as block:
                @block.vector
                def _(dve):
                    c = Chain(dve, mrg_chain, layer * MERGE_LINKS)
                    if inner:
                        nc.vector.tensor_copy(mix_cur[:, :], block_of(mix, layer - 1))
                    nc.vector.tensor_scalar(out=bias_cur[:, :], in0=block_of(bias_all, layer), scalar1=share_of_conv,
                                            scalar2=None, op0=ALU.mult)
                    c.link(nc.vector.tensor_add(logit, hx[:, :, P + 1], blk[:, :, 0]))
                    c.link(nc.vector.tensor_add(logit, logit, loop_term[:, at(layer), :].rearrange("p a b -> p (a b)")))
                    c.link(nc.vector.scalar_tensor_tensor(out=sloped, in0=logit, scalar=ATT_SLOPE, in1=logit,
                                                          op0=ALU.mult, op1=ALU.max))
                    c.link(nc.vector.tensor_max(top, sloped, blk[:, :, 2]))
                    c.link(nc.vector.tensor_sub(diff, blk[:, :, 2], top))
                    nc.vector.tensor_sub(logit, sloped, top).then_inc(mrg_sub, 1)
                    dve.wait_ge(mrg_exp, layer + 1)
                    c.link(nc.vector.tensor_mul(weight, acc[:, :, P], from_acc))
                    c.link(nc.vector.tensor_add(weight, weight, from_self))
                    c.link(nc.vector.reciprocal(share, weight))
                    c.link(nc.vector.tensor_scalar(out=share, in0=share, scalar1=share_of_conv, scalar2=None,
                                                   op0=ALU.mult))
                    nc.vector.tensor_mul(from_acc, from_acc, share)
                    nc.vector.tensor_mul(from_self, from_self, share)

                @block.scalar
                def _(act):
                    act.wait_ge(mrg_sub, layer + 1)
                    nc.scalar.activation(from_acc, diff, ACT.Exp)
                    nc.scalar.activation(from_self, logit, ACT.Exp).then_inc(mrg_exp, 1)

        def layer_output(dve, chain, i, k):
            chain.link(nc.vector.scalar_tensor_tensor(out=part[:, k, :], in0=block_of(acc, i, P),
                                                      scalar=from_acc[:, at(i)], in1=bias_cur[:, :],
                                                      op0=ALU.mult, op1=ALU.add))
            chain.link(nc.vector.scalar_tensor_tensor(out=part[:, k, :], in0=block_of(hx, i, P),
                                                      scalar=from_self[:, at(i)], in1=part[:, k, :],
                                                      op0=ALU.mult, op1=ALU.add))

        with nc.Block() as block:
            @block.gpsimd
            def _(pool):
                pool.sem_inc(slot_free, RING)

        def conv_base(layer):
            return NB + (0 if isinstance(layer, int) and layer == 0 else 3 * NB + (layer - 1) * 2 * NB)

        store_table(0)
        with nc.Block() as block:
            attend(block, 0, with_sums=True)

        with nc.Block() as block:
            @block.vector
            def _(dve):
                c = Chain(dve, degree_chain)
                c.link(nc.vector.tensor_scalar_max(inv_deg[:, :], sums[:, :, L], 1.0))
                c.link(nc.vector.reciprocal(inv_deg[:, :], inv_deg[:, :]))
                for l in range(L):
                    nc.vector.tensor_mul(loop_term[:, l, :], sums[:, :, l], inv_deg[:, :])

        merge_self_loops(0)

        def keep_x0(dve, i, k):
            c = Chain(dve, src_chain, conv_base(0) + i * 3)
            layer_output(dve, c, i, k)
            c.link(nc.vector.tensor_copy(block_of(x0, i), part[:, k, :]))
            return nc.vector.tensor_copy(hp[:, k, :], part[:, k, :])
        with nc.Block() as block:
            prepare_rows(block, 1, keep_x0, None, w_ext[:, 1, :], to_hx)

        with nc.Fori(1, L - 1) as layer:
            store_table(layer)
            with nc.Block() as block:
                attend(block, layer)
            merge_self_loops(layer)

            def residual(dve, i, k):
                c = Chain(dve, src_chain, conv_base(layer) + i * 2)
                layer_output(dve, c, i, k)
                return nc.vector.scalar_tensor_tensor(out=hp[:, k, :], in0=block_of(x0, i), scalar=ALPHA,
                                                      in1=part[:, k, :], op0=ALU.mult, op1=ALU.add)
            with nc.Block() as block:
                prepare_rows(block, layer + 1, residual, layer - 1,
                             w_ext[:, bass.ds(layer + 1, 1), :].rearrange("p a c -> p (a c)"), to_hx)

        store_table(L - 1)
        with nc.Block() as block:
            attend(block, L - 1)

            @block.scalar
            def _(act):
                act.dma_start(x0[:, 0:NB - 1, :], x[0:(NB - 1) * P, :].rearrange("(b p) c -> p b c", p=P))\
                    .then_inc(loaded, 16)
                act.dma_start(x0[0:TAIL, NB - 1, :], x[(NB - 1) * P:N, :]).then_inc(loaded, 16)
        merge_self_loops(L - 1)

        with nc.Block() as block:
            @block.vector
            def _(dve):
                dve.wait_ge(loaded, 16 * (len(loads) + 4))

                def add(i, k, turn):
                    c = Chain(dve, src_chain, conv_base(L - 1) + i * 3)
                    layer_output(dve, c, i, k)
                    c.link(nc.vector.tensor_add(block_of(x0, i), block_of(x0, i), part[:, k, :]))
                software_pipeline(dve, NB, 2, [(0, add)])

        with nc.Block() as block:
            normalise(block, 1, x0)

        def norm_relu_kept(dve, i, k):
            c = Chain(dve, keep_chain, i * 2)
            c.link(nc.vector.tensor_scalar(out=part[:, k, :], in0=block_of(x0, i), scalar1=ln_mv[:, at(i), 0],
                                           scalar2=ln_mv[:, at(i), 1], op0=ALU.subtract, op1=ALU.mult))
            c.link(nc.vector.tensor_scalar(out=block_of(hx, i, P), in0=part[:, k, :], scalar1=real_rows[:, at(i)],
                                           scalar2=0.0, op0=ALU.mult, op1=ALU.max))
            return nc.vector.tensor_scalar_max(hp[:, k, :], block_of(hx, i, P), 0.0)

        def to_uv(i, product):
            nc.scalar.activation(block_of(ub, i), product[:, 0:P], ACT.Copy)
            return nc.scalar.activation(block_of(acc, i, P), product[:, P:2 * P], ACT.Copy)

        with nc.Block() as block:
            prepare_rows(block, L, norm_relu_kept, None, uv_w[:, :], to_uv)

        with nc.Block() as block:
            @block.sync
            def _(sp):
                sp.dma_start(tab_blocks[:, :, 0:P], acc[:, :, 0:P]).then_inc(table_stored, 16)
                sp.wait_ge(table_stored, 16 * (L + 1))

        hot_t = exp_pair[:, :, 0, :]
        u_cur = exp_pair[:, :, 1, 0:P]
        feat = ring_b
        g0, t0 = L * NG, L * (NG // RING)
        with nc.Block() as block:
            stream_rows(block, L)

            @block.tensor
            def _(pe):
                def spread_lanes(i, k, turn):
                    r = k % 2
                    pe.wait_ge(rec_landed[k], 16 * (t0 + turn + 1))
                    if past(i, 2):
                        pe.wait_ge(hot_made, i - 1)
                    for q in range(G):
                        last = nc.tensor.matmul(bank[r][:, q * P:(q + 1) * P],
                                                rec_word(k, q, R_LANE).broadcast_to([P, P]), ident[:, :],
                                                start=True, stop=True)
                    last.then_inc(lanes_spread, 1)

                def features(i, k, turn):
                    r = k % 2
                    pe.wait_ge(hot_made, i + 1)
                    pe.wait_ge(rows_landed[k], 16 * G * (t0 + turn + 1))
                    if past(i, 2):
                        pe.wait_ge(feat_copied, i - 1)
                    nc.tensor.matmul(bank[2 + r][:, :], u_cur[:, r, :], hot_t[:, r, :], start=True, stop=False)
                    for q in range(G):
                        last = nc.tensor.matmul(bank[2 + r][:, q * P:(q + 1) * P], row_words(k, q, 0, P),
                                                ident[:, :], start=False, stop=(q == G - 1))
                    last.then_inc(slot_free, 1)
                software_pipeline(pe, NG, RING, [(1, spread_lanes), (0, features)])

            @block.vector
            def _(dve):
                def one_hot(i, k, turn):
                    r = k % 2
                    b = dve.value_load(bid[0:1, at(i)], min_val=0, max_val=NB - 1)
                    if past(i, 2):
                        dve.wait_ge(slot_free, RING + g0 + i - 1)
                        stand_alone(dve, "dve")
                    nc.vector.tensor_copy(u_cur[:, r, :], block_of(ub, b))
                    dve.wait_ge(lanes_spread, i + 1)
                    nc.vector.tensor_scalar(out=hot_t[:, r, :], in0=bank[r][:, :], scalar1=lane_col[:, :],
                                            scalar2=None, op0=ALU.is_equal).then_inc(hot_made, 1)

                def count(i, k, turn):
                    dve.wait_ge(feat_copied, i + 1)
                    nc.vector.bn_stats(bn_st[:, at(i), :].rearrange("p a c -> p (a c)"), feat[:, k % 2, :])\
                        .then_inc(feat_counted, 1)
                software_pipeline(dve, NG, RING, [(1, one_hot), (-1, count)])

            @block.scalar
            def _(act):
                def store(i, k, turn):
                    r = k % 2
                    act.wait_ge(slot_free, RING + g0 + i + 1)
                    if past(i, 2):
                        act.wait_ge(feat_counted, i - 1)
                        act.wait_ge(feat_stored[r], 16 * stored_turns(i, k, turn))
                    nc.scalar.activation(feat[:, r, :], bank[2 + r][:, :], ACT.Copy).then_inc(feat_copied, 1)
                    act.wait_ge(feat_copied, i + 1)
                    act.dma_start(e0_dram[:, span(i * GE, GE)], feat[:, r, :]).then_inc(feat_stored[r], 16)

                def stored_turns(i, k, turn):
                    return turn * (RING // 2) + k // 2
                software_pipeline(act, NG, RING, [(0, store)])
                for r in range(2):
                    act.wait_ge(feat_stored[r], 16 * (NG // 2))

        FILL = SLOTS / E
        mean, var, scale, shift_c, tmp, pad_y = (aff[:, i:i + 1] for i in range(6))
        scale1, shift1 = aff[:, 6:7], aff[:, 7:8]

        def affine(dve, act_turn, c, gamma, beta, to_scale, to_shift):
            c.link(nc.vector.tensor_mul(tmp, mean, mean))
            nc.vector.tensor_sub(var, var, tmp).then_inc(bn_ready, 1)
            dve.wait_ge(bn_act, act_turn)
            c.link(nc.vector.reciprocal(var, var))
            c.link(nc.vector.tensor_mul(to_scale, var, gamma))
            c.link(nc.vector.tensor_mul(tmp, mean, to_scale))
            c.link(nc.vector.tensor_sub(to_shift, beta, tmp))

        def whole_moments(c, factor):
            c.link(nc.vector.bn_aggr(bn_mv[:, :], bn_st[:, :, :].rearrange("p a c -> p (a c)")))
            c.link(nc.vector.tensor_mul(tmp, bn_mv[:, 0:1], bn_mv[:, 0:1]))
            c.link(nc.vector.tensor_add(var, bn_mv[:, 1:2], tmp))
            c.link(nc.vector.tensor_scalar(out=var, in0=var, scalar1=factor, scalar2=None, op0=ALU.mult))
            c.link(nc.vector.tensor_scalar(out=mean, in0=bn_mv[:, 0:1], scalar1=factor, scalar2=None, op0=ALU.mult))

        def square_root(act, turn):
            act.wait_ge(bn_ready, turn)
            nc.scalar.activation(var, var, ACT.Sqrt, bias=eps_col[:, :]).then_inc(bn_act, 1)

        with nc.Block() as block:
            @block.vector
            def _(dve):
                c = Chain(dve, bn_chain)
                whole_moments(c, FILL)
                affine(dve, 1, c, bn_par[:, 0:1], bn_par[:, 1:2], scale, shift_c)
                nc.vector.tensor_scalar_max(tmp, shift_c, 0.0).then_inc(bn_pad, 1)

            @block.scalar
            def _(act):
                square_root(act, 1)

        feat_in, relued = ring_a, ring_b
        with nc.Block() as block:
            @block.sync
            def _(sp):
                def load(i, k, turn):
                    if past(i, 4):
                        sp.wait_ge(relu_made, i - 3)
                    sp.dma_start(feat_in[:, k % 4, :], e0_dram[:, span(i * GE, GE)]).then_inc(feat_landed[k % 4], 16)
                software_pipeline(sp, NG, RING, [(0, load)])

            @block.scalar
            def _(act):
                def relu(i, k, turn):
                    act.wait_ge(feat_landed[k % 4], 16 * (turn * 2 + k // 4 + 1))
                    if past(i, 2):
                        act.wait_ge(fc_made, i - 1)
                    nc.scalar.activation(relued[:, k % 2, :], feat_in[:, k % 4, :], ACT.Relu, bias=shift_c, scale=scale)\
                        .then_inc(relu_made, 1)
                software_pipeline(act, NG, RING, [(0, relu)])

            @block.tensor
            def _(pe):
                def multiply(i, k, turn):
                    pe.wait_ge(relu_made, i + 1)
                    if past(i, 2):
                        pe.wait_ge(fc_counted, i - 1)
                    nc.tensor.matmul(bank[k % 2][:, :], fc_t[:, :], relued[:, k % 2, :], start=True, stop=True)\
                        .then_inc(fc_made, 1)
                software_pipeline(pe, NG, RING, [(0, multiply)])
                pe.wait_ge(bn_pad, 1)
                nc.tensor.matmul(bank[2][:, 0:1], fc_t[:, :], tmp, start=True, stop=True).then_inc(bn_pe, 1)

            @block.vector
            def _(dve):
                def count(i, k, turn):
                    dve.wait_ge(fc_made, i + 1)
                    nc.vector.bn_stats(bn_st[:, at(i), :].rearrange("p a c -> p (a c)"), bank[k % 2][:, :])\
                        .then_inc(fc_counted, 1)
                software_pipeline(dve, NG, RING, [(0, count)])
                dve.wait_ge(bn_pe, 1)
                nc.vector.tensor_copy(pad_y, bank[2][:, 0:1])

        EMPTY = (SLOTS - E) / E
        shift_row = ring_b
        with nc.Block() as block:
            @block.vector
            def _(dve):
                c = Chain(dve, bn_chain1)
                whole_moments(c, FILL)
                c.link(nc.vector.scalar_tensor_tensor(out=mean, in0=pad_y, scalar=-EMPTY, in1=mean,
                                                      op0=ALU.mult, op1=ALU.add))
                c.link(nc.vector.tensor_mul(tmp, pad_y, pad_y))
                c.link(nc.vector.scalar_tensor_tensor(out=var, in0=tmp, scalar=-EMPTY, in1=var,
                                                      op0=ALU.mult, op1=ALU.add))
                affine(dve, 2, c, bn_par[:, 2:3], bn_par[:, 3:4], scale1, shift1)
                nc.vector.tensor_scalar(out=fc_in[:, :], in0=fc_in[:, :], scalar1=scale1, scalar2=None, op0=ALU.mult)\
                    .then_inc(fc_scaled, 1)
                dve.wait_ge(bn_pe, 2)
                nc.vector.tensor_copy(fc_scaled_t[:, :], bank[0][:, 0:P])
                for q in range(G):
                    nc.vector.tensor_copy(shift_row[:, 0, q * P:(q + 1) * P], bank[0][:, P:2 * P])
                nc.vector.memset(acc[:, :, :], 0.0)

            @block.scalar
            def _(act):
                square_root(act, 2)

            @block.tensor
            def _(pe):
                pe.wait_ge(fc_scaled, 1)
                nc.tensor.transpose(bank[0][:, 0:P], fc_in[:, :], ident[:, :])
                nc.tensor.matmul(bank[0][:, P:2 * P], shift1.broadcast_to([P, P]), ident[:, :], start=True, stop=True)\
                    .then_inc(bn_pe, 1)

        relued3 = att_t
        lane_hots, biased, message = exp_pair, att, hot
        with nc.Block() as block:
            @block.sync
            def _(sp):
                def load(i, k, turn):
                    if past(i, 4):
                        sp.wait_ge(c_summed, i - 3)
                    sp.dma_start(recs[:, k % 4, :], rec_groups[at(i)].rearrange("a p w -> (a p) w"))\
                        .then_inc(c_landed[k % 4], 16)
                    sp.dma_start(feat_in[:, k % 4, :], e0_dram[:, span(i * GE, GE)]).then_inc(c_landed[k % 4], 16)
                software_pipeline(sp, NG, RING, [(0, load)])

            @block.scalar
            def _(act):
                def relu(i, k, turn):
                    act.wait_ge(c_landed[k % 4], 32 * (turn * 2 + k // 4 + 1))
                    if past(i, 2):
                        act.wait_ge(c_fc, i - 1)
                    nc.scalar.activation(relued3[:, k % 2, :], feat_in[:, k % 4, :], ACT.Relu, bias=shift_c, scale=scale)\
                        .then_inc(c_relu, 1)

                def relu_message(i, k, turn):
                    act.wait_ge(c_biased, i + 1)
                    if past(i, 2):
                        act.wait_ge(c_summed, i - 1)
                    nc.scalar.activation(message[:, k % 2, :], biased[:, k % 2, :], ACT.Relu).then_inc(c_msg, 1)
                software_pipeline(act, NG, RING, [(1, relu), (-1, relu_message)])

            @block.tensor
            def _(pe):
                def multiply(i, k, turn):
                    pe.wait_ge(c_relu, i + 1)
                    if past(i, 2):
                        pe.wait_ge(c_biased, i - 1)
                    for q in range(G):
                        last = nc.tensor.matmul(bank[k % 2][:, q * P:(q + 1) * P],
                                                relued3[:, k % 2, q * P:(q + 1) * P], fc_scaled_t[:, :],
                                                start=True, stop=True)
                    last.then_inc(c_fc, 1)

                def add_up(i, k, turn):
                    pe.wait_ge(c_msg, i + 1)
                    pe.wait_ge(c_hot, i + 1)
                    if past(i, 2):
                        pe.wait_ge(c_added, i - 1)
                    for q in range(G):
                        last = nc.tensor.matmul(bank[2 + k % 2][:, 0:P], lane_hots[:, k % 2, 0, q * P:(q + 1) * P],
                                                message[:, k % 2, q * P:(q + 1) * P],
                                                start=(q == 0), stop=(q == G - 1))
                    last.then_inc(c_summed, 1)
                software_pipeline(pe, NG, RING, [(1, multiply), (-1, add_up)])

            @block.vector
            def _(dve):
                def hots(i, k, turn):
                    dve.wait_ge(c_landed[k % 4], 32 * (turn * 2 + k // 4 + 1))
                    if past(i, 2):
                        dve.wait_ge(c_summed, i - 1)
                    for q in range(G):
                        last = nc.vector.tensor_scalar(out=lane_hots[:, k % 2, 0, q * P:(q + 1) * P], in0=lane_row[:, :],
                                                       scalar1=rec_word(k % 4, q, R_LANE), scalar2=None,
                                                       op0=ALU.is_equal)
                    last.then_inc(c_hot, 1)

                def add_shift(i, k, turn):
                    dve.wait_ge(c_fc, i + 1)
                    if past(i, 2):
                        dve.wait_ge(c_msg, i - 1)
                    nc.vector.tensor_add(biased[:, k % 2, :], bank[k % 2][:, :], shift_row[:, 0, :])\
                        .then_inc(c_biased, 1)

                def add_group(i, k, turn):
                    b = dve.value_load(bid[0:1, at(i)], min_val=0, max_val=NB - 1)
                    dve.wait_ge(c_summed, i + 1)
                    if past(i, 1):
                        dve.wait_ge(c_added, i)
                    nc.vector.tensor_add(block_of(acc, b, P), block_of(acc, b, P), bank[2 + k % 2][:, 0:P])\
                        .then_inc(c_added, 1)
                software_pipeline(dve, NG, RING, [(0, add_shift), (0, hots), (-2, add_group)])

        with nc.Block() as block:
            @block.vector
            def _(dve):
                def finish(i, k, turn):
                    c = Chain(dve, fin_chain, i)
                    c.link(nc.vector.scalar_tensor_tensor(out=part[:, k, :], in0=block_of(acc, i, P),
                                                          scalar=inv_deg[:, at(i)], in1=block_of(hx, i, P),
                                                          op0=ALU.mult, op1=ALU.add))
                    nc.vector.scalar_tensor_tensor(out=block_of(ub, i), in0=part[:, k, :], scalar=0.0,
                                                   in1=block_of(x0, i), op0=ALU.max, op1=ALU.add)\
                        .then_inc(out_made, 1)
                software_pipeline(dve, NB, 2, [(0, finish)])

            @block.sync
            def _(sp):
                sp.wait_ge(out_made, NB)
                sp.dma_start(out[0:(NB - 1) * P, :].rearrange("(b p) c -> p b c", p=P), ub[:, 0:NB - 1, :])\
                    .then_inc(out_stored, 16)
                sp.dma_start(out[(NB - 1) * P:N, :], ub[0:TAIL, NB - 1, :]).then_inc(out_stored, 16)
                sp.wait_ge(out_stored, 32)

    return None


_INS = ['x', 'src', 'dst', 'edge_attr_16', 'L0_gnn_Ws', 'L0_gnn_Wes', 'L0_gnn_a_srcs', 'L0_gnn_a_dsts',
        'L0_gnn_a_edges', 'L0_gnn_biases', 'L0_gnn_mid_ws', 'L1_gnn_theta_w', 'L1_gnn_phi_w', 'L1_gnn_fc1_w',
        'L1_gnn_bn0_g', 'L1_gnn_bn0_b', 'L1_gnn_bn1_g', 'L1_gnn_bn1_b']


def kernel(**inputs):
    import concourse.bacc as bacc
    from concourse.bass_utils import run_bass_kernel_spmd

    nc = bacc.Bacc("TRN2", target_bir_lowering=False, num_devices=1)
    arrays, args = {}, []
    for name in _INS:
        a = np.ascontiguousarray(inputs[name])
        arrays[f"in_{name}"] = a
        args.append(nc.dram_tensor(f"in_{name}", a.shape, mybir.dt.from_np(a.dtype), kind="ExternalInput").ap())
    shape = tuple(inputs['x'].shape)
    out = nc.dram_tensor("out", shape, F32, kind="ExternalOutput").ap()
    gnn_kernel(nc, *args, out)
    r = run_bass_kernel_spmd(nc, [arrays], core_ids=[0])
    return r.results[0]["out"]
```

```python
import math
from contextlib import ExitStack

import numpy as np
import concourse.bass as bass
from concourse import mybir

ALU = mybir.AluOpType
ACT = mybir.ActivationFunctionType
AX = mybir.AxisListType
F32 = mybir.dt.float32
BF16 = mybir.dt.bfloat16
I32 = mybir.dt.int32
U32 = mybir.dt.uint32

P = 128
G = 4
GE = G * P
RING = 10
REC = 8
R_SRC, R_LANE, R_TERM = 0, 1, 2
NO_LANE = 255.0
BIG = 2.0 ** 100
NO_MAX = -1e20
ATT_SLOPE, OUT_SLOPE = 0.2, 0.01
ALPHA, THETA = 0.2, 0.2
EPS = 1e-5


class Chain:

    def __init__(self, eng, sem, base=0):
        self.eng, self.sem, self.base, self.n = eng, sem, base, 0

    def link(self, ins):
        self.n += 1
        ins.then_inc(self.sem, 1)
        self.eng.wait_ge(self.sem, self.base + self.n)


def at(i):
    return slice(i, i + 1) if isinstance(i, int) else bass.ds(i, 1)


def span(start, size):
    return slice(start, start + size) if isinstance(start, int) else bass.ds(start, size)


def past(i, n):
    return i >= n if isinstance(i, int) else True


def software_pipeline(eng, n, unroll, stages):
    low, high = min(o for o, _ in stages), max(o for o, _ in stages)
    first = -(-(unroll - low) // unroll)
    last = (n - high) // unroll

    def step(turn, k):
        for offset, stage in stages:
            i = turn * unroll + (k + offset)
            if not isinstance(i, int) or 0 <= i < n:
                stage(i, (k + offset) % unroll, turn + (k + offset) // unroll)

    for j in range(-high, first * unroll):
        step(j // unroll, j % unroll)
    if last > first:
        with eng.Fori(first, last) as turn:
            for k in range(unroll):
                step(turn, k)
    for j in range(max(last, first) * unroll, n - low):
        step(j // unroll, j % unroll)


def gnn_kernel(nc, x, src, dst, edge_attr_16, Ws, Wes, a_srcs, a_dsts, a_edges, biases, mid_ws,
               theta_w, phi_w, fc1_w, bn0_g, bn0_b, bn1_g, bn1_b, out):
    N, C = x.shape
    E = src.shape[0]
    ED = edge_attr_16.shape[1]
    L = Ws.shape[0]
    assert C == P and L == 5 and REC == L + 3
    NB = -(-N // P)
    TAIL = N - (NB - 1) * P
    BATCH = 8
    NG_STEP = math.lcm(RING, BATCH)
    NG = -(-((E + NB * (GE - 1)) // GE) // NG_STEP) * NG_STEP
    SLOTS = NG * GE
    NGP = -(-NG // P)
    EP = max(p for p in range(1, P + 1) if E % p == 0)
    ET = E // EP
    CH = 32
    TC = P // ED
    assert ET % (2 * CH) == 0 and CH * ED == GE and P % ED == 0 and NG % BATCH == 0
    NCH = ET // CH
    TW = P + 3
    TABLE_PARTS = max(p for p in range(1, 9) if NB % p == 0)
    PB = NB // TABLE_PARTS
    HW = L + 1
    LANE_BITS = 7
    betas = [math.log(THETA / (i + 1) + 1.0) for i in range(mid_ws.shape[0])]

    listed_dram = nc.dram_tensor("records_as_listed", [E + GE, REC], F32, kind="Internal").ap()
    first_dram = nc.dram_tensor("group_firsts", [NGP * P], I32, kind="Internal").ap()
    base_dram = nc.dram_tensor("group_bases", [NGP * P], F32, kind="Internal").ap()
    rec_dram = nc.dram_tensor("edge_records", [SLOTS, REC], F32, kind="Internal").ap()
    tab_dram = nc.dram_tensor("node_table", [NB * P, TW], F32, kind="Internal").ap()
    bid_dram = nc.dram_tensor("group_blocks", [NGP * P], I32, kind="Internal").ap()
    e0_dram = nc.dram_tensor("edge_features", [P, SLOTS], F32, kind="Internal").ap()
    rec_groups = rec_dram.rearrange("(g p q) w -> g p (q w)", p=P, q=G)
    tab_blocks = tab_dram.rearrange("(b p) c -> p b c", p=P)

    ctx = ExitStack()
    with ctx:
        def sb(name, shape, dt=F32):
            return ctx.enter_context(nc.sbuf_tensor(name, shape, dt))

        def sem(name):
            return ctx.enter_context(nc.semaphore(name))

        ident = sb("ident", [P, P])
        mask_ident = sb("mask_ident", [P, P], BF16)
        lane_row = sb("lane_row", [P, P])
        lane_row_b = sb("lane_row_b", [P, P], BF16)
        lane_col = sb("lane_col", [P, 1])
        before = sb("before", [P, P])
        ones = sb("ones", [P, P])
        group_no = sb("group_no", [P, NGP])
        slopes = sb("slopes", [P, 2])
        eps_col = sb("eps_col", [P, 1])
        real_rows = sb("real_rows", [P, NB])
        w_ext = sb("w_ext", [P, L, P + 2])
        mix = sb("mix", [P, L - 2, P])
        bias_last = sb("bias_last", [P, P])
        bias_cols = sb("bias_cols", [P, L])
        mix_cur = sb("mix_cur", [P, P])
        bias_cur = sb("bias_cur", [P, 1])
        uv_w = sb("uv_w", [P, 2 * P])
        fc_in = sb("fc_in", [P, P])
        fc_t = sb("fc_t", [P, P])
        fc_scaled_t = sb("fc_scaled_t", [P, P])
        own_columns = sb("own_columns", [P, TC, L])
        term_w = sb("term_w", [P, TC, L])
        bn_par = sb("bn_par", [P, 4])
        acc = sb("acc", [P, NB, P + 1])
        hx = sb("hx", [P, NB, TW])
        x0 = sb("x0", [P, NB, P])
        ub = sb("ub", [P, NB, P])
        blk = sb("blk", [P, NB, 3])
        sums = sb("sums", [P, NB, HW])
        loop_term = sb("loop_term", [P, L, NB])
        inv_deg = sb("inv_deg", [P, NB])
        small = sb("small", [P, 8, NB])
        ln_stat = sb("ln_stat", [P, NB, 6])
        ln_mv = sb("ln_mv", [P, NB, 2])
        bid = sb("bid", [1, NGP * P], I32)
        first = sb("first", [1, NGP * P], I32)
        flag = sb("flag", [1, 1], I32)
        group_tables = sb("group_tables", [P, 5, NGP])
        recs = sb("recs", [P, RING, G * REC])
        rows = sb("rows", [P, RING, G * TW])
        other_lane = sb("other_lane", [P, 2, G * P], BF16)
        u_edge = sb("u_edge", [P, 2, G])
        exp_pair = sb("exp_pair", [P, 2, 2, GE])
        att_t = sb("att_t", [P, 2, GE])
        att = sb("att", [P, 2, GE])
        cur = sb("cur", [P, 2, 3])
        gmax = sb("gmax", [P, 2, 4])
        shift = sb("shift", [P, 2, 3])
        rescale = sb("rescale", [P, RING, 1])
        bn_st = sb("bn_st", [P, NG, 6])
        bn_mv = sb("bn_mv", [P, 2])
        aff = sb("aff", [P, 12])
        ring_a = sb("ring_a", [P, 4, GE])
        ring_b = sb("ring_b", [P, 2, GE])
        node_ring = sb("node_ring", [P, 6, 2, P])
        hot = sb("hot", [P, 2, GE])
        slot_ring = sb("slot_ring", [EP, 2, CH], U32)

        bank = [ctx.enter_context(nc.psum_tensor(f"bank{i}", [P, 512], F32)) for i in range(8)]

        x0_flat = x0[:, :, :].rearrange("p b c -> p (b c)")
        acc_flat = acc[:, :, :].rearrange("p b c -> p (b c)")
        ub_flat = ub[:, :, :].rearrange("p b c -> p (b c)")
        assert 3 * ET <= NB * P and 4 * CH * REC <= 2 * GE and 4 * BATCH * G * REC <= 2 * GE and NGP * P <= GE
        slot_f = x0_flat[0:EP, 0:ET]
        dst_f = x0_flat[0:EP, ET:2 * ET]
        src_i = x0_flat[0:EP, 2 * ET:3 * ET].bitcast(I32)
        hi_f = acc_flat[0:EP, 0:ET]
        hit_i = acc_flat[0:EP, ET:2 * ET].bitcast(I32)
        run_f = acc_flat[0:EP, 2 * ET:3 * ET]
        dst_i = ub_flat[0:EP, 0:ET].bitcast(I32)
        tmp_i = ub_flat[0:EP, ET:2 * ET].bitcast(I32)
        lane_f = ub_flat[0:EP, ET:2 * ET]
        hit_f = ub_flat[0:EP, 2 * ET:3 * ET]
        attr_ring, attr_t = ring_a, ring_b
        rec_ring = exp_pair[0:EP, 0, :, :].rearrange("p a e -> p (a e)").rearrange("p (r t w) -> p r t w", r=4, w=REC)
        move_ring = exp_pair[:, 1, :, :].rearrange("p a e -> p (a e)").rearrange("p (r e) -> p r e", r=4)
        group_base = att[:, 0, :]

        loaded = sem("loaded")
        constants_made = sem("constants_made")
        bias_chain = sem("bias_chain")
        dve_chain = sem("dve_chain")
        pool_chain = sem("pool_chain")
        transposed = sem("transposed")
        copied = sem("copied")
        projected = sem("projected")
        count_chain = sem("count_chain")
        slot_chain = sem("slot_chain")
        counted = sem("counted")
        offsets_made = sem("offsets_made")
        summed = sem("summed")
        tables_stored = sem("tables_stored")
        tables_loaded = sem("tables_loaded")
        order_seen = sem("order_seen")
        order_chain = sem("order_chain")
        order_summed = sem("order_summed")
        attr_landed = [sem(f"attr_landed{i}") for i in range(4)]
        attr_turned = sem("attr_turned")
        attr_copied = sem("attr_copied")
        terms_made = sem("terms_made")
        terms_copied = sem("terms_copied")
        ends_copied = sem("ends_copied")
        listed = [sem(f"listed{i}") for i in range(4)]
        tail_stored = sem("tail_stored")
        move_landed = [sem(f"move_landed{i}") for i in range(4)]
        move_landed_pool = [sem(f"move_landed_pool{i}") for i in range(4)]
        moved = [sem(f"moved{i}") for i in range(4)]
        move_chain = sem("move_chain")
        pads_made = sem("pads_made")
        pads_stored = sem("pads_stored")
        chunk_landed = [sem(f"chunk_landed{i}") for i in range(2)]
        scattered = [sem(f"scattered{i}") for i in range(2)]
        chunk_made = sem("chunk_made")
        lanes_hot = sem("lanes_hot")
        sums_made = sem("sums_made")
        sums_cleared = sem("sums_cleared")
        sums_added = sem("sums_added")
        x_landed = sem("x_landed")
        ln_act = sem("ln_act")
        ln_counted = sem("ln_counted")
        ln_chain = sem("ln_chain")
        src_made = sem("src_made")
        src_transposed = sem("src_transposed")
        src_copied = sem("src_copied")
        mixed = sem("mixed")
        mix_copied = sem("mix_copied")
        mix_bent = sem("mix_bent")
        rows_made = sem("rows_made")
        rows_copied = sem("rows_copied")
        table_stored = sem("table_stored")
        start_chain = sem("start_chain")
        rec_landed = [sem(f"rec_landed{i}") for i in range(RING)]
        rows_landed = [sem(f"rows_landed{i}") for i in range(RING)]
        slot_free = sem("slot_free")
        u_made = sem("u_made")
        logits_made = sem("logits_made")
        max_chain = sem("max_chain")
        shift_made = sem("shift_made")
        exps_made = sem("exps_made")
        att_t_made = sem("att_t_made")
        att_turned = sem("att_turned")
        att_made = sem("att_made")
        acc_added = sem("acc_added")
        mrg_chain = sem("mrg_chain")
        mrg_sub = sem("mrg_sub")
        own_made = sem("own_made")
        part_made = sem("part_made")
        x0_kept = sem("x0_kept")
        x0_added = sem("x0_added")
        degree_chain = sem("degree_chain")
        mrg_exp = sem("mrg_exp")
        lanes_spread = sem("lanes_spread")
        hot_made = sem("hot_made")
        feat_counted = sem("feat_counted")
        feat_copied = sem("feat_copied")
        feat_stored = [sem(f"feat_stored{i}") for i in range(2)]
        bn_chain = sem("bn_chain")
        bn_chain1 = sem("bn_chain1")
        bn_ready = sem("bn_ready")
        bn_pad = sem("bn_pad")
        fc_scaled = sem("fc_scaled")
        rows_kept = sem("rows_kept")
        waited = {e: sem(f"waited_{e}") for e in ("dve", "pool", "sp")}
        bn_act = sem("bn_act")
        bn_pe = sem("bn_pe")
        feat_landed = [sem(f"feat_landed{i}") for i in range(4)]
        relu_made = sem("relu_made")
        fc_made = sem("fc_made")
        fc_counted = sem("fc_counted")
        c_landed = [sem(f"c_landed{i}") for i in range(4)]
        c_rec_landed = [sem(f"c_rec_landed{i}") for i in range(BATCH)]
        c_relu = sem("c_relu")
        c_hot = sem("c_hot")
        c_hot_late = sem("c_hot_late")
        c_fc = sem("c_fc")
        c_biased = sem("c_biased")
        c_msg = sem("c_msg")
        c_summed = sem("c_summed")
        c_added = sem("c_added")
        means_made = sem("means_made")
        sums_finished = sem("sums_finished")
        out_made = sem("out_made")
        out_stored = sem("out_stored")

        def stand_alone(eng, name):
            eng.sem_inc(waited[name], 1)

        wst = hx[:, 0:L, 0:P]
        w_t = hx[:, L:2 * L, 0:P]
        midst = hx[:, 2 * L:2 * L + 3, 0:P]
        thst, phst = hx[:, 13, 0:P], hx[:, 14, 0:P]
        west, aest = hx[:, 19:19 + L, 0:P], hx[:, 19 + L:19 + 2 * L, 0:P]
        a_rows = [hx[0:L, 17, 0:P], hx[0:L, 18, 0:P]]
        b_rows = hx[0:L, 15, 0:P]
        a_cols = small[:, 0:2, 0:L]
        term_cols = small[:, 2, 0:L]
        loads = [
            (dst_i, dst.rearrange("(p t) -> p t", p=EP)),
            (src_i, src.rearrange("(p t) -> p t", p=EP)),
            (wst, Ws.rearrange("l k j -> k l j")),
            (midst, mid_ws.rearrange("l k j -> k l j")),
            (thst, theta_w), (phst, phi_w), (fc_in[:, :], fc1_w),
            (a_rows[0], a_srcs), (a_rows[1], a_dsts), (b_rows, biases),
            (bias_last[:, :], biases[L - 1:L, :].broadcast_to([P, P])),
        ]
        for l in range(L):
            loads.append((aest[:, l, :], a_edges[l:l + 1, :].broadcast_to([P, P])))
        for t in range(TC):
            loads.append((west[t * ED:(t + 1) * ED, :, :], Wes.rearrange("l k j -> k l j")))
        for i, v in enumerate((bn0_g, bn0_b, bn1_g, bn1_b)):
            loads.append((bn_par[:, i:i + 1], v.rearrange("(p a) -> p a", a=1)))

        with nc.Block() as block:
            @block.sync
            def _(sp):
                for to, of in loads:
                    sp.dma_start(to, of).then_inc(loaded, 16)

            @block.gpsimd
            def _(pool):
                c = Chain(pool, pool_chain)
                c.link(nc.gpsimd.memset(ident[:, :], 0.0))
                c.link(nc.gpsimd.affine_select(out=ident[:, :], in_=ident[:, :], compare_op=ALU.not_equal,
                                               fill=1.0, base=0, pattern=[[-1, P]], channel_multiplier=1))
                for to, pattern, lane_step in ((lane_row[:, :], [[1, P]], 0), (lane_row_b[:, :], [[1, P]], 0),
                                               (lane_col[:, :], [[0, 1]], 1),
                                               (group_no[:, :], [[1, NGP]], NGP)):
                    nc.gpsimd.iota(to, pattern=pattern, base=0, channel_multiplier=lane_step,
                                   allow_small_or_imprecise_dtypes=True)
                c.link(nc.gpsimd.memset(ones[:, :], 1.0))
                nc.gpsimd.affine_select(out=before[:, :], in_=ones[:, :], compare_op=ALU.is_gt,
                                        fill=0.0, base=0, pattern=[[1, P]], channel_multiplier=-1)
                nc.gpsimd.affine_select(out=real_rows[:, :], in_=ones[:, 0:NB], compare_op=ALU.is_gt,
                                        fill=0.0, base=N, pattern=[[-P, NB]], channel_multiplier=-1)
                c.link(nc.gpsimd.memset(own_columns[:, :, :], 1.0))
                c.link(nc.gpsimd.affine_select(out=own_columns[:, :, :], in_=own_columns[:, :, :],
                                               compare_op=ALU.is_ge, fill=0.0, base=0, pattern=[[-ED, TC], [0, L]],
                                               channel_multiplier=1))
                nc.gpsimd.affine_select(out=own_columns[:, :, :], in_=own_columns[:, :, :], compare_op=ALU.is_gt,
                                        fill=0.0, base=ED, pattern=[[ED, TC], [0, L]], channel_multiplier=-1)
                nc.gpsimd.memset(slopes[:, 0:1], 1.0)
                nc.gpsimd.memset(slopes[:, 1:2], ATT_SLOPE)
                nc.gpsimd.memset(eps_col[:, :], EPS)
                nc.gpsimd.memset(rec_ring[:, :, :, R_TERM + L:REC], 1.0)
                c.link(nc.gpsimd.memset(recs[:, 0, :], 1.0))
                tail = recs[:, 0, :].rearrange("p (q w) -> p q w", w=REC)
                nc.gpsimd.memset(tail[:, :, R_SRC].bitcast(I32), N)
                nc.gpsimd.memset(tail[:, :, R_LANE], float(2 * NB * P))
                nc.gpsimd.memset(small[:, :, :], 0.0).then_inc(constants_made, 1)

            @block.vector
            def _(dve):
                c = Chain(dve, dve_chain)
                dve.wait_ge(constants_made, 1)
                dve.wait_ge(loaded, 16 * len(loads))
                nc.vector.tensor_scalar(out=mask_ident[:, :], in0=ident[:, :], scalar1=-BIG, scalar2=None,
                                        op0=ALU.mult)
                for i, beta in enumerate(betas):
                    c.link(nc.vector.tensor_scalar(out=mix[:, i, :], in0=ident[:, :], scalar1=1.0 - beta,
                                                   scalar2=None, op0=ALU.mult))
                    nc.vector.scalar_tensor_tensor(out=mix[:, i, :], in0=midst[:, i, :], scalar=beta,
                                                   in1=mix[:, i, :], op0=ALU.mult, op1=ALU.add)
                nc.vector.tensor_copy(w_ext[:, :, 0:P], wst)
                nc.vector.tensor_sub(phst, phst, thst)
                c.link(nc.vector.tensor_mul(west, west, aest))
                c.link(nc.vector.reduce_sum(term_cols, west, AX.X))
                nc.vector.tensor_tensor(
                    out=term_w[:, :, :], in0=own_columns[:, :, :],
                    in1=term_cols.rearrange("p (a l) -> p a l", a=1).broadcast_to([P, TC, L]), op=ALU.mult)
                nc.vector.tensor_copy(dst_f, dst_i)
                c.link(nc.vector.tensor_single_scalar(tmp_i, dst_i, LANE_BITS, op=ALU.arith_shift_right))
                c.link(nc.vector.tensor_copy(hi_f, tmp_i))
                c.link(nc.vector.tensor_single_scalar(tmp_i, dst_i, P - 1, op=ALU.bitwise_and))
                nc.vector.tensor_copy(lane_f, tmp_i)

        with nc.Block() as block:
            @block.tensor
            def _(pe):
                for l in range(L):
                    nc.tensor.transpose(bank[l // 4][:, (l % 4) * P:(l % 4 + 1) * P], wst[:, l, :], ident[:, :])
                nc.tensor.transpose(bank[2][:, 0:P], thst, ident[:, :])
                nc.tensor.transpose(bank[2][:, P:2 * P], phst, ident[:, :])
                nc.tensor.transpose(bank[2][:, 2 * P:3 * P], fc_in[:, :], ident[:, :])
                for i in range(2):
                    nc.tensor.transpose(bank[3][:, i * L:(i + 1) * L], a_rows[i], ident[0:L, 0:L])
                nc.tensor.transpose(bank[3][:, 2 * L:3 * L], b_rows, ident[0:L, 0:L]).then_inc(transposed, 1)
                pe.wait_ge(copied, 1)
                for l in range(L):
                    last = nc.tensor.matmul(bank[5][:, 2 * l:2 * l + 2], w_t[:, l, :], a_cols[:, :, l],
                                            start=True, stop=True)
                last.then_inc(projected, 1)

            @block.vector
            def _(dve):
                dve.wait_ge(transposed, 1)
                for l in range(L):
                    nc.vector.tensor_copy(w_t[:, l, :], bank[l // 4][:, (l % 4) * P:(l % 4 + 1) * P])
                nc.vector.tensor_copy(uv_w[:, :], bank[2][:, 0:2 * P])
                nc.vector.tensor_copy(fc_t[:, :], bank[2][:, 2 * P:3 * P])
                nc.vector.tensor_copy(a_cols, bank[3][:, 0:2 * L].rearrange("p (s l) -> p s l", s=2))\
                    .then_inc(copied, 1)
                c = Chain(dve, bias_chain)
                c.link(nc.vector.tensor_copy(bias_cols[:, :], bank[3][:, 2 * L:3 * L]))
                for l in range(1, L - 1):
                    c.link(nc.vector.tensor_scalar(out=bias_cols[:, l:l + 1], in0=bias_cols[:, l:l + 1],
                                                   scalar1=1.0 - ALPHA, scalar2=None, op0=ALU.mult))
                    nc.vector.scalar_tensor_tensor(out=bias_cols[:, l:l + 1], in0=bias_cols[:, 0:1], scalar=ALPHA,
                                                   in1=bias_cols[:, l:l + 1], op0=ALU.mult, op1=ALU.add)
                dve.wait_ge(projected, 1)
                nc.vector.tensor_copy(w_ext[:, :, P:P + 2],
                                      bank[5][:, 0:2 * L].rearrange("p (l s) -> p l s", s=2))

        cnt = small[0:EP, 3, :]
        total, groups, ends, base = (small[:, i, :] for i in (4, 5, 6, 7))
        filled = small[:, 1, :]
        out_of_order = small[0:EP, 2, 0:1]
        ones_nb = ones[:, 0:NB]
        whole_i = small[:, 0, :].bitcast(I32)
        bid_f, base_f, first_f = (group_tables[:, i, :] for i in range(3))
        bid_i, first_i = (group_tables[:, i, :].bitcast(I32) for i in (3, 4))
        below = ln_stat[:, :, 0]
        attr_cols = edge_attr_16.rearrange("(p t) k -> p t k", p=EP)
        listed_cols = listed_dram[0:E, :].rearrange("(p t) w -> p t w", p=EP)
        with nc.Block() as block:
            @block.sync
            def _(sp):
                sp.dma_start(listed_dram[E:E + GE, :].rearrange("(p q) w -> p (q w)", p=P), recs[:, 0, :])\
                    .then_inc(tail_stored, 16)

                def load(i, k, turn):
                    if past(i, 4):
                        sp.wait_ge(attr_turned, i - 3)
                    sp.dma_start(attr_ring[0:EP, k, :].rearrange("p (t d) -> p t d", d=ED),
                                 attr_cols[:, span(i * CH, CH), :]).then_inc(attr_landed[k], 16)

                def store(i, k, turn):
                    sp.wait_ge(terms_copied, i + 1)
                    sp.wait_ge(ends_copied, i + 1)
                    sp.dma_start(listed_cols[:, span(i * CH, CH), :], rec_ring[:, k, :, :]).then_inc(listed[k], 16)
                software_pipeline(sp, NCH, 4, [(2, load), (-1, store)])
                sp.wait_ge(summed, 1)
                for to, of in ((bid_dram, bid_i), (first_dram, first_i), (base_dram, base_f)):
                    sp.dma_start(to.rearrange("(p j) -> p j", j=NGP), of).then_inc(tables_stored, 16)
                sp.wait_ge(tables_stored, 48)
                sp.dma_start(bid[:, :], bid_dram.rearrange("(a g) -> a g", a=1)).then_inc(tables_loaded, 16)
                sp.dma_start(first[:, :], first_dram.rearrange("(a g) -> a g", a=1)).then_inc(tables_loaded, 16)
                sp.dma_start(group_base[:, 0:NGP * P],
                             base_dram.rearrange("(a g) -> a g", a=1).broadcast_to([P, NGP * P]))\
                    .then_inc(tables_loaded, 16)
                sp.wait_ge(tables_loaded, 48)
                sp.wait_ge(tail_stored, 16)
                for k in range(4):
                    sp.wait_ge(listed[k], 16 * len(range(k, NCH, 4)))

            @block.tensor
            def _(pe):
                def turn_attributes(i, k, turn):
                    r = k % 2
                    pe.wait_ge(attr_landed[k], 16 * (turn + 1))
                    if past(i, 2):
                        pe.wait_ge(attr_copied, i - 1)
                    for j in range(CH // TC):
                        last = nc.tensor.transpose(bank[r][:, j * EP:(j + 1) * EP],
                                                   attr_ring[0:EP, k, j * P:(j + 1) * P], ident[0:EP, 0:EP])
                    last.then_inc(attr_turned, 1)

                def make_terms(i, k, turn):
                    r = k % 2
                    pe.wait_ge(attr_copied, i + 1)
                    if past(i, 2):
                        pe.wait_ge(terms_copied, i - 1)
                    for j in range(CH // TC):
                        last = nc.tensor.matmul(bank[2 + r][0:EP, j * TC * L:(j + 1) * TC * L],
                                                attr_t[:, r, j * EP:(j + 1) * EP],
                                                term_w[:, :, :].rearrange("p t l -> p (t l)"), start=True, stop=True)
                    last.then_inc(terms_made, 1)
                software_pipeline(pe, NCH, 4, [(0, turn_attributes), (-1, make_terms)])
                pe.wait_ge(count_chain, NB)
                nc.tensor.matmul(bank[6][:, 0:NB], before[0:EP, :], cnt, start=True, stop=True)
                nc.tensor.matmul(bank[6][:, 64:64 + NB], ones[0:EP, :], cnt, start=True, stop=True)
                nc.tensor.matmul(bank[6][0:EP - 1, 128:129], ident[0:EP, 1:EP], hi_f[:, 0:1], start=True, stop=True)\
                    .then_inc(counted, 1)
                pe.wait_ge(order_seen, 1)
                nc.tensor.matmul(bank[6][0:1, 130:131], out_of_order, ones[0:EP, 0:1], start=True, stop=True)\
                    .then_inc(order_summed, 1)

            @block.scalar
            def _(act):
                def copy_turned(i, k, turn):
                    act.wait_ge(attr_turned, i + 1)
                    if past(i, 2):
                        act.wait_ge(terms_made, i - 1)
                    nc.scalar.activation(attr_t[:, k % 2, 0:EP * (CH // TC)], bank[k % 2][:, 0:EP * (CH // TC)], ACT.Copy)\
                        .then_inc(attr_copied, 1)

                def copy_terms(i, k, turn):
                    act.wait_ge(terms_made, i + 1)
                    if past(i, 4):
                        act.wait_ge(listed[k], 16 * turn)
                    nc.scalar.activation(rec_ring[:, k, :, R_TERM:R_TERM + L],
                                         bank[2 + k % 2][0:EP, 0:CH * L].rearrange("p (t l) -> p t l", l=L), ACT.Copy)\
                        .then_inc(terms_copied, 1)
                software_pipeline(act, NCH, 4, [(0, copy_turned), (-1, copy_terms)])

            @block.gpsimd
            def _(pool):
                def copy_ends(i, k, turn):
                    if past(i, 4):
                        pool.wait_ge(listed[k], 16 * turn)
                        stand_alone(pool, "pool")
                    nc.gpsimd.tensor_copy(rec_ring[:, k, :, R_SRC].bitcast(I32), src_i[:, span(i * CH, CH)])
                    nc.gpsimd.tensor_copy(rec_ring[:, k, :, R_LANE], dst_f[:, span(i * CH, CH)]).then_inc(ends_copied, 1)
                software_pipeline(pool, NCH, 4, [(0, copy_ends)])

            @block.vector
            def _(dve):
                with dve.Fori(0, NB) as b:
                    Chain(dve, count_chain, b).link(
                        nc.vector.tensor_scalar(out=hit_f, in0=hi_f, scalar1=lane_row[0:EP, at(b)], scalar2=None,
                                                op0=ALU.is_equal, op1=ALU.add, accum_out=cnt[:, at(b)]))
                    stand_alone(dve, "dve")
                c = Chain(dve, order_chain)
                c.link(nc.vector.tensor_tensor(out=hit_f[:, 0:ET - 1], in0=hi_f[:, 0:ET - 1], in1=hi_f[:, 1:ET],
                                               op=ALU.is_gt))
                c.link(nc.vector.reduce_sum(out_of_order, hit_f[:, 0:ET - 1], AX.X))
                dve.wait_ge(counted, 1)
                c.link(nc.vector.tensor_tensor(out=hit_f[0:EP - 1, 0:1], in0=hi_f[0:EP - 1, ET - 1:ET],
                                               in1=bank[6][0:EP - 1, 128:129], op=ALU.is_gt))
                c.link(nc.vector.tensor_add(out_of_order[0:EP - 1, :], out_of_order[0:EP - 1, :],
                                            hit_f[0:EP - 1, 0:1]))
                c = Chain(dve, offsets_made)
                c.link(nc.vector.tensor_scalar_add(total, bank[6][:, 64:64 + NB], float(GE - 1)))
                c.link(nc.vector.tensor_copy(whole_i, total))
                c.link(nc.vector.tensor_single_scalar(whole_i, whole_i, GE.bit_length() - 1,
                                                      op=ALU.arith_shift_right))
                c.link(nc.vector.tensor_copy(groups, whole_i))
                c.link(nc.vector.tensor_tensor_scan(ends, ones_nb, groups, 0.0, ALU.mult, ALU.add))
                c.link(nc.vector.tensor_sub(base, ends, groups))
                c.link(nc.vector.tensor_scalar(out=base, in0=base, scalar1=float(GE), scalar2=-1.0,
                                               op0=ALU.mult, op1=ALU.add))
                c.link(nc.vector.tensor_add(base, base, bank[6][:, 0:NB]))
                c.link(nc.vector.scalar_tensor_tensor(out=filled, in0=groups, scalar=float(GE), in1=total,
                                                      op0=ALU.mult, op1=ALU.subtract))
                c.link(nc.vector.tensor_scalar_add(filled, filled, float(GE - 1)))
                nc.vector.memset(bid_f, 0.0).then_inc(order_seen, 1)
                dve.wait_ge(order_seen, 1)
                for j in range(NGP):
                    c.link(nc.vector.tensor_scalar(out=below, in0=ends, scalar1=group_no[:, j:j + 1], scalar2=None,
                                                   op0=ALU.is_le, op1=ALU.add, accum_out=bid_f[:, j:j + 1]))
                    c.link(nc.vector.tensor_mul(below, below, filled))
                    c.link(nc.vector.reduce_sum(first_f[:, j:j + 1], below, AX.X))
                c.link(nc.vector.scalar_tensor_tensor(out=first_f, in0=group_no[:, :], scalar=float(GE), in1=first_f,
                                                      op0=ALU.mult, op1=ALU.subtract))
                c.link(nc.vector.tensor_scalar(out=first_f, in0=first_f, scalar1=float(E), scalar2=0.0,
                                               op0=ALU.min, op1=ALU.max))
                c.link(nc.vector.tensor_scalar_min(bid_f, bid_f, float(NB - 1)))
                nc.vector.tensor_scalar(out=base_f, in0=bid_f, scalar1=float(P), scalar2=None, op0=ALU.mult)
                nc.vector.tensor_copy(first_i, first_f)
                nc.vector.tensor_copy(bid_i, bid_f).then_inc(summed, 1)
                dve.wait_ge(order_summed, 1)
                nc.vector.tensor_scalar_min(flag[:, 0:1], bank[6][0:1, 130:131], 1.0)

        move_groups = rec_dram.rearrange("(a g p q) w -> a p g (q w)", g=BATCH, p=P, q=G)
        NBATCH = NG // BATCH
        MOVE_LINKS = 4
        BY_SP, BY_ACT, BY_POOL = range(0, 4), range(4, 5), range(5, BATCH)
        pad = hx[:, :, :].rearrange("p b c -> p (b c)")
        PARTS = -(-(SLOTS // P * REC) // (NB * TW))
        while SLOTS // P % PARTS:
            PARTS += 1
        PR = SLOTS // P // PARTS
        pad_recs = pad[:, 0:PR * REC].rearrange("p (r w) -> p r w", w=REC)

        def load_in_order(eng, mine, landed):
            def load(i, k, turn):
                if past(i, 4):
                    eng.wait_ge(moved[k], 16 * turn)
                for j in mine:
                    start = eng.value_load(first[0:1, at(i * BATCH + j)], min_val=0, max_val=E)
                    eng.dma_start(move_ring[:, k, j * G * REC:(j + 1) * G * REC],
                                  listed_dram[bass.ds(start, GE), :].rearrange("(p q) w -> p (q w)", p=P))\
                        .then_inc(landed[k], 16)
            return load

        def place_in_order(dve):
            source_f, kept = (att_t[:, i, 0:BATCH * G].rearrange("p (g q) -> p g q", q=G) for i in range(2))

            def place(i, k, turn):
                c = Chain(dve, move_chain, i * MOVE_LINKS)
                words = move_ring[:, k, :].rearrange("p (g q w) -> p g q w", g=BATCH, w=REC)
                lanes, sources = words[:, :, :, R_LANE], words[:, :, :, R_SRC].bitcast(I32)
                dve.wait_ge(move_landed[k], 16 * (len(BY_SP) + len(BY_ACT)) * (turn + 1))
                dve.wait_ge(move_landed_pool[k], 16 * len(BY_POOL) * (turn + 1))
                stand_alone(dve, "dve")
                nc.vector.tensor_copy(source_f, sources)
                c.link(nc.vector.tensor_tensor(
                    out=lanes, in0=lanes,
                    in1=group_base[:, span(i * BATCH, BATCH)].rearrange("p (g a) -> p g a", a=1)
                    .broadcast_to([P, BATCH, G]), op=ALU.subtract))
                c.link(nc.vector.tensor_scalar_add(source_f, source_f, -float(N)))
                c.link(nc.vector.scalar_tensor_tensor(out=kept, in0=lanes, scalar=float(P), in1=source_f,
                                                      op0=ALU.is_lt, op1=ALU.mult))
                c.link(nc.vector.tensor_scalar_add(sources, kept, float(N)))
            software_pipeline(dve, NBATCH, 4, [(0, place)])

        def store_in_order(act):
            def store(i, k, turn):
                act.wait_ge(move_chain, (i + 1) * MOVE_LINKS)
                act.dma_start(move_groups[at(i)].rearrange("a p g w -> p (a g) w"),
                              move_ring[:, k, :].rearrange("p (g w) -> p g w", g=BATCH)).then_inc(moved[k], 16)
            software_pipeline(act, NBATCH, 4, [(2, load_in_order(act, BY_ACT, move_landed)), (-1, store)])
            for k in range(4):
                act.wait_ge(moved[k], 16 * len(range(k, NBATCH, 4)))

        def load_for_scatter(sp):
            sp.wait_ge(pads_made, 2)
            lanes = rec_dram.rearrange("(p a r) w -> a p (r w)", p=P, a=PARTS)
            for a in range(PARTS):
                sp.dma_start(lanes[a], pad[:, 0:PR * REC]).then_inc(pads_stored, 16)

            def load(i, k, turn):
                if past(i, 2):
                    sp.wait_ge(scattered[k], 16 * CH * turn)
                sp.dma_start(rec_ring[:, k, :, :], listed_cols[:, span(i * CH, CH), :]).then_inc(chunk_landed[k], 16)
            software_pipeline(sp, NCH, 2, [(0, load)])

        def place_for_scatter(dve):
            with dve.Fori(0, NB) as b:
                c = Chain(dve, slot_chain, b * 3)
                c.link(nc.vector.tensor_scalar(out=hit_i, in0=hi_f, scalar1=lane_row[0:EP, at(b)], scalar2=None,
                                               op0=ALU.is_equal))
                c.link(nc.vector.tensor_tensor_scan(run_f, hit_i, hit_i, base[0:EP, at(b)], ALU.add, ALU.bypass))
                stand_alone(dve, "dve")
                c.link(nc.vector.copy_predicated(slot_f, hit_i, run_f))
                stand_alone(dve, "dve")

            def place(i, k, turn):
                dve.wait_ge(chunk_landed[k], 16 * (turn + 1))
                if past(i, 2):
                    dve.wait_ge(scattered[k], 16 * CH * turn)
                stand_alone(dve, "dve")
                nc.vector.tensor_copy(rec_ring[:, k, :, R_LANE], lane_f[:, span(i * CH, CH)])
                nc.vector.tensor_copy(slot_ring[:, k, :], slot_f[:, span(i * CH, CH)]).then_inc(chunk_made, 1)
            software_pipeline(dve, NCH, 2, [(0, place)])

        def scatter_all(pool):
            c = Chain(pool, pads_made)
            c.link(nc.gpsimd.memset(pad_recs, 0.0))
            nc.gpsimd.memset(pad_recs[:, :, R_SRC].bitcast(I32), N)
            c.link(nc.gpsimd.memset(pad_recs[:, :, R_LANE], NO_LANE))
            pool.wait_ge(pads_stored, 16 * PARTS)

            def scatter(i, k, turn):
                pool.wait_ge(chunk_made, i + 1)
                stand_alone(pool, "pool")
                for t in range(CH):
                    nc.gpsimd.indirect_dma_start(
                        rec_dram, bass.IndirectOffsetOnAxis(ap=slot_ring[:, k, t:t + 1], axis=0),
                        rec_ring[:, k, t, :], None).then_inc(scattered[k], 16)
            software_pipeline(pool, NCH, 2, [(0, scatter)])
            for k in range(2):
                pool.wait_ge(scattered[k], 16 * CH * len(range(k, NCH, 2)))

        with nc.Block() as block:
            @block.sync
            def _(sp):
                unordered = sp.value_load(flag[0:1, 0:1], min_val=0, max_val=1)
                with sp.If(unordered == 0):
                    software_pipeline(sp, NBATCH, 4, [(2, load_in_order(sp, BY_SP, move_landed))])
                with sp.Else():
                    load_for_scatter(sp)

            @block.vector
            def _(dve):
                unordered = dve.value_load(flag[0:1, 0:1], min_val=0, max_val=1)
                with dve.If(unordered == 0):
                    place_in_order(dve)
                with dve.Else():
                    place_for_scatter(dve)

            @block.scalar
            def _(act):
                unordered = act.value_load(flag[0:1, 0:1], min_val=0, max_val=1)
                with act.If(unordered == 0):
                    store_in_order(act)

            @block.gpsimd
            def _(pool):
                unordered = pool.value_load(flag[0:1, 0:1], min_val=0, max_val=1)
                with pool.If(unordered == 0):
                    software_pipeline(pool, NBATCH, 4, [(2, load_in_order(pool, BY_POOL, move_landed_pool))])
                with pool.Else():
                    scatter_all(pool)

        hp, hp_t, mx, hm_t, part, own = (node_ring[:, i, :, :] for i in range(6))

        def prepare_rows(block, call, sources, turned, mixed_call, weights, evacuate, table):
            width = weights.shape[1]
            n0 = call * NB
            m0 = 0 if mixed_call is None else mixed_call * NB

            @block.sync
            def _(sp):
                to, of = table
                for part_no in range(TABLE_PARTS):
                    blocks = slice(part_no * PB, (part_no + 1) * PB)
                    sp.wait_ge(rows_copied, n0 + (part_no + 1) * PB)
                    stand_alone(sp, "sp")
                    sp.dma_start(to[:, blocks, :], of[:, blocks, :]).then_inc(table_stored, 16)
                sp.wait_ge(table_stored, 16 * TABLE_PARTS * (call + 1))
                stand_alone(sp, "sp")

            @block.vector
            def _(dve):
                def bend(i, k, turn):
                    dve.wait_ge(mix_copied, m0 + i + 1)
                    if past(i, 2):
                        dve.wait_ge(rows_made, n0 + i - 1)
                    nc.vector.scalar_tensor_tensor(out=hm_t[:, k, :], in0=mx[:, k, :], scalar=OUT_SLOPE,
                                                   in1=mx[:, k, :], op0=ALU.mult, op1=ALU.max).then_inc(mix_bent, 1)
                software_pipeline(dve, NB, 2, sources(dve) + ([] if mixed_call is None else [(-3, bend)]))

            @block.tensor
            def _(pe):
                def turn_rows(i, k, turn):
                    pe.wait_ge(src_made, n0 + i + 1)
                    if past(i, 2):
                        pe.wait_ge(src_copied, n0 + i - 1)
                    nc.tensor.transpose(bank[k][:, 0:P], hp[:, k, :], ident[:, :]).then_inc(src_transposed, 1)

                def mix_rows(i, k, turn):
                    pe.wait_ge(src_copied, n0 + i + 1)
                    if past(i, 2):
                        pe.wait_ge(mix_copied, m0 + i - 1)
                    nc.tensor.matmul(bank[2 + k][:, 0:P], mix_cur[:, :], hp_t[:, k, :], start=True, stop=True)\
                        .then_inc(mixed, 1)

                def project(i, k, turn):
                    if mixed_call is None:
                        pe.wait_ge(src_copied, n0 + i + 1)
                    else:
                        pe.wait_ge(mix_bent, m0 + i + 1)
                    if past(i, 2):
                        pe.wait_ge(rows_copied, n0 + i - 1)
                    rows_t = hp_t if mixed_call is None else hm_t
                    nc.tensor.matmul(bank[4 + k][:, 0:width], rows_t[:, k, :], weights, start=True, stop=True)\
                        .then_inc(rows_made, 1)
                software_pipeline(pe, NB, 2, [(0, turn_rows)] + ([(-1, project)] if mixed_call is None
                                                              else [(-1, mix_rows), (-2, project)]))

            @block.scalar
            def _(act):
                def copy_turned(i, k, turn):
                    act.wait_ge(src_transposed, n0 + i + 1)
                    if past(i, 2):
                        if mixed_call is None:
                            act.wait_ge(rows_made, n0 + i - 1)
                        else:
                            act.wait_ge(mixed, m0 + i - 1)
                    turned(hp_t[:, k, :], bank[k][:, 0:P]).then_inc(src_copied, 1)

                def copy_mixed(i, k, turn):
                    act.wait_ge(mixed, m0 + i + 1)
                    if past(i, 2):
                        act.wait_ge(mix_bent, m0 + i - 1)
                    nc.scalar.activation(mx[:, k, :], bank[2 + k][:, 0:P], ACT.Copy).then_inc(mix_copied, 1)

                def copy_rows(i, k, turn):
                    act.wait_ge(rows_made, n0 + i + 1)
                    evacuate(i, bank[4 + k][:, 0:width]).then_inc(rows_copied, 1)
                software_pipeline(act, NB, 2, [(0, copy_turned)] + ([(-1, copy_rows)] if mixed_call is None
                                                                    else [(-1, copy_mixed), (-2, copy_rows)]))

        LN_LINKS = 7

        def normalise(block, call, rows_in):
            @block.vector
            def _(dve):
                with dve.Fori(0, NB) as b:
                    nc.vector.bn_stats(ln_stat[:, at(b), :].rearrange("p a c -> p (a c)"),
                                       rows_in[:, at(b), :].rearrange("p a c -> p (a c)")).then_inc(ln_counted, 1)
                dve.wait_ge(ln_counted, (call + 1) * NB)
                c = Chain(dve, ln_chain, call * LN_LINKS)
                mean_e, mean_o, sq_e, sq_o = (ln_stat[:, :, i] for i in (1, 4, 2, 5))
                half_gap = ln_stat[:, :, 0]
                c.link(nc.vector.tensor_add(ln_mv[:, :, 0], mean_e, mean_o))
                c.link(nc.vector.tensor_sub(half_gap, mean_e, mean_o))
                c.link(nc.vector.tensor_scalar(out=ln_mv[:, :, 0], in0=ln_mv[:, :, 0], scalar1=0.5, scalar2=None,
                                               op0=ALU.mult))
                c.link(nc.vector.tensor_mul(half_gap, half_gap, half_gap))
                c.link(nc.vector.tensor_add(sq_e, sq_e, sq_o))
                c.link(nc.vector.scalar_tensor_tensor(out=sq_e, in0=half_gap, scalar=C / 4.0, in1=sq_e,
                                                      op0=ALU.mult, op1=ALU.add))
                dve.wait_ge(ln_act, call + 1)
                c.link(nc.vector.reciprocal(ln_mv[:, :, 1], ln_stat[:, :, 3]))
                nc.vector.tensor_mul(ln_mv[:, :, 1], ln_mv[:, :, 1], real_rows[:, :])

            @block.scalar
            def _(act):
                act.wait_ge(ln_chain, call * LN_LINKS + 6)
                nc.scalar.activation(ln_stat[:, :, 3], ln_stat[:, :, 2], ACT.Sqrt, bias=eps_col[:, :], scale=1.0 / C)\
                    .then_inc(ln_act, 1)

        def block_of(t, b):
            return t[:, at(b), :].rearrange("p a c -> p (a c)")

        def rows_of(t, b):
            return t[:, at(b), 1:P + 1].rearrange("p a c -> p (a c)")

        with nc.Block() as block:
            @block.vector
            def _(dve):
                dve.memset(x0[:, NB - 1, :], 0.0).then_inc(x_landed, 1)

            @block.sync
            def _(sp):
                sp.wait_ge(x_landed, 1)
                sp.dma_start(x0[:, 0:NB - 1, :], x[0:(NB - 1) * P, :].rearrange("(b p) c -> p b c", p=P))\
                    .then_inc(loaded, 16)
                sp.dma_start(x0[0:TAIL, NB - 1, :], x[(NB - 1) * P:N, :]).then_inc(loaded, 16)
                sp.wait_ge(loaded, 16 * (len(loads) + 2))

        with nc.Block() as block:
            normalise(block, 0, x0)

            @block.gpsimd
            def _(pool):
                nc.gpsimd.memset(hx[:, :, 0], 1.0)

        def norm_rows(call):
            def sources(dve):
                def make(i, k, turn):
                    if past(i, 2):
                        dve.wait_ge(src_transposed, call * NB + i - 1)
                    nc.vector.tensor_scalar(out=hp[:, k, :], in0=block_of(x0, i), scalar1=ln_mv[:, at(i), 0],
                                            scalar2=ln_mv[:, at(i), 1], op0=ALU.subtract, op1=ALU.mult)\
                        .then_inc(src_made, 1)
                return [(0, make)]
            return sources

        def relu_turned(to, of):
            return nc.scalar.activation(to, of, ACT.Relu)

        def biased_turned(to, of):
            return nc.scalar.activation(to, of, ACT.Identity, bias=bias_cur[:, :])

        def to_hx(i, product):
            return nc.scalar.activation(hx[:, at(i), 1:TW].rearrange("p a c -> p (a c)"), product, ACT.Copy)

        hx_table = (tab_blocks, hx)
        with nc.Block() as block:
            prepare_rows(block, 0, norm_rows(0), relu_turned, None, w_ext[:, 0, :], to_hx, hx_table)

        def rec_word(k, q, word):
            return recs[:, k, q * REC + word:q * REC + word + 1]

        def row_words(k, q, lo, hi):
            return rows[:, k, q * TW + lo:q * TW + hi]

        def stream_rows(block, layer):
            g0 = layer * NG
            t0 = layer * (NG // RING)

            @block.sync
            def _(sp):
                def load(i, k, turn):
                    sp.wait_ge(slot_free, g0 + i + 1)
                    sp.dma_start(recs[:, k, :], rec_groups[at(i)].rearrange("a p w -> (a p) w"))\
                        .then_inc(rec_landed[k], 16)
                software_pipeline(sp, NG, RING, [(0, load)])

            @block.gpsimd
            def _(pool):
                def gather(i, k, turn):
                    if k % 2 == 0:
                        pool.wait_ge(rec_landed[k], 16 * (t0 + turn + 1))
                        pool.wait_ge(rec_landed[k + 1], 16 * (t0 + turn + 1))
                        stand_alone(pool, "pool")
                    for q in range(G):
                        nc.gpsimd.indirect_dma_start(
                            row_words(k, q, 0, TW), None, tab_dram,
                            bass.IndirectOffsetOnAxis(ap=rec_word(k, q, R_SRC).bitcast(U32), axis=0))\
                            .then_inc(rows_landed[k], 16)
                software_pipeline(pool, NG, RING, [(0, gather)])

        MAX_LINKS = 4

        def attend(block, layer, with_sums=False):
            g0 = layer * NG
            t0 = layer * (NG // RING)
            term_word = R_TERM + layer
            stream_rows(block, layer)

            @block.vector
            def _(dve):
                c = Chain(dve, start_chain, layer * 2)
                nc.vector.tensor_copy(blk[:, :, 0], hx[:, :, P + 2])
                nc.vector.memset(blk[:, :, 2], NO_MAX)
                c.link(nc.vector.tensor_scalar_mul(blk[:, :, 1], hx[:, :, P + 2], ATT_SLOPE))
                c.link(nc.vector.memset(acc[:, :, :], 0.0))

                def edge_side(i, k, turn):
                    r = k % 2
                    dve.wait_ge(rec_landed[k], 16 * (t0 + turn + 1))
                    if with_sums and past(i, 2):
                        dve.wait_ge(lanes_hot, i - 1)
                    for q in range(G):
                        nc.vector.tensor_scalar(out=other_lane[:, r, q * P:(q + 1) * P], in0=lane_row_b[:, :],
                                                scalar1=rec_word(k, q, R_LANE), scalar2=None,
                                                op0=ALU.not_equal)
                    dve.wait_ge(rows_landed[k], 16 * G * (t0 + turn + 1))
                    nc.vector.tensor_add(
                        u_edge[:, r, :], rows[:, k, :].rearrange("p (q w) -> p q w", w=TW)[:, :, P + 1],
                        recs[:, k, :].rearrange("p (q w) -> p q w", w=REC)[:, :, at(term_word)]
                        .rearrange("p q a -> p (q a)")).then_inc(u_made, 1)

                def maximum(i, k, turn):
                    r = k % 2
                    c = Chain(dve, max_chain, (g0 + i) * MAX_LINKS)
                    b = dve.value_load(bid[0:1, at(i)], min_val=0, max_val=NB - 1)
                    nc.vector.tensor_copy(cur[:, r, :], block_of(blk, b))
                    dve.wait_ge(logits_made, g0 + i + 1)
                    c.link(nc.vector.reduce_max(gmax[:, r, 0:1], bank[r][:, :], AX.X))
                    c.link(nc.vector.scalar_tensor_tensor(out=gmax[:, r, 1:3], in0=slopes[:, :],
                                                          scalar=gmax[:, r, 0:1], in1=cur[:, r, 0:2],
                                                          op0=ALU.mult, op1=ALU.add))
                    c.link(nc.vector.tensor_scalar(out=gmax[:, r, 3:4], in0=gmax[:, r, 1:2],
                                                   scalar1=gmax[:, r, 2:3], scalar2=cur[:, r, 2:3],
                                                   op0=ALU.max, op1=ALU.max))
                    nc.vector.tensor_scalar(out=shift[:, r, :], in0=cur[:, r, :], scalar1=gmax[:, r, 3:4],
                                            scalar2=None, op0=ALU.subtract).then_inc(shift_made, 1)
                    c.link(nc.vector.tensor_copy(blk[:, at(b), 2], gmax[:, r, 3:4]))

                def larger_exp(i, k, turn):
                    r = k % 2
                    dve.wait_ge(exps_made, g0 + i + 1)
                    if past(i, 2):
                        dve.wait_ge(att_turned, g0 + i - 1)
                    nc.vector.tensor_max(att_t[:, r, :], exp_pair[:, r, 0, :], exp_pair[:, r, 1, :])\
                        .then_inc(att_t_made, 1)

                def accumulate(i, k, turn):
                    b = dve.value_load(bid[0:1, at(i)], min_val=0, max_val=NB - 1)
                    dve.wait_ge(slot_free, RING + g0 + i + 1)
                    if past(i, 1):
                        dve.wait_ge(acc_added, g0 + i)
                    nc.vector.scalar_tensor_tensor(out=block_of(acc, b), in0=block_of(acc, b),
                                                   scalar=rescale[:, k, :], in1=bank[4 + k % 2][:, 0:P + 1],
                                                   op0=ALU.mult, op1=ALU.add).then_inc(acc_added, 1)

                def add_sums(i, k, turn):
                    b = dve.value_load(bid[0:1, at(i)], min_val=0, max_val=NB - 1)
                    dve.wait_ge(sums_made, i + 1)
                    if past(i, 1):
                        dve.wait_ge(sums_added, i)
                    nc.vector.tensor_add(block_of(sums, b), block_of(sums, b), bank[6 + k % 2][:, 0:HW])\
                        .then_inc(sums_added, 1)
                if with_sums:
                    nc.vector.memset(sums[:, :, :], 0.0).then_inc(sums_cleared, 1)
                    dve.wait_ge(sums_cleared, 1)
                software_pipeline(dve, NG, RING, [(0, maximum), (-1, larger_exp), (2, edge_side), (-4, accumulate)]
                                  + ([(-1, add_sums)] if with_sums else []))

            @block.tensor
            def _(pe):
                def logits(i, k, turn):
                    r = k % 2
                    pe.wait_ge(u_made, g0 + i + 1)
                    if past(i, 2):
                        pe.wait_ge(exps_made, g0 + i - 1)
                    for q in range(G):
                        nc.tensor.matmul(bank[r][:, q * P:(q + 1) * P], u_edge[:, r, q:q + 1].broadcast_to([P, P]),
                                         ident[:, :], start=True, stop=False)
                        last = nc.tensor.matmul(bank[r][:, q * P:(q + 1) * P], other_lane[:, r, q * P:(q + 1) * P],
                                                mask_ident[:, :], start=False, stop=True)
                    last.then_inc(logits_made, 1)

                def turn_att(i, k, turn):
                    r = k % 2
                    pe.wait_ge(att_t_made, g0 + i + 1)
                    if past(i, 2):
                        pe.wait_ge(att_made, g0 + i - 1)
                    for q in range(G):
                        last = nc.tensor.transpose(bank[2 + r][:, q * P:(q + 1) * P],
                                                   att_t[:, r, q * P:(q + 1) * P], ident[:, :])
                    last.then_inc(att_turned, 1)

                def weigh(i, k, turn):
                    r = k % 2
                    pe.wait_ge(att_made, g0 + i + 1)
                    pe.wait_ge(rows_landed[k], 16 * G * (t0 + turn + 1))
                    if past(i, 2):
                        pe.wait_ge(acc_added, g0 + i - 1)
                    for q in range(G):
                        last = nc.tensor.matmul(bank[4 + r][:, 0:P + 1], att[:, r, q * P:(q + 1) * P],
                                                row_words(k, q, 0, P + 1), start=(q == 0), stop=(q == G - 1))
                    last.then_inc(slot_free, 1)

                def sum_terms(i, k, turn):
                    pe.wait_ge(lanes_hot, i + 1)
                    if past(i, 2):
                        pe.wait_ge(sums_added, i - 1)
                    for q in range(G):
                        last = nc.tensor.matmul(bank[6 + k % 2][:, 0:HW], hot[:, k % 2, q * P:(q + 1) * P],
                                                recs[:, k, q * REC + R_TERM:(q + 1) * REC],
                                                start=(q == 0), stop=(q == G - 1))
                    last.then_inc(sums_made, 1)
                software_pipeline(pe, NG, RING, [(-3, weigh), (2, logits), (-1, turn_att)]
                                  + ([(0, sum_terms)] if with_sums else []))

            @block.scalar
            def _(act):
                def exps(i, k, turn):
                    r = k % 2
                    act.wait_ge(shift_made, g0 + i + 1)
                    if past(i, 2):
                        act.wait_ge(att_t_made, g0 + i - 1)
                    nc.scalar.activation(rescale[:, k, :], shift[:, r, 2:3], ACT.Exp)
                    nc.scalar.activation(exp_pair[:, r, 0, :], bank[r][:, :], ACT.Exp, bias=shift[:, r, 0:1])
                    nc.scalar.activation(exp_pair[:, r, 1, :], bank[r][:, :], ACT.Exp, bias=shift[:, r, 1:2],
                                         scale=ATT_SLOPE).then_inc(exps_made, 1)

                def copy_att(i, k, turn):
                    r = k % 2
                    act.wait_ge(att_turned, g0 + i + 1)
                    if past(i, 2):
                        act.wait_ge(slot_free, RING + g0 + i - 1)
                    nc.scalar.activation(att[:, r, :], bank[2 + r][:, :], ACT.Copy).then_inc(att_made, 1)

                def hot_lanes(i, k, turn):
                    act.wait_ge(u_made, g0 + i + 1)
                    if past(i, 2):
                        act.wait_ge(sums_made, i - 1)
                    nc.scalar.activation(hot[:, k % 2, :], other_lane[:, k % 2, :], ACT.Identity,
                                         bias=slopes[:, 0:1], scale=-1.0).then_inc(lanes_hot, 1)
                software_pipeline(act, NG, RING, [(0, exps), (-2, copy_att)]
                                  + ([(1, hot_lanes)] if with_sums else []))

        MERGE_LINKS = 9
        from_acc, from_self = small[:, 0, :], small[:, 1, :]

        def merge_self_loops(layer):
            logit, sloped, top, diff, weight, share = (small[:, i, :] for i in range(2, 8))
            inner = not isinstance(layer, int)
            share_of_conv = 1.0 - ALPHA if inner else 1.0
            with nc.Block() as block:
                @block.vector
                def _(dve):
                    c = Chain(dve, mrg_chain, layer * MERGE_LINKS)
                    if inner:
                        nc.vector.tensor_copy(mix_cur[:, :], block_of(mix, layer - 1))
                    nc.vector.tensor_copy(bias_cur[:, :], bias_cols[:, at(layer)])
                    c.link(nc.vector.tensor_add(logit, hx[:, :, P + 1], blk[:, :, 0]))
                    c.link(nc.vector.tensor_add(logit, logit, loop_term[:, at(layer), :].rearrange("p a b -> p (a b)")))
                    c.link(nc.vector.scalar_tensor_tensor(out=sloped, in0=logit, scalar=ATT_SLOPE, in1=logit,
                                                          op0=ALU.mult, op1=ALU.max))
                    c.link(nc.vector.tensor_max(top, sloped, blk[:, :, 2]))
                    c.link(nc.vector.tensor_sub(diff, blk[:, :, 2], top))
                    nc.vector.tensor_sub(logit, sloped, top).then_inc(mrg_sub, 1)
                    dve.wait_ge(mrg_exp, layer + 1)
                    c.link(nc.vector.tensor_mul(weight, acc[:, :, 0], from_acc))
                    c.link(nc.vector.tensor_add(weight, weight, from_self))
                    c.link(nc.vector.reciprocal(share, weight))
                    c.link(nc.vector.tensor_scalar(out=share, in0=share, scalar1=share_of_conv, scalar2=None,
                                                   op0=ALU.mult))
                    nc.vector.tensor_mul(from_acc, from_acc, share)
                    nc.vector.tensor_mul(from_self, from_self, share)

                @block.scalar
                def _(act):
                    act.wait_ge(mrg_sub, layer + 1)
                    nc.scalar.activation(from_acc, diff, ACT.Exp)
                    nc.scalar.activation(from_self, logit, ACT.Exp).then_inc(mrg_exp, 1)

        def scale_sums(block, layer):
            @block.gpsimd
            def _(pool):
                def scale(i, k, turn):
                    if past(i, 2):
                        pool.wait_ge(own_made, layer * NB + i - 1)
                        stand_alone(pool, "pool")
                    nc.gpsimd.tensor_mul(part[:, k, :], rows_of(acc, i), from_acc[:, at(i)].broadcast_to([P, P]))\
                        .then_inc(part_made, 1)
                software_pipeline(pool, NB, 2, [(0, scale)])

        def conv_rows(layer, finish, used):
            def sources(dve):
                def add_own(i, k, turn):
                    dve.wait_ge(part_made, layer * NB + i + 1)
                    stand_alone(dve, "dve")
                    nc.vector.scalar_tensor_tensor(out=own[:, k, :], in0=rows_of(hx, i), scalar=from_self[:, at(i)],
                                                   in1=part[:, k, :], op0=ALU.mult, op1=ALU.add)\
                        .then_inc(own_made, 1)

                def make(i, k, turn):
                    dve.wait_ge(own_made, layer * NB + i + 1)
                    if used is src_made and past(i, 2):
                        dve.wait_ge(src_transposed, (layer + 1) * NB + i - 1)
                    stand_alone(dve, "dve")
                    finish(i, k).then_inc(used, 1)
                return [(-1, make), (0, add_own)]
            return sources

        with nc.Block() as block:
            @block.gpsimd
            def _(pool):
                pool.sem_inc(slot_free, RING)

        with nc.Block() as block:
            attend(block, 0, with_sums=True)

        with nc.Block() as block:
            @block.vector
            def _(dve):
                c = Chain(dve, degree_chain)
                c.link(nc.vector.tensor_scalar_max(inv_deg[:, :], sums[:, :, L], 1.0))
                c.link(nc.vector.reciprocal(inv_deg[:, :], inv_deg[:, :]))
                for l in range(L):
                    nc.vector.tensor_mul(loop_term[:, l, :], sums[:, :, l], inv_deg[:, :])

        merge_self_loops(0)

        def keep_x0(i, k):
            nc.vector.tensor_copy(block_of(x0, i), own[:, k, :])
            return nc.vector.tensor_copy(hp[:, k, :], own[:, k, :])
        with nc.Block() as block:
            scale_sums(block, 0)
            prepare_rows(block, 1, conv_rows(0, keep_x0, src_made), biased_turned, None, w_ext[:, 1, :], to_hx, hx_table)

        with nc.Fori(1, L - 1) as layer:
            with nc.Block() as block:
                attend(block, layer)
            merge_self_loops(layer)

            def residual(i, k):
                return nc.vector.scalar_tensor_tensor(out=hp[:, k, :], in0=block_of(x0, i), scalar=ALPHA,
                                                      in1=own[:, k, :], op0=ALU.mult, op1=ALU.add)
            with nc.Block() as block:
                scale_sums(block, layer)
                prepare_rows(block, layer + 1, conv_rows(layer, residual, src_made), biased_turned, layer - 1,
                             w_ext[:, bass.ds(layer + 1, 1), :].rearrange("p a c -> p (a c)"), to_hx, hx_table)

        with nc.Block() as block:
            attend(block, L - 1)

            @block.scalar
            def _(act):
                act.dma_start(x0[:, 0:NB - 1, :], x[0:(NB - 1) * P, :].rearrange("(b p) c -> p b c", p=P))\
                    .then_inc(loaded, 16)
                act.dma_start(x0[0:TAIL, NB - 1, :], x[(NB - 1) * P:N, :]).then_inc(loaded, 16)
        merge_self_loops(L - 1)

        with nc.Block() as block:
            scale_sums(block, L - 1)

            @block.vector
            def _(dve):
                dve.wait_ge(loaded, 16 * (len(loads) + 4))
                bias_blocks = bias_last[:, :].rearrange("p (a c) -> p a c", a=1).broadcast_to([P, NB, P])
                nc.vector.tensor_add(x0[:, :, :], x0[:, :, :], bias_blocks).then_inc(x0_kept, 1)
                dve.wait_ge(x0_kept, 1)

                def add(i, k):
                    return nc.vector.tensor_add(block_of(x0, i), block_of(x0, i), own[:, k, :])
                software_pipeline(dve, NB, 2, conv_rows(L - 1, add, x0_added)(dve))

        with nc.Block() as block:
            normalise(block, 1, x0)

        def norm_rows_kept(dve):
            def keep(i, k, turn):
                dve.wait_ge(src_made, L * NB + i + 1)
                nc.vector.tensor_scalar_max(rows_of(hx, i), hp[:, k, :], 0.0).then_inc(rows_kept, 1)

            make = norm_rows(L)(dve)[0][1]

            def make_again(i, k, turn):
                if past(i, 2):
                    dve.wait_ge(rows_kept, i - 1)
                make(i, k, turn)
            return [(0, make_again), (-1, keep)]

        def to_uv(i, product):
            nc.scalar.activation(block_of(ub, i), product[:, 0:P], ACT.Copy)
            return nc.scalar.activation(rows_of(acc, i), product[:, P:2 * P], ACT.Copy)

        with nc.Block() as block:
            prepare_rows(block, L, norm_rows_kept, relu_turned, None, uv_w[:, :], to_uv,
                         (tab_blocks[:, :, 1:P + 1], acc[:, :, 1:P + 1]))

        hot_t = exp_pair[:, :, 0, :]
        u_cur = exp_pair[:, :, 1, 0:P]
        feat = ring_b
        g0, t0 = L * NG, L * (NG // RING)
        with nc.Block() as block:
            stream_rows(block, L)

            @block.tensor
            def _(pe):
                def spread_lanes(i, k, turn):
                    r = k % 2
                    pe.wait_ge(rec_landed[k], 16 * (t0 + turn + 1))
                    if past(i, 2):
                        pe.wait_ge(hot_made, i - 1)
                    for q in range(G):
                        last = nc.tensor.matmul(bank[r][:, q * P:(q + 1) * P],
                                                rec_word(k, q, R_LANE).broadcast_to([P, P]), ident[:, :],
                                                start=True, stop=True)
                    last.then_inc(lanes_spread, 1)

                def features(i, k, turn):
                    r = k % 2
                    pe.wait_ge(hot_made, i + 1)
                    pe.wait_ge(rows_landed[k], 16 * G * (t0 + turn + 1))
                    if past(i, 2):
                        pe.wait_ge(feat_copied, i - 1)
                    nc.tensor.matmul(bank[2 + r][:, :], u_cur[:, r, :], hot_t[:, r, :], start=True, stop=False)
                    for q in range(G):
                        last = nc.tensor.matmul(bank[2 + r][:, q * P:(q + 1) * P], row_words(k, q, 1, P + 1),
                                                ident[:, :], start=False, stop=(q == G - 1))
                    last.then_inc(slot_free, 1)
                software_pipeline(pe, NG, RING, [(1, spread_lanes), (0, features)])

            @block.vector
            def _(dve):
                def one_hot(i, k, turn):
                    r = k % 2
                    b = dve.value_load(bid[0:1, at(i)], min_val=0, max_val=NB - 1)
                    if past(i, 2):
                        dve.wait_ge(slot_free, RING + g0 + i - 1)
                        stand_alone(dve, "dve")
                    nc.vector.tensor_copy(u_cur[:, r, :], block_of(ub, b))
                    dve.wait_ge(lanes_spread, i + 1)
                    nc.vector.tensor_scalar(out=hot_t[:, r, :], in0=bank[r][:, :], scalar1=lane_col[:, :],
                                            scalar2=None, op0=ALU.is_equal).then_inc(hot_made, 1)

                def count(i, k, turn):
                    dve.wait_ge(feat_copied, i + 1)
                    nc.vector.bn_stats(bn_st[:, at(i), :].rearrange("p a c -> p (a c)"), feat[:, k % 2, :])\
                        .then_inc(feat_counted, 1)
                software_pipeline(dve, NG, RING, [(1, one_hot), (-1, count)])

            @block.scalar
            def _(act):
                def store(i, k, turn):
                    r = k % 2
                    act.wait_ge(slot_free, RING + g0 + i + 1)
                    if past(i, 2):
                        act.wait_ge(feat_counted, i - 1)
                        act.wait_ge(feat_stored[r], 16 * stored_turns(i, k, turn))
                    nc.scalar.activation(feat[:, r, :], bank[2 + r][:, :], ACT.Copy).then_inc(feat_copied, 1)
                    act.wait_ge(feat_copied, i + 1)
                    act.dma_start(e0_dram[:, span(i * GE, GE)], feat[:, r, :]).then_inc(feat_stored[r], 16)

                def stored_turns(i, k, turn):
                    return turn * (RING // 2) + k // 2
                software_pipeline(act, NG, RING, [(0, store)])
                for r in range(2):
                    act.wait_ge(feat_stored[r], 16 * (NG // 2))

        FILL = SLOTS / E
        mean, var, scale, shift_c, tmp, pad_y = (aff[:, i:i + 1] for i in range(6))
        scale1, shift1 = aff[:, 6:7], aff[:, 7:8]

        def affine(dve, act_turn, c, gamma, beta, to_scale, to_shift):
            c.link(nc.vector.tensor_mul(tmp, mean, mean))
            nc.vector.tensor_sub(var, var, tmp).then_inc(bn_ready, 1)
            dve.wait_ge(bn_act, act_turn)
            c.link(nc.vector.reciprocal(var, var))
            c.link(nc.vector.tensor_mul(to_scale, var, gamma))
            c.link(nc.vector.tensor_mul(tmp, mean, to_scale))
            c.link(nc.vector.tensor_sub(to_shift, beta, tmp))

        def whole_moments(c, factor):
            c.link(nc.vector.bn_aggr(bn_mv[:, :], bn_st[:, :, :].rearrange("p a c -> p (a c)")))
            c.link(nc.vector.tensor_mul(tmp, bn_mv[:, 0:1], bn_mv[:, 0:1]))
            c.link(nc.vector.tensor_add(var, bn_mv[:, 1:2], tmp))
            c.link(nc.vector.tensor_scalar(out=var, in0=var, scalar1=factor, scalar2=None, op0=ALU.mult))
            c.link(nc.vector.tensor_scalar(out=mean, in0=bn_mv[:, 0:1], scalar1=factor, scalar2=None, op0=ALU.mult))

        def square_root(act, turn):
            act.wait_ge(bn_ready, turn)
            nc.scalar.activation(var, var, ACT.Sqrt, bias=eps_col[:, :]).then_inc(bn_act, 1)

        with nc.Block() as block:
            @block.vector
            def _(dve):
                c = Chain(dve, bn_chain)
                whole_moments(c, FILL)
                affine(dve, 1, c, bn_par[:, 0:1], bn_par[:, 1:2], scale, shift_c)
                nc.vector.tensor_scalar_max(tmp, shift_c, 0.0).then_inc(bn_pad, 1)

            @block.scalar
            def _(act):
                square_root(act, 1)

        feat_in, relued = ring_a, ring_b
        with nc.Block() as block:
            @block.sync
            def _(sp):
                def load(i, k, turn):
                    if past(i, 4):
                        sp.wait_ge(relu_made, i - 3)
                    sp.dma_start(feat_in[:, k % 4, :], e0_dram[:, span(i * GE, GE)]).then_inc(feat_landed[k % 4], 16)
                software_pipeline(sp, NG, BATCH, [(0, load)])

            @block.scalar
            def _(act):
                def relu(i, k, turn):
                    act.wait_ge(feat_landed[k % 4], 16 * (turn * 2 + k // 4 + 1))
                    if past(i, 2):
                        act.wait_ge(fc_made, i - 1)
                    nc.scalar.activation(relued[:, k % 2, :], feat_in[:, k % 4, :], ACT.Relu, bias=shift_c, scale=scale)\
                        .then_inc(relu_made, 1)
                software_pipeline(act, NG, BATCH, [(0, relu)])

            @block.tensor
            def _(pe):
                def multiply(i, k, turn):
                    pe.wait_ge(relu_made, i + 1)
                    if past(i, 2):
                        pe.wait_ge(fc_counted, i - 1)
                    nc.tensor.matmul(bank[k % 2][:, :], fc_t[:, :], relued[:, k % 2, :], start=True, stop=True)\
                        .then_inc(fc_made, 1)
                software_pipeline(pe, NG, BATCH, [(0, multiply)])
                pe.wait_ge(bn_pad, 1)
                nc.tensor.matmul(bank[2][:, 0:1], fc_t[:, :], tmp, start=True, stop=True).then_inc(bn_pe, 1)

            @block.vector
            def _(dve):
                def count(i, k, turn):
                    dve.wait_ge(fc_made, i + 1)
                    nc.vector.bn_stats(bn_st[:, at(i), :].rearrange("p a c -> p (a c)"), bank[k % 2][:, :])\
                        .then_inc(fc_counted, 1)
                software_pipeline(dve, NG, BATCH, [(0, count)])
                dve.wait_ge(bn_pe, 1)
                nc.vector.tensor_copy(pad_y, bank[2][:, 0:1])

        EMPTY = (SLOTS - E) / E
        shift_row = ring_b
        with nc.Block() as block:
            @block.vector
            def _(dve):
                c = Chain(dve, bn_chain1)
                whole_moments(c, FILL)
                c.link(nc.vector.scalar_tensor_tensor(out=mean, in0=pad_y, scalar=-EMPTY, in1=mean,
                                                      op0=ALU.mult, op1=ALU.add))
                c.link(nc.vector.tensor_mul(tmp, pad_y, pad_y))
                c.link(nc.vector.scalar_tensor_tensor(out=var, in0=tmp, scalar=-EMPTY, in1=var,
                                                      op0=ALU.mult, op1=ALU.add))
                affine(dve, 2, c, bn_par[:, 2:3], bn_par[:, 3:4], scale1, shift1)
                nc.vector.tensor_scalar(out=fc_in[:, :], in0=fc_in[:, :], scalar1=scale1, scalar2=None, op0=ALU.mult)\
                    .then_inc(fc_scaled, 1)
                dve.wait_ge(bn_pe, 2)
                nc.vector.tensor_copy(fc_scaled_t[:, :], bank[0][:, 0:P])
                for q in range(G):
                    nc.vector.tensor_copy(shift_row[:, 0, q * P:(q + 1) * P], bank[0][:, P:2 * P])
                nc.vector.memset(acc[:, :, :], 0.0)

            @block.scalar
            def _(act):
                square_root(act, 2)

            @block.tensor
            def _(pe):
                pe.wait_ge(fc_scaled, 1)
                nc.tensor.transpose(bank[0][:, 0:P], fc_in[:, :], ident[:, :])
                nc.tensor.matmul(bank[0][:, P:2 * P], shift1.broadcast_to([P, P]), ident[:, :], start=True, stop=True)\
                    .then_inc(bn_pe, 1)

        relued3 = att_t
        lane_hots, biased, message = exp_pair, att, hot

        def hots(unit, eng, name, tiles, made):
            def stage(i, k, turn):
                eng.wait_ge(c_rec_landed[k], 16 * (turn + 1))
                if past(i, 2):
                    eng.wait_ge(c_summed, i - 1)
                stand_alone(eng, name)
                for q in tiles:
                    last = unit.tensor_scalar(out=lane_hots[:, k % 2, 0, q * P:(q + 1) * P], in0=lane_row[:, :],
                                              scalar1=rec_word(k, q, R_LANE), scalar2=None, op0=ALU.is_equal)
                last.then_inc(made, 1)
            return stage

        with nc.Block() as block:
            @block.gpsimd
            def _(pool):
                software_pipeline(pool, NG, BATCH, [(0, hots(nc.gpsimd, pool, "pool", range(2, G), c_hot_late))])

            @block.sync
            def _(sp):
                def load(i, k, turn):
                    if past(i, BATCH):
                        sp.wait_ge(c_summed, i - (BATCH - 1))
                    sp.dma_start(recs[:, k, :], rec_groups[at(i)].rearrange("a p w -> (a p) w"))\
                        .then_inc(c_rec_landed[k], 16)
                    if past(i, 4):
                        sp.wait_ge(c_relu, i - 3)
                    sp.dma_start(feat_in[:, k % 4, :], e0_dram[:, span(i * GE, GE)]).then_inc(c_landed[k % 4], 16)
                software_pipeline(sp, NG, BATCH, [(0, load)])

            @block.scalar
            def _(act):
                def relu(i, k, turn):
                    act.wait_ge(c_landed[k % 4], 16 * (turn * 2 + k // 4 + 1))
                    if past(i, 2):
                        act.wait_ge(c_fc, i - 1)
                    nc.scalar.activation(relued3[:, k % 2, :], feat_in[:, k % 4, :], ACT.Relu, bias=shift_c, scale=scale)\
                        .then_inc(c_relu, 1)

                def relu_message(i, k, turn):
                    act.wait_ge(c_biased, i + 1)
                    if past(i, 2):
                        act.wait_ge(c_summed, i - 1)
                    nc.scalar.activation(message[:, k % 2, :], biased[:, k % 2, :], ACT.Relu).then_inc(c_msg, 1)
                software_pipeline(act, NG, BATCH, [(2, relu), (-1, relu_message)])

            @block.tensor
            def _(pe):
                def multiply(i, k, turn):
                    pe.wait_ge(c_relu, i + 1)
                    if past(i, 2):
                        pe.wait_ge(c_biased, i - 1)
                    for q in range(G):
                        last = nc.tensor.matmul(bank[k % 2][:, q * P:(q + 1) * P],
                                                relued3[:, k % 2, q * P:(q + 1) * P], fc_scaled_t[:, :],
                                                start=True, stop=True)
                    last.then_inc(c_fc, 1)

                def add_up(i, k, turn):
                    pe.wait_ge(c_msg, i + 1)
                    pe.wait_ge(c_hot, i + 1)
                    pe.wait_ge(c_hot_late, i + 1)
                    if past(i, 2):
                        pe.wait_ge(c_added, i - 1)
                    for q in range(G):
                        last = nc.tensor.matmul(bank[2 + k % 2][:, 0:P], lane_hots[:, k % 2, 0, q * P:(q + 1) * P],
                                                message[:, k % 2, q * P:(q + 1) * P],
                                                start=(q == 0), stop=(q == G - 1))
                    last.then_inc(c_summed, 1)
                software_pipeline(pe, NG, BATCH, [(1, multiply), (-2, add_up)])

            @block.vector
            def _(dve):
                def add_shift(i, k, turn):
                    dve.wait_ge(c_fc, i + 1)
                    if past(i, 2):
                        dve.wait_ge(c_msg, i - 1)
                    nc.vector.tensor_add(biased[:, k % 2, :], bank[k % 2][:, :], shift_row[:, 0, :])\
                        .then_inc(c_biased, 1)

                def add_group(i, k, turn):
                    b = dve.value_load(bid[0:1, at(i)], min_val=0, max_val=NB - 1)
                    dve.wait_ge(c_summed, i + 1)
                    if past(i, 1):
                        dve.wait_ge(c_added, i)
                    nc.vector.tensor_add(rows_of(acc, b), rows_of(acc, b), bank[2 + k % 2][:, 0:P])\
                        .then_inc(c_added, 1)
                software_pipeline(dve, NG, BATCH, [(0, add_shift), (-1, hots(nc.vector, dve, "dve", range(0, 2), c_hot)),
                                             (-3, add_group)])

        with nc.Block() as block:
            @block.vector
            def _(dve):
                def part_of(n):
                    blocks = slice(n * PB, (n + 1) * PB)
                    return acc[:, blocks, 1:P + 1], hx[:, blocks, 1:P + 1], x0[:, blocks, :], ub[:, blocks, :]

                def mean_messages(n):
                    messages = part_of(n)[0]
                    means = inv_deg[:, n * PB:(n + 1) * PB].rearrange("p (b a) -> p b a", a=1)
                    nc.vector.tensor_mul(messages, messages, means.broadcast_to([P, PB, P])).then_inc(means_made, 1)

                def add_rows(n):
                    messages, own_rows, _, _ = part_of(n)
                    dve.wait_ge(means_made, n + 1)
                    nc.vector.tensor_add(messages, messages, own_rows).then_inc(sums_finished, 1)

                def finish(n):
                    messages, _, x1, result = part_of(n)
                    dve.wait_ge(sums_finished, n + 1)
                    nc.vector.scalar_tensor_tensor(out=result, in0=messages, scalar=0.0, in1=x1,
                                                   op0=ALU.max, op1=ALU.add).then_inc(out_made, 1)
                for n in range(TABLE_PARTS + 2):
                    for lag, stage in enumerate((mean_messages, add_rows, finish)):
                        if 0 <= n - lag < TABLE_PARTS:
                            stage(n - lag)

            @block.sync
            def _(sp):
                for n in range(TABLE_PARTS):
                    sp.wait_ge(out_made, n + 1)
                    first_block, end = n * PB, min((n + 1) * PB, NB - 1)
                    if end > first_block:
                        sp.dma_start(out[first_block * P:end * P, :].rearrange("(b p) c -> p b c", p=P),
                                     ub[:, first_block:end, :]).then_inc(out_stored, 16)
                sp.dma_start(out[(NB - 1) * P:N, :], ub[0:TAIL, NB - 1, :]).then_inc(out_stored, 16)
                parts = sum(n * PB < NB - 1 for n in range(TABLE_PARTS))
                sp.wait_ge(out_stored, 16 * (parts + 1))

    return None


_INS = ['x', 'src', 'dst', 'edge_attr_16', 'L0_gnn_Ws', 'L0_gnn_Wes', 'L0_gnn_a_srcs', 'L0_gnn_a_dsts',
        'L0_gnn_a_edges', 'L0_gnn_biases', 'L0_gnn_mid_ws', 'L1_gnn_theta_w', 'L1_gnn_phi_w', 'L1_gnn_fc1_w',
        'L1_gnn_bn0_g', 'L1_gnn_bn0_b', 'L1_gnn_bn1_g', 'L1_gnn_bn1_b']


def kernel(**inputs):
    import concourse.bacc as bacc
    from concourse.bass_utils import run_bass_kernel_spmd

    nc = bacc.Bacc("TRN2", target_bir_lowering=False, num_devices=1)
    arrays, args = {}, []
    for name in _INS:
        a = np.ascontiguousarray(inputs[name])
        arrays[f"in_{name}"] = a
        args.append(nc.dram_tensor(f"in_{name}", a.shape, mybir.dt.from_np(a.dtype), kind="ExternalInput").ap())
    shape = tuple(inputs['x'].shape)
    out = nc.dram_tensor("out", shape, F32, kind="ExternalOutput").ap()
    gnn_kernel(nc, *args, out)
    r = run_bass_kernel_spmd(nc, [arrays], core_ids=[0])
    return r.results[0]["out"]
```
